# Optimizing a Trainium2 kernel written in Bass

```python
import numpy as np
import jax
import jax.numpy as jnp

def _softmax(x, axis=-1):
    return jax.nn.softmax(x, axis=axis)

def _gelu(x):
    return jax.nn.gelu(x, approximate=True)

def _silu(x):
    return jax.nn.silu(x)

def _sigmoid(x):
    return jax.nn.sigmoid(x)

def _layernorm(x, axis=-1, eps=1e-05):
    m = jnp.mean(x, axis=axis, keepdims=True)
    v = jnp.var(x, axis=axis, keepdims=True)
    return (x - m) / jnp.sqrt(v + eps)

def _scatter_add(tgt, idx, src, axis=0):
    return tgt.at[idx].add(src)

def _segment_sum(src, seg, n):
    return jax.ops.segment_sum(src, seg, n)
kernel_name = 'mk_prb_d1_jaxref_r2_8f5741'

def setup_inputs(seed: int=0):
    np.random.seed(seed)
    _w = jnp.asarray

    def _L0_attn_setup():
        import jax, jax.numpy as jnp
        import numpy as np
        NUM_HEADS = 32
        EPS = 1e-15
        key = jax.random.key(seed)
        k1, k2, k3, k4 = jax.random.split(key, 4)
        B, N, C = (8, 2048, 512)
        x = jax.random.normal(k1, (B, N, C), dtype=jnp.float32)
        qkv_weight = jax.random.normal(k2, (3 * C, C), dtype=jnp.float32) * C ** (-0.5)
        proj_weight = jax.random.normal(k3, (C, C), dtype=jnp.float32) * C ** (-0.5)
        proj_bias = jax.random.normal(k4, (C,), dtype=jnp.float32) * 0.01
        return {'x': x, 'qkv_weight': qkv_weight, 'proj_weight': proj_weight, 'proj_bias': proj_bias}
    _L0_attn_in = _L0_attn_setup()

    def _L0_ffn_setup():
        import jax, jax.numpy as jnp
        import numpy as np
        D_MODEL = 512
        HIDDEN = 1024
        MOE_DIM = 64
        N_EXPERTS = 8
        TOP_K = 2
        EXP_HIDDEN = HIDDEN // 2
        B, S = (4, 1024)
        key = jax.random.key(seed)
        ks = jax.random.split(key, 20)

        def w(k, shape, fan_in):
            return (jax.random.normal(k, shape, dtype=jnp.float32) / np.sqrt(fan_in)).astype(jnp.float32)
        return {'inputs_embeds': jax.random.normal(ks[0], (B, S, D_MODEL), dtype=jnp.float32), 'enc_w': w(ks[1], (D_MODEL, HIDDEN), D_MODEL), 'enc_b': jnp.zeros((HIDDEN,), jnp.float32), 's2c_w': w(ks[2], (HIDDEN, MOE_DIM), HIDDEN), 's2c_b': jnp.zeros((MOE_DIM,), jnp.float32), 'r_w1': w(ks[3], (MOE_DIM, 64), MOE_DIM), 'r_b1': jnp.zeros((64,), jnp.float32), 'r_w2': w(ks[4], (64, N_EXPERTS), 64), 'r_b2': jnp.zeros((N_EXPERTS,), jnp.float32), 'e_w1': w(ks[5], (N_EXPERTS, MOE_DIM, EXP_HIDDEN), MOE_DIM), 'e_b1': jnp.zeros((N_EXPERTS, EXP_HIDDEN), jnp.float32), 'e_w2': w(ks[6], (N_EXPERTS, EXP_HIDDEN, MOE_DIM), EXP_HIDDEN), 'e_b2': jnp.zeros((N_EXPERTS, MOE_DIM), jnp.float32), 'c2s_w': w(ks[7], (MOE_DIM, HIDDEN), MOE_DIM), 'c2s_b': jnp.zeros((HIDDEN,), jnp.float32), 'dec_w': w(ks[8], (HIDDEN, D_MODEL), HIDDEN), 'dec_b': jnp.zeros((D_MODEL,), jnp.float32), 'ln_g': jnp.ones((D_MODEL,), jnp.float32), 'ln_b': jnp.zeros((D_MODEL,), jnp.float32)}
    _L0_ffn_in = _L0_ffn_setup()
    _d = {'L0_attn_x': _L0_attn_in['x'], 'L0_attn_qkv_weight': _L0_attn_in['qkv_weight'], 'L0_attn_proj_weight': _L0_attn_in['proj_weight'], 'L0_attn_proj_bias': _L0_attn_in['proj_bias'], 'L0_ffn_enc_w': _L0_ffn_in['enc_w'], 'L0_ffn_enc_b': _L0_ffn_in['enc_b'], 'L0_ffn_s2c_w': _L0_ffn_in['s2c_w'], 'L0_ffn_s2c_b': _L0_ffn_in['s2c_b'], 'L0_ffn_r_w1': _L0_ffn_in['r_w1'], 'L0_ffn_r_b1': _L0_ffn_in['r_b1'], 'L0_ffn_r_w2': _L0_ffn_in['r_w2'], 'L0_ffn_r_b2': _L0_ffn_in['r_b2'], 'L0_ffn_e_w1': _L0_ffn_in['e_w1'], 'L0_ffn_e_b1': _L0_ffn_in['e_b1'], 'L0_ffn_e_w2': _L0_ffn_in['e_w2'], 'L0_ffn_e_b2': _L0_ffn_in['e_b2'], 'L0_ffn_c2s_w': _L0_ffn_in['c2s_w'], 'L0_ffn_c2s_b': _L0_ffn_in['c2s_b'], 'L0_ffn_dec_w': _L0_ffn_in['dec_w'], 'L0_ffn_dec_b': _L0_ffn_in['dec_b'], 'L0_ffn_ln_g': _L0_ffn_in['ln_g'], 'L0_ffn_ln_b': _L0_ffn_in['ln_b']}
    _x0 = _d['L0_attn_x']
    _d['L0_attn_x'] = jax.random.normal(jax.random.fold_in(jax.random.key(seed), 1), (2, 4096, 512), dtype=_x0.dtype)
    del _x0
    return _d

def reference(L0_attn_x, L0_attn_qkv_weight, L0_attn_proj_weight, L0_attn_proj_bias, L0_ffn_enc_w, L0_ffn_enc_b, L0_ffn_s2c_w, L0_ffn_s2c_b, L0_ffn_r_w1, L0_ffn_r_b1, L0_ffn_r_w2, L0_ffn_r_b2, L0_ffn_e_w1, L0_ffn_e_b1, L0_ffn_e_w2, L0_ffn_e_b2, L0_ffn_c2s_w, L0_ffn_c2s_b, L0_ffn_dec_w, L0_ffn_dec_b, L0_ffn_ln_g, L0_ffn_ln_b):

    def _L0_attn_ref(x, qkv_weight, proj_weight, proj_bias):
        import jax, jax.numpy as jnp
        import numpy as np
        NUM_HEADS = 32
        EPS = 1e-15
        B, N, C = x.shape
        H = NUM_HEADS
        D = C // H
        qkv = jax.nn.relu(jnp.einsum('bnc,oc->bno', x, qkv_weight))
        qkv = qkv.reshape(B, N, 3, H, D)
        q, k, v = (qkv[:, :, 0], qkv[:, :, 1], qkv[:, :, 2])
        v_pad = jnp.concatenate([v, jnp.ones((B, N, H, 1), dtype=v.dtype)], axis=-1)
        vk = jnp.einsum('bnhe,bnhd->bhed', v_pad.astype(jnp.float32), k.astype(jnp.float32))
        vk_q = jnp.einsum('bhed,bnhd->bnhe', vk, q.astype(jnp.float32))
        proj_input = (vk_q[..., :D] / (vk_q[..., D:] + EPS)).astype(qkv.dtype)
        proj_input = proj_input.reshape(B, N, C)
        y = jnp.einsum('bnc,oc->bno', proj_input, proj_weight) + proj_bias
        return y

    def _L0_ffn_ref(inputs_embeds, enc_w, enc_b, s2c_w, s2c_b, r_w1, r_b1, r_w2, r_b2, e_w1, e_b1, e_w2, e_b2, c2s_w, c2s_b, dec_w, dec_b, ln_g, ln_b):
        import jax, jax.numpy as jnp
        import numpy as np
        D_MODEL = 512
        HIDDEN = 1024
        MOE_DIM = 64
        N_EXPERTS = 8
        TOP_K = 2
        EXP_HIDDEN = HIDDEN // 2
        B, S = (4, 1024)
        b, s, _ = inputs_embeds.shape
        spikes = jax.nn.sigmoid(inputs_embeds @ enc_w + enc_b)
        cont = spikes.reshape(b * s, -1) @ s2c_w + s2c_b
        rh = jax.nn.relu(cont @ r_w1 + r_b1)
        probs = jax.nn.softmax(rh @ r_w2 + r_b2, axis=-1)
        topw, topi = jax.lax.top_k(probs, TOP_K)
        topw = topw / jnp.sum(topw, axis=-1, keepdims=True)
        comb = jnp.sum(jax.nn.one_hot(topi, N_EXPERTS, dtype=cont.dtype) * topw[..., None], axis=1)
        eh = jax.nn.relu(jnp.einsum('nd,edh->neh', cont, e_w1) + e_b1)
        eo = jnp.einsum('neh,ehd->ned', eh, e_w2) + e_b2
        moe_out = jnp.einsum('ned,ne->nd', eo, comb)
        rates = jax.nn.sigmoid(moe_out @ c2s_w + c2s_b)
        x = rates.reshape(b, s, -1)
        dec = jax.nn.sigmoid(x @ dec_w + dec_b)
        mu = jnp.mean(dec, axis=-1, keepdims=True)
        var = jnp.var(dec, axis=-1, keepdims=True)
        return (dec - mu) * jax.lax.rsqrt(var + 1e-05) * ln_g + ln_b
    x = L0_attn_x
    xn = _layernorm(x, axis=-1)
    x = x + _L0_attn_ref(xn, L0_attn_qkv_weight, L0_attn_proj_weight, L0_attn_proj_bias) + _L0_ffn_ref(xn, L0_ffn_enc_w, L0_ffn_enc_b, L0_ffn_s2c_w, L0_ffn_s2c_b, L0_ffn_r_w1, L0_ffn_r_b1, L0_ffn_r_w2, L0_ffn_r_b2, L0_ffn_e_w1, L0_ffn_e_b1, L0_ffn_e_w2, L0_ffn_e_b2, L0_ffn_c2s_w, L0_ffn_c2s_b, L0_ffn_dec_w, L0_ffn_dec_b, L0_ffn_ln_g, L0_ffn_ln_b)
    return x

_drawn_inputs = setup_inputs


def setup_inputs(seed=0):
    import zlib

    import numpy as np

    out = dict(_drawn_inputs(seed))
    spreads = {'L0_ffn_enc_b': (0.0, 0.519),
     'L0_ffn_s2c_b': (0.0, 0.1),
     'L0_ffn_r_b1': (0.0, 0.287),
     'L0_ffn_r_b2': (0.0, 0.1),
     'L0_ffn_e_b1': (0.0, 0.481),
     'L0_ffn_e_b2': (0.0, 0.346),
     'L0_ffn_c2s_b': (0.0, 0.332),
     'L0_ffn_dec_b': (0.0, 0.1),
     'L0_ffn_ln_g': (1.0, 0.2),
     'L0_ffn_ln_b': (0.0, 0.1)}
    factors = {'L0_attn_qkv_weight': 3.705, 'L0_attn_proj_bias': 8.0}
    for name, (base, spread) in spreads.items():
        noise = np.random.default_rng([zlib.crc32(name.encode()), seed]).standard_normal(out[name].shape)
        drawn = base * np.exp(spread * noise) if base else spread * noise
        out[name] = jnp.asarray(drawn.astype(out[name].dtype))
    for name, factor in factors.items():
        out[name] = (out[name] * factor).astype(out[name].dtype)
    return out
```

```python
from contextlib import ExitStack

import concourse.bass as bass
from concourse import mybir

ALU = mybir.AluOpType
ACT = mybir.ActivationFunctionType
AX = mybir.AxisListType
F32 = mybir.dt.float32
F32R = mybir.dt.float32r

P = 128
BATCH, SEQ, DIM = 2, 4096, 512
TOK = BATCH * SEQ
BLK = 512
NB = TOK // BLK
NT = BLK // P
KC = DIM // P
HID = 1024
HC = HID // P
MOE = 64
NE = 8
EH = 512
EC = EH // P
NJ = NE * EC
HEADS, HD = 32, 16
HG = P // HD
LN_EPS = 1e-5
DEN_EPS = 1e-15


def wait(eng, sem, value):
    if isinstance(value, int) and value <= 0:
        return
    eng.wait_ge(sem, value)


def f32(ap):
    return ap.bitcast(F32)


class Bench:

    def __init__(self, nc, ctx, tag):
        self.nc, self.ctx, self.tag = nc, ctx, tag

    def sb(self, name, shape, dt=F32):
        return self.ctx.enter_context(self.nc.sbuf_tensor(self.tag + name, shape, dt))

    def psum(self, name):
        return self.ctx.enter_context(self.nc.psum_tensor(self.tag + name, [P, 512], F32))

    def sem(self, name):
        return self.ctx.enter_context(self.nc.semaphore(self.tag + name))


def pass3(pe, out, w_hi, w_lo, x_hi, x_lo, start, stop):
    pe.matmul(out, w_hi, x_hi, start=start, stop=False)
    pe.matmul(out, w_lo, x_hi, start=False, stop=False)
    return pe.matmul(out, w_hi, x_lo, start=False, stop=stop)



def ffn_weights(b, nc, d):
    w = {}
    w["enc_h"], w["enc_l"] = b.sb("enc_h", [P, KC, HID], F32R), b.sb("enc_l", [P, KC, HID], F32R)
    w["dec_h"], w["dec_l"] = b.sb("dec_h", [P, HC, DIM], F32R), b.sb("dec_l", [P, HC, DIM], F32R)
    w["s2c_h"], w["s2c_l"] = b.sb("s2c_h", [P, HC, P], F32R), b.sb("s2c_l", [P, HC, P], F32R)
    w["e1"] = b.sb("e1", [P, NE * EH], F32R)
    w["e2"] = b.sb("e2", [P, NJ, P], F32R)
    w["c2s"] = b.sb("c2s", [P, HID], F32R)
    w["r1"] = b.sb("r1", [P, P], F32R)
    w["r2"] = b.sb("r2", [P, NE], F32R)
    w["b2h"], w["b2l"] = b.sb("b2h", [2 * NE, P], F32R), b.sb("b2l", [2 * NE, P], F32R)
    w["twice"] = b.sb("twice", [P, P], F32R)
    w["pick"] = b.sb("pick", [2 * NE, NE], F32R)
    w["ident"] = b.sb("ident", [P, P], F32)
    w["rows"] = b.sb("rows", [P, BLK], F32R)
    w["pick_bias"] = b.sb("pick_bias", [P, P], F32R)
    w["enc_b"], w["c2s_b"] = b.sb("enc_b", [P, HC]), b.sb("c2s_b", [P, HC])
    w["e_b1"] = b.sb("e_b1", [P, NJ])
    w["r_b1"], w["s2c_b"] = b.sb("r_b1", [P, 1]), b.sb("s2c_b", [P, 1])
    w["r_b2"] = b.sb("r_b2", [P, NE])
    w["ln_g"] = b.sb("ln_g", [P, DIM])
    w["half_down"] = b.sb("half_down", [P, NT])
    w["probs"] = b.sb("probs", [P, NT, 2 * NE])
    w["top2"] = b.sb("top2", [P, NT, NE])
    w["comb_pad"] = b.sb("comb_pad", [P, NT, P])
    return w


def load_ffn(nc, d, w):
    with ExitStack() as ctx:
        b = Bench(nc, ctx, "fw_")
        CH = 2048
        raw = [b.sb(f"raw{i}", [P, CH]) for i in range(4)]
        small = b.sb("small", [P, 4 * P])
        ones = b.sb("ones", [P, P], F32R)
        onesf = b.sb("onesf", [P, P])
        twicef = b.sb("twicef", [P, P])
        pickf = b.sb("pickf", [2 * NE, NE])
        pbf = b.sb("pbf", [P, P])
        dec_b = b.sb("dec_b", [P, DIM])
        bias = b.sb("bias", [P, DIM])
        sums = b.psum("sums")
        row = b.psum("row")
        arrived = [b.sem(f"arrived{i}") for i in range(4)]
        small_in, vectors_in = b.sem("small_in"), b.sem("vectors_in")
        hi_done, lo_done = b.sem("hi_done"), b.sem("lo_done")
        consts, const_copied, summed, biased = (b.sem(n) for n in ("consts", "const_copied", "summed", "biased"))

        def flat(t):
            return t[:, :, :].rearrange("p a b -> p (a b)")
        enc_h, enc_l, dec_h, dec_l = (flat(w[n]) for n in ("enc_h", "enc_l", "dec_h", "dec_l"))
        chunks = []
        for c in range(2):
            s = slice(c * CH, (c + 1) * CH)
            chunks.append((d["enc_w"][:, s], CH, [(enc_h[:, s], enc_l[:, s], 0)]))
        chunks.append((d["s2c_w"][:, :], HC * MOE, [(w["s2c_h"][:, :, 0:MOE], w["s2c_l"][:, :, 0:MOE], 0),
                                                    (w["s2c_h"][:, :, MOE:P], w["s2c_l"][:, :, MOE:P], 0)]))
        for c in range(2):
            s = slice(c * CH, (c + 1) * CH)
            chunks.append((d["e_w1"][:, s], CH, [(w["e1"][:, s], None, MOE)]))
        chunks.append((d["e_w2"][:, :], CH, [(w["e2"][:, :, 0:MOE], w["e2"][:, :, MOE:P], 0)]))
        chunks.append((d["c2s_w"][:, :], HID, [(w["c2s"][:, :], None, MOE)]))
        for c in range(2):
            s = slice(c * CH, (c + 1) * CH)
            chunks.append((d["dec_w"][:, s], CH, [(dec_h[:, s], dec_l[:, s], 0)]))
        jobs = [(n, src, size, t) for n, (src, size, ts) in enumerate(chunks) for t in ts]
        hi_of = {}
        for k, (n, _, _, _) in enumerate(jobs):
            hi_of[n] = k + 1

        block = ctx.enter_context(nc.Block())

        @block.sync
        def _(sp):
            for n, (src, size, _) in enumerate(chunks):
                if n >= 4:
                    sp.wait_ge(lo_done, hi_of[n - 4])
                sp.dma_start(raw[n % 4][:, 0:size], src).then_inc(arrived[n % 4], 16)

        @block.gpsimd
        def _(pool):
            pool.dma_start(small[:, 0:P], d["r_w1"][:, :]).then_inc(small_in, 16)
            pool.dma_start(small[:, P:P + NE], d["r_w2"][:, :]).then_inc(small_in, 16)
            pool.dma_start(small[0:2 * NE, 2 * P:3 * P], d["e_b2"][:, :]).then_inc(small_in, 16)
            for k, name in (("enc_b", "enc_b"), ("c2s_b", "c2s_b"), ("e_b1", "e_b1"), ("r_b1", "r_b1"),
                            ("s2c_b", "s2c_b"), ("r_b2", "r_b2"), ("ln_g", "ln_g")):
                pool.dma_start(w[k][:, :], d[name][:, :]).then_inc(vectors_in, 16)
            pool.dma_start(dec_b[:, :], d["dec_b"][:, :]).then_inc(vectors_in, 16)
            pool.memset(w["ident"][:, :], 0.0).then_inc(consts, 1)
            pool.memset(twicef[:, :], 0.0).then_inc(consts, 1)
            pool.memset(pickf[:, :], 0.0).then_inc(consts, 1)
            pool.memset(onesf[:, :], 1.0).then_inc(consts, 1)
            pool.memset(pbf[:, :], 0.0).then_inc(consts, 1)
            pool.memset(w["half_down"][:, :], -0.5).then_inc(consts, 1)
            pool.memset(w["probs"][:, :, :], -1.0).then_inc(consts, 1)
            pool.memset(w["top2"][:, :, :], -1.0).then_inc(consts, 1)
            pool.memset(w["comb_pad"][:, :, :], 0.0).then_inc(consts, 1)
            pool.wait_ge(consts, 9)

            def diagonal(t, base, n):
                pool.wait_ge(consts, n)
                pool.affine_select(out=t, in_=t, compare_op=ALU.not_equal, fill=1.0, base=base,
                                   pattern=[[-1, t.shape[1]]], channel_multiplier=1).then_inc(consts, 1)
            diagonal(w["ident"][:, :], 0, 9)
            for k, base in enumerate((0, MOE, -MOE)):
                diagonal(twicef[:, :], base, 10 + k)
            for k, base in enumerate((0, -NE)):
                diagonal(pickf[:, :], base, 13 + k)
            for k, r in enumerate((64, 96)):
                pool.memset(pbf[r:r + 1, :], 1.0).then_inc(consts, 1)

        @block.scalar
        def _(act):
            for k, (n, _, size, (hi, _, _)) in enumerate(jobs):
                act.wait_ge(arrived[n % 4], 16 * (n // 4 + 1))
                src = raw[n % 4][:, 0:size]
                if len(hi.shape) == 3:
                    src = src.rearrange("p (a b) -> p a b", b=hi.shape[2])
                act.activation(hi, src, ACT.Copy).then_inc(hi_done, 1)

        @block.vector
        def _(dve):
            dve.wait_ge(consts, 17)
            dve.tensor_copy(ones[:, :], onesf[:, :]).then_inc(const_copied, 1)
            dve.tensor_copy(w["twice"][:, :], twicef[:, :]).then_inc(const_copied, 1)
            dve.tensor_copy(w["pick"][:, :], pickf[:, :]).then_inc(const_copied, 1)
            dve.tensor_copy(w["pick_bias"][:, :], pbf[:, :]).then_inc(const_copied, 1)
            dve.wait_ge(small_in, 48)
            dve.tensor_copy(w["r1"][:, :], small[:, 0:P]).then_inc(const_copied, 1)
            dve.tensor_copy(w["r2"][:, :], small[:, P:P + NE]).then_inc(const_copied, 1)
            dve.tensor_copy(w["b2h"][:, :], small[0:2 * NE, 2 * P:3 * P]).then_inc(const_copied, 1)
            dve.wait_ge(const_copied, 7)
            dve.tensor_tensor(w["r1"][MOE:P, :], small[MOE:P, 0:P], f32(w["r1"][MOE:P, :]),
                              ALU.subtract).then_inc(const_copied, 1)
            dve.tensor_tensor(w["r2"][MOE:P, :], small[MOE:P, P:P + NE], f32(w["r2"][MOE:P, :]),
                              ALU.subtract).then_inc(const_copied, 1)
            dve.tensor_tensor(w["b2l"][:, :], small[0:2 * NE, 2 * P:3 * P], f32(w["b2h"][:, :]),
                              ALU.subtract).then_inc(const_copied, 1)
            dve.wait_ge(vectors_in, 16 * 8)
            dve.tensor_scalar(w["enc_b"][:, :], w["enc_b"][:, :], 0.5, None, ALU.mult).then_inc(const_copied, 1)
            dve.tensor_scalar(w["c2s_b"][:, :], w["c2s_b"][:, :], 0.5, None, ALU.mult).then_inc(const_copied, 1)
            for k, (n, _, size, (hi, lo, r)) in enumerate(jobs):
                dve.wait_ge(hi_done, k + 1)
                if lo is None:
                    lo, hi = hi[r:, :], hi[r:, :]
                src = raw[n % 4][r:, 0:size]
                if len(hi.shape) == 3:
                    src = src.rearrange("p (a b) -> p a b", b=hi.shape[2])
                dve.tensor_tensor(lo, src, f32(hi), ALU.subtract).then_inc(lo_done, 1)
            dve.wait_ge(summed, 1)
            dve.scalar_tensor_tensor(out=w["s2c_b"][:, :], in0=sums[:, 0:1], scalar=0.5, in1=w["s2c_b"][:, :],
                                     op0=ALU.mult, op1=ALU.add).then_inc(biased, 1)
            dve.wait_ge(summed, 2)
            dve.scalar_tensor_tensor(out=bias[:, :], in0=dec_b[:, :], scalar=2.0, in1=row[:, :],
                                     op0=ALU.mult, op1=ALU.add).then_inc(biased, 1)
            dve.wait_ge(biased, 2)
            dve.tensor_copy(w["rows"][64:P, :], bias[64:P, :]).then_inc(biased, 1)
            dve.wait_ge(biased, 3)
            dve.tensor_tensor(w["rows"][96:P, :], bias[96:P, :], f32(w["rows"][96:P, :]),
                              ALU.subtract).then_inc(biased, 1)
            dve.wait_ge(biased, 4)

        @block.tensor
        def _(pe):
            pe.wait_ge(lo_done, len(jobs))
            pe.wait_ge(const_copied, 1)
            for k in range(HC):
                pe.matmul(sums[:, 0:2], w["s2c_h"][:, k, :], ones[:, 0:2], start=(k == 0), stop=False)
                m = pe.matmul(sums[:, 0:2], w["s2c_l"][:, k, :], ones[:, 0:2], start=False, stop=(k == HC - 1))
            m.then_inc(summed, 1)
            for k in range(HC):
                pe.matmul(row[:, :], ones[:, :], w["dec_h"][:, k, :], start=(k == 0), stop=False)
                m = pe.matmul(row[:, :], ones[:, :], w["dec_l"][:, k, :], start=False, stop=(k == HC - 1))
            m.then_inc(summed, 1)


def ffn_steps():
    steps = [("rt1", 0)] + [("e1", j) for j in range(4)] + [("fin_stats", 0), ("logits", 0)]
    comb_at = {5: [("comb_t", 0)], 7: [("spread", 0), ("z", 0)], 8: [("spread", 1), ("z", 1)]}
    for e in range(2, NE):
        comb_at.setdefault(4 * e + 1, []).append(("spread", e))
        comb_at.setdefault(4 * e + 3, []).append(("z", e))
    for j in range(NJ):
        steps.append(("e2", j))
        if j + 4 < NJ:
            steps.append(("e1", j + 4))
        steps += comb_at.get(j, [])
        if j == 6:
            steps.append(("fin_norm", 0))
        if j == 12:
            steps.append(("ln_stats", 0))
        if j == 16:
            steps.append(("ln_norm", 0))
        if j % 4 == 2:
            steps.append(("enc", j // 4))
        if j >= 8 and j % 4 == 0:
            steps.append(("s2c", j // 4 - 2))
    steps += [("s2c", 6), ("turn", 0), ("turn", 1), ("acc", 0), ("dup", 0), ("turn", 2), ("s2c", 7), ("turn", 3),
              ("c2s", 0), ("c2s", 1)]
    for k in range(HC):
        steps.append(("dec", k))
        if k + 2 < HC:
            steps.append(("c2s", k + 2))
    return steps


def ffn_prologue_steps():
    steps = [("ln_stats", 0), ("ln_norm", 0)] + [("turn", c) for c in range(KC)]
    for m in range(HC + 2):
        if m < HC:
            steps.append(("enc", m))
        if m == 4:
            steps += [("ln_stats", 1), ("ln_norm", 1)]
        if m >= 2:
            steps.append(("s2c", m - 2))
    return steps + [("turn", 10 + c) for c in range(KC)]


def run_ffn(nc, d, w):
    with ExitStack() as ctx:
        b = Bench(nc, ctx, "f_")
        x = b.sb("x", [P, NT, DIM])
        xt = b.sb("xt", [P, 2, BLK])
        xh, xl = b.sb("xh", [P, KC, BLK], F32R), b.sb("xl", [P, KC, BLK], F32R)
        sp_t, sph, spl = b.sb("sp_t", [P, 2, BLK]), b.sb("sph", [P, 2, BLK], F32R), b.sb("spl", [P, 2, BLK], F32R)
        hid, hidh, hidl = b.sb("hid", [P, 2, BLK]), b.sb("hidh", [P, 4, BLK], F32R), b.sb("hidl", [P, 4, BLK], F32R)
        cont, conth, contl = b.sb("cont", [P, BLK]), b.sb("conth", [P, BLK], F32R), b.sb("contl", [P, BLK], F32R)
        midh, midl = b.sb("midh", [P, BLK], F32R), b.sb("midl", [P, BLK], F32R)
        comb_b = b.sb("comb_b", [P, 2, BLK])
        z, acc = b.sb("z", [P, 2, BLK]), b.sb("acc", [P, BLK])
        out = b.sb("out", [P, NT, DIM])
        st, mv = b.sb("st", [P, NT, 6]), b.sb("mv", [P, NT, 2])
        ve, rs = b.sb("ve", [P, NT]), b.sb("rs", [P, NT])
        st2, mv2 = b.sb("st2", [P, NT, 6]), b.sb("mv2", [P, NT, 2])
        ve2, rs2 = b.sb("ve2", [P, NT]), b.sb("rs2", [P, NT])
        lg, lgm, ex = b.sb("lg", [P, NT, NE]), b.sb("lgm", [P, NT, NE]), b.sb("ex", [P, NT, NE])
        top, left = b.sb("top", [P, NT, NE]), b.sb("left", [P, NT, 2 * NE])
        picked, comb = b.sb("picked", [P, NT, NE]), b.sb("comb", [P, NT, NE])
        comb_r = b.sb("comb_r", [P, NT, NE], F32R)
        s4 = b.sb("s4", [P, 6, NT])
        held = b.sb("held", [P, 4])
        eps, eps4 = b.sb("eps", [P, NT]), b.sb("eps4", [P, NT])

        bE, bD = [b.psum(f"E{i}") for i in range(2)], [b.psum(f"D{i}") for i in range(4)]
        bS, bG = b.psum("S"), b.psum("G")

        names = {}

        def sem(name):
            names[name] = b.sem(name)
            return names[name]

        x_in, out_stored = sem("x_in"), sem("out_stored")
        xt_stored = [sem("xt_stored0"), sem("xt_stored1")]
        turned, enc_done, s2c_done, rt1_done, logits_done = (sem(n) for n in (
            "turned", "enc_done", "s2c_done", "rt1_done", "logits_done"))
        combt_done, spread_done, e1_done, e2_done, dup_done, c2s_done, dec_done = (sem(n) for n in (
            "combt_done", "spread_done", "e1_done", "e2_done", "dup_done", "c2s_done", "dec_done"))
        xt_out, sp_out, rate_out, cont_out, rh_out, exp_out = (sem(n) for n in (
            "xt_out", "sp_out", "rate_out", "cont_out", "rh_out", "exp_out"))
        combrow_out, combb_out, hid_out, hidh_act, moeh_out, dec_out = (sem(n) for n in (
            "combrow_out", "combb_out", "hid_out", "hidh_act", "moeh_out", "dec_out"))
        xstat, xmv, xnorm, xh_out, xl_out, sph_out, spl_out = (sem(n) for n in (
            "xstat", "xmv", "xnorm", "xh_out", "xl_out", "sph_out", "spl_out"))
        hidh_dve, hidl_out, rateh_out, ratel_out, conth_out, contl_out = (sem(n) for n in (
            "hidh_dve", "hidl_out", "rateh_out", "ratel_out", "conth_out", "contl_out"))
        rhh_out, rhl_out, route, comb_out, z_out, acch_out, accl_out, moel_out = (sem(n) for n in (
            "rhh_out", "rhl_out", "route", "comb_out", "z_out", "acch_out", "accl_out", "moel_out"))
        fstat, fmv, fnorm = sem("fstat"), sem("fmv"), sem("fnorm")
        xeps = sem("xeps")
        xve, xrs, acc_out, fve, frs, scaled = (sem(n) for n in ("xve", "xrs", "acc_out", "fve", "frs", "scaled"))

        def prior_on_e(order):
            e_uses = [s for s in order if s[0] in ("enc", "e1", "turn")]
            return {s: (k % 2, e_uses[k - 2] if k >= 2 else None) for k, s in enumerate(e_uses)}

        steps = ffn_steps()
        uses_full = prior_on_e(steps)
        n_full = [s for s in steps if s[0] in ("enc", "e1", "turn")]
        assert len(n_full) % 2 == 0 and len([s for s in n_full if s[0] != "turn"]) % 2 == 0

        block = ctx.enter_context(nc.Block())

        def run(eng, step, idle=()):
            for name, k in ffn_prologue_steps():
                if name in ("turn",):
                    step(name, k % 10, -2 if k < 10 else -1, "first", True, True)
                elif name in ("ln_stats", "ln_norm"):
                    step(name, 0, k - 2, "first", True, True)
                else:
                    step(name, k, -1, "first", True, True)

            def body(i, where, ahead, two_ahead):
                for name, k in steps:
                    if name in ("enc", "s2c") and not ahead:
                        continue
                    if name in ("turn", "ln_stats", "ln_norm") and not two_ahead:
                        continue
                    step(name, k, i, where, ahead, two_ahead)

            body(0, "peeled", True, True)
            with eng.Fori(1, NB - 2) as i:
                body(i, "loop", True, True)
            body(NB - 2, "peeled", True, False)
            body(NB - 1, "peeled", False, False)
            for name in ("fin_stats", "fin_norm"):
                step(name, 0, NB, "peeled", False, False)

        def e_bank(name, k, where, ahead, two_ahead):
            if where == "first":
                return bE[k % 2]
            order = [s for s in steps if s[0] in ("enc", "e1", "turn")]
            if not ahead:
                order = [s for s in order if s[0] != "enc"]
            if not two_ahead:
                order = [s for s in order if s[0] != "turn"]
            return bE[order.index((name, k)) % 2]

        def wait_e_bank(pe, name, k, i, where, ahead, two_ahead):
            def read(s, blk_i):
                n, q = s
                if n == "enc":
                    wait(pe, sp_out, (blk_i + 1) * HC + q + 1)
                elif n == "turn":
                    wait(pe, xt_out, (blk_i + 2) * KC + q + 1)
                else:
                    wait(pe, hid_out, blk_i * NJ + q + 1)
            if where == "first":
                if name == "turn" and k < 2 and isinstance(i, int) and i == -2:
                    return
                if name == "turn":
                    read(("turn", k - 2) if k >= 2 else ("enc", HC - 2 + k), -2 if i == -2 else -1)
                else:
                    read(("enc", k - 2), -1) if k >= 2 else read(("turn", KC - 2 + k), -2)
                return
            order = [s for s in steps if s[0] in ("enc", "e1", "turn")]
            before = list(order)
            if not ahead:
                order = [s for s in order if s[0] != "enc"]
            if not two_ahead:
                order = [s for s in order if s[0] != "turn"]
            n = order.index((name, k))
            if n >= 2:
                return read(order[n - 2], i)
            if isinstance(i, int) and i == 0:
                return read(("turn", KC - 2 + n), -1)
            if isinstance(i, int) and i == NB - 1:
                before = [s for s in before if s[0] != "turn"]
            return read(before[n - 2], i - 1)

        @block.sync
        def _(sp):
            def load_x(blk):
                wait(sp, turned, blk * KC)
                sp.dma_start(x[:, :, :], d["x"][bass.ds(blk * NT, NT), :, :].rearrange("t p c -> p t c"))\
                    .then_inc(x_in, 16)

            def store_xt(blk, c):
                sp.wait_ge(xt_out, blk * KC + c + 1)
                sp.dma_start(d["xt"][:, bass.ds(blk * KC * BLK + c * BLK, BLK)],
                             xt[:, c % 2, :]).then_inc(xt_stored[c % 2], 16)

            def step(name, k, i, where, ahead, two_ahead):
                if name == "ln_stats" and where == "first" or name == "rt1" and two_ahead:
                    load_x(i + 2)
                if name == "turn":
                    store_xt(i + 2, k)
                if name == "fin_norm":
                    blk = i - 1
                    if isinstance(blk, int) and blk < 0:
                        return
                    sp.wait_ge(scaled, blk * NT + NT)
                    sp.dma_start(d["ffn"][bass.ds(blk * NT, NT), :, :].rearrange("t p c -> p t c"),
                                 out[:, :, :]).then_inc(out_stored, 16)
            run(sp, step)
            sp.wait_ge(out_stored, 16 * NB)
            for s in xt_stored:
                sp.wait_ge(s, 16 * NB * KC // 2)

        @block.tensor
        def _(pe):
            def step(name, k, i, where, ahead, two_ahead):
                if name == "turn":
                    blk = i + 2
                    pe.wait_ge(xnorm, blk * NT + NT)
                    wait_e_bank(pe, name, k, i, where, ahead, two_ahead)
                    bank = e_bank(name, k, where, ahead, two_ahead)
                    for t in range(NT):
                        m = pe.transpose(bank[:, t * P:(t + 1) * P], x[:, t, k * P:(k + 1) * P], w["ident"][:, :])
                    m.then_inc(turned, 1)
                elif name == "enc":
                    blk = i + 1
                    pe.wait_ge(xl_out, blk * KC + KC)
                    wait_e_bank(pe, name, k, i, where, ahead, two_ahead)
                    bank = e_bank(name, k, where, ahead, two_ahead)
                    for c in range(KC):
                        s = slice(k * P, (k + 1) * P)
                        m = pass3(pe, bank[:, :], w["enc_h"][:, c, s], w["enc_l"][:, c, s], xh[:, c, :], xl[:, c, :],
                                  c == 0, c == KC - 1)
                    m.then_inc(enc_done, 1)
                elif name == "s2c":
                    blk = i + 1
                    pe.wait_ge(spl_out, blk * HC + k + 1)
                    if k == 0:
                        wait(pe, cont_out, blk)
                    pass3(pe, bS[:, :], w["s2c_h"][:, k, :], w["s2c_l"][:, k, :], sph[:, k % 2, :], spl[:, k % 2, :],
                          k == 0, k == HC - 1).then_inc(s2c_done, 1)
                elif name == "rt1":
                    pe.wait_ge(contl_out, i + 1)
                    wait(pe, rate_out, i * HC)
                    pe.matmul(bG[:, :], w["r1"][:, :], conth[:, :], start=True, stop=False)
                    pe.matmul(bG[:, :], w["r1"][:, :], contl[:, :], start=False, stop=True).then_inc(rt1_done, 1)
                elif name == "logits":
                    pe.wait_ge(rhl_out, i + 1)
                    for t in range(NT):
                        s = slice(t * P, (t + 1) * P)
                        pe.matmul(bG[:, t * NE:(t + 1) * NE], midh[:, s], w["r2"][:, :], start=True, stop=False)
                        m = pe.matmul(bG[:, t * NE:(t + 1) * NE], midl[:, s], w["r2"][:, :], start=False, stop=True)
                    m.then_inc(logits_done, 1)
                elif name == "comb_t":
                    pe.wait_ge(comb_out, i + 1)
                    for t in range(NT):
                        m = pe.transpose(bG[:, t * P:(t + 1) * P], w["comb_pad"][:, t, :], w["ident"][:, :])
                    m.then_inc(combt_done, 1)
                elif name == "spread":
                    pe.wait_ge(combrow_out, i + 1)
                    if k == 0:
                        wait(pe, dec_out, i * NT)
                    else:
                        pe.wait_ge(combb_out, i * NE + k)
                    pe.matmul(bD[3][:, :], w["pick"][:, k:k + 1].broadcast_to([2 * NE, P]), w["rows"][0:2 * NE, :],
                              start=True, stop=True).then_inc(spread_done, 1)
                elif name == "e1":
                    wait_e_bank(pe, name, k, i, where, ahead, two_ahead)
                    bank = e_bank(name, k, where, ahead, two_ahead)
                    s = slice(k * P, (k + 1) * P)
                    pe.matmul(bank[:, :], w["e1"][:, s], conth[:, :], start=True, stop=False)
                    pe.matmul(bank[:, :], w["e1"][:, s], contl[:, :], start=False, stop=True).then_inc(e1_done, 1)
                elif name == "e2":
                    e, q = divmod(k, EC)
                    pe.wait_ge(hidl_out, i * NJ + k + 1)
                    if q == 0 and e < 3:
                        wait(pe, dec_out, (i - 1) * NT + e + 1)
                    elif q == 0:
                        pe.wait_ge(z_out, i * NE + e - 2)
                    pe.matmul(bD[e % 3][:, :], w["e2"][:, k, :], hidh[:, k % 4, :], start=(q == 0), stop=False)
                    pe.matmul(bD[e % 3][:, :], w["e2"][:, k, :], hidl[:, k % 4, :], start=False,
                              stop=(q == EC - 1)).then_inc(e2_done, 1)
                elif name == "dup":
                    pe.wait_ge(accl_out, i + 1)
                    pe.matmul(bG[:, :], w["twice"][:, :], midh[:, :], start=True, stop=False)
                    pe.matmul(bG[:, :], w["twice"][:, :], midl[:, :], start=False, stop=False)
                    pe.matmul(bG[:, :], w["b2h"][:, :], w["rows"][0:2 * NE, :], start=False, stop=False)
                    pe.matmul(bG[:, :], w["b2l"][:, :], w["rows"][0:2 * NE, :], start=False, stop=True)\
                        .then_inc(dup_done, 1)
                elif name == "c2s":
                    pe.wait_ge(moel_out, i + 1)
                    if k:
                        pe.wait_ge(rate_out, i * HC + k)
                    s = slice(k * P, (k + 1) * P)
                    pe.matmul(bG[:, :], w["c2s"][:, s], midh[:, :], start=True, stop=False)
                    pe.matmul(bG[:, :], w["c2s"][:, s], midl[:, :], start=False, stop=True).then_inc(c2s_done, 1)
                elif name == "dec":
                    pe.wait_ge(ratel_out, i * HC + k + 1)
                    if k == 0:
                        pe.wait_ge(z_out, i * NE + NE)
                        pe.wait_ge(combb_out, i * NE + NE)
                        for t in range(NT):
                            pe.matmul(bD[t][:, :], w["pick_bias"][64:P, :], w["rows"][64:P, :], start=True, stop=False)
                    for t in range(NT):
                        s = slice(t * P, (t + 1) * P)
                        last = k == HC - 1
                        pe.matmul(bD[t][:, :], hidh[:, k % 4, s], w["dec_h"][:, k, :], start=False, stop=False)
                        pe.matmul(bD[t][:, :], hidh[:, k % 4, s], w["dec_l"][:, k, :], start=False, stop=False)
                        m = pe.matmul(bD[t][:, :], hidl[:, k % 4, s], w["dec_h"][:, k, :], start=False, stop=last)
                        if last:
                            m.then_inc(dec_done, 1)
                    if not last:
                        m.then_inc(dec_done, 1)
            run(pe, step)

        DEC = HC - 1 + NT

        @block.scalar
        def _(act):
            def step(name, k, i, where, ahead, two_ahead):
                if name == "turn":
                    blk = i + 2
                    n = blk * KC + k
                    act.wait_ge(turned, n + 1)
                    if not (isinstance(n, int) and n < 2):
                        act.wait_ge(xl_out, n - 1)
                        act.wait_ge(xt_stored[k % 2], (blk * KC // 2 + k // 2) * 16)
                    act.activation(xt[:, k % 2, :], e_bank(name, k, where, ahead, two_ahead)[:, :], ACT.Copy)\
                        .then_inc(xt_out, 1)
                elif name == "enc":
                    n = (i + 1) * HC + k
                    act.wait_ge(enc_done, n + 1)
                    wait(act, spl_out, n - 1)
                    act.activation(sp_t[:, k % 2, :], e_bank(name, k, where, ahead, two_ahead)[:, :], ACT.Tanh,
                                   bias=w["enc_b"][:, k:k + 1], scale=0.5).then_inc(sp_out, 1)
                elif name == "s2c" and k == HC - 1:
                    blk = i + 1
                    act.wait_ge(s2c_done, blk * HC + HC)
                    wait(act, rhl_out, blk)
                    act.activation(cont[:, :], bS[:, :], ACT.Identity, bias=w["s2c_b"][:, :], scale=0.5)\
                        .then_inc(cont_out, 1)
                elif name == "rt1":
                    act.wait_ge(rt1_done, i + 1)
                    act.wait_ge(contl_out, i + 1)
                    act.activation(cont[:, :], bG[:, :], ACT.Relu, bias=w["r_b1"][:, :]).then_inc(rh_out, 1)
                elif name == "logits":
                    act.wait_ge(route, i * 17 + 3)
                    act.activation(ex[:, :, :], lgm[:, :, :], ACT.Exp).then_inc(exp_out, 1)
                elif name == "comb_t":
                    act.wait_ge(combt_done, i + 1)
                    wait(act, dup_done, i)
                    act.activation(w["rows"][0:2 * NE, :], bG[0:2 * NE, :], ACT.Copy).then_inc(combrow_out, 1)
                elif name == "spread":
                    n = i * NE + k
                    act.wait_ge(spread_done, n + 1)
                    wait(act, z_out, n - 1)
                    act.activation(comb_b[:, k % 2, :], bD[3][:, :], ACT.Copy).then_inc(combb_out, 1)
                elif name == "e1":
                    n = i * NJ + k
                    act.wait_ge(e1_done, n + 1)
                    if k >= 2:
                        act.wait_ge(hidl_out, n - 1)
                    else:
                        wait(act, ratel_out, (i - 1) * HC + HC - 1 + k)
                    act.activation(hid[:, k % 2, :], e_bank(name, k, where, ahead, two_ahead)[:, :], ACT.Relu,
                                   bias=w["e_b1"][:, k:k + 1]).then_inc(hid_out, 1)
                    if k % 2:
                        act.wait_ge(hid_out, n + 1)
                        if k >= 4:
                            act.wait_ge(e2_done, n - 3)
                        else:
                            wait(act, dec_done, i * DEC)
                        act.activation(hidh[:, k % 4, :], hid[:, k % 2, :], ACT.Copy).then_inc(hidh_act, 1)
                elif name == "dup":
                    act.wait_ge(dup_done, i + 1)
                    act.activation(midh[:, :], bG[:, :], ACT.Copy).then_inc(moeh_out, 1)
                elif name == "c2s":
                    n = i * HC + k
                    act.wait_ge(c2s_done, n + 1)
                    if k >= 2:
                        act.wait_ge(ratel_out, n - 1)
                    else:
                        act.wait_ge(hidl_out, i * NJ + NJ - 1 + k)
                        if k % 2:
                            act.wait_ge(hidh_act, i * (NJ // 2) + NJ // 2)
                    act.activation(hid[:, k % 2, :], bG[:, :], ACT.Tanh, bias=w["c2s_b"][:, k:k + 1], scale=0.5)\
                        .then_inc(rate_out, 1)
                elif name == "dec" and k == HC - 1:
                    wait(act, out_stored, i * 16)
                    for t in range(NT):
                        act.wait_ge(dec_done, i * DEC + HC + t)
                        act.activation(out[:, t, :], bD[t][:, :], ACT.Tanh, scale=0.25).then_inc(dec_out, 1)
            run(act, step)

        @block.vector
        def _(dve):
            def hold(k, sem, value):
                dve.wait_ge(sem, value)
                dve.memset(held[:, k:k + 1], 0.0)

            def split(src, hi, lo, hi_sem, lo_sem, n):
                dve.tensor_copy(hi, src).then_inc(hi_sem, 1)
                dve.wait_ge(hi_sem, n)
                dve.tensor_tensor(lo, src, f32(hi), ALU.subtract).then_inc(lo_sem, 1)

            def step(name, k, i, where, ahead, two_ahead):
                if name == "ln_stats":
                    blk = i + 2
                    dve.wait_ge(x_in, blk * 16 + 16)
                    for t in range(NT):
                        dve.bn_stats(st[:, t, :], x[:, t, :]).then_inc(xstat, 1)
                    hold(0, xstat, blk * NT + NT)
                    for t in range(NT):
                        dve.bn_aggr(mv[:, t, :], st[:, t, :]).then_inc(xmv, 1)
                elif name == "ln_norm":
                    blk = i + 2
                    dve.wait_ge(xrs, blk + 1)
                    dve.wait_ge(xmv, blk * NT + NT)
                    for t in range(NT):
                        dve.tensor_scalar(x[:, t, :], x[:, t, :], mv[:, t, 0:1], rs[:, t:t + 1],
                                          ALU.subtract, ALU.mult).then_inc(xnorm, 1)
                elif name == "turn":
                    blk = i + 2
                    n = blk * KC + k
                    dve.wait_ge(xt_out, n + 1)
                    wait(dve, enc_done, (i + 2) * HC)
                    split(xt[:, k % 2, :], xh[:, k, :], xl[:, k, :], xh_out, xl_out, n + 1)
                elif name == "enc":
                    n = (i + 1) * HC + k
                    dve.wait_ge(sp_out, n + 1)
                    wait(dve, s2c_done, n - 1)
                    split(sp_t[:, k % 2, :], sph[:, k % 2, :], spl[:, k % 2, :], sph_out, spl_out, n + 1)
                elif name == "s2c" and k == HC - 1:
                    blk = i + 1
                    dve.wait_ge(cont_out, blk + 1)
                    wait(dve, e1_done, blk * NJ)
                    split(cont[:, :], conth[:, :], contl[:, :], conth_out, contl_out, blk + 1)
                elif name == "rt1":
                    dve.wait_ge(rh_out, i + 1)
                    wait(dve, c2s_done, i * HC)
                    split(cont[:, :], midh[:, :], midl[:, :], rhh_out, rhl_out, i + 1)
                elif name == "logits":
                    r = i * 17
                    wide = [P, NT, NE]

                    def over(q):
                        return s4[:, q, :].unsqueeze(2).broadcast_to(wide)
                    dve.wait_ge(logits_done, i + 1)
                    dve.tensor_tensor(lg[:, :, :], bG[:, 0:NT * NE].rearrange("p (t e) -> p t e", e=NE),
                                      w["r_b2"][:, :].unsqueeze(1).broadcast_to(wide), ALU.add).then_inc(route, 1)
                    dve.wait_ge(route, r + 1)
                    dve.tensor_reduce(s4[:, 0, :], lg[:, :, :], AX.X, ALU.max).then_inc(route, 1)
                    dve.wait_ge(route, r + 2)
                    dve.tensor_tensor(lgm[:, :, :], lg[:, :, :], over(0), ALU.subtract).then_inc(route, 1)
                    dve.wait_ge(exp_out, i + 1)
                    dve.tensor_reduce(s4[:, 1, :], ex[:, :, :], AX.X, ALU.add).then_inc(route, 1)
                    dve.wait_ge(route, r + 4)
                    dve.reciprocal(s4[:, 2, :], s4[:, 1, :]).then_inc(route, 1)
                    dve.wait_ge(route, r + 5)
                    dve.tensor_tensor(w["probs"][:, :, 0:NE], ex[:, :, :], over(2), ALU.mult).then_inc(route, 1)
                    hold(2, route, r + 6)
                    for t in range(NT):
                        m = dve.max(top[:, t, :], w["probs"][:, t, 0:NE])
                    m.then_inc(route, 1)
                    dve.wait_ge(route, r + 7)
                    dve.tensor_copy(w["top2"][:, :, 0:2], top[:, :, 0:2]).then_inc(route, 1)
                    hold(3, route, r + 8)
                    for t in range(NT):
                        m = dve.match_replace(left[:, t, :], w["top2"][:, t, :], w["probs"][:, t, :], -2.0)
                    m.then_inc(route, 1)
                    dve.wait_ge(route, r + 9)
                    dve.scalar_tensor_tensor(out=picked[:, :, :], in0=left[:, :, 0:NE], scalar=0.0,
                                             in1=w["probs"][:, :, 0:NE], op0=ALU.is_lt, op1=ALU.mult).then_inc(route, 1)
                    dve.wait_ge(route, r + 10)
                    dve.tensor_reduce(s4[:, 3, :], picked[:, :, :], AX.X, ALU.add).then_inc(route, 1)
                    dve.wait_ge(route, r + 11)
                    dve.reciprocal(s4[:, 4, :], s4[:, 3, :]).then_inc(route, 1)
                    dve.wait_ge(route, r + 12)
                    dve.tensor_tensor(comb[:, :, :], picked[:, :, :], over(4), ALU.mult).then_inc(route, 1)
                    dve.wait_ge(route, r + 13)
                    dve.tensor_copy(comb_r[:, :, :], comb[:, :, :]).then_inc(route, 1)
                    dve.wait_ge(route, r + 14)
                    wait(dve, combt_done, i)
                    dve.tensor_copy(w["comb_pad"][:, :, 0:NE], f32(comb_r[:, :, :])).then_inc(route, 1)
                    dve.tensor_tensor(w["comb_pad"][:, :, NE:2 * NE], comb[:, :, :], f32(comb_r[:, :, :]),
                                      ALU.subtract).then_inc(route, 1)
                    dve.wait_ge(route, r + 16)
                    dve.tensor_copy(s4[:, 5, 0:1], s4[:, 4, 0:1]).then_inc(route, 1)
                    dve.wait_ge(route, r + 17)
                    dve.tensor_copy(s4[:, 5, 1:2], s4[:, 5, 0:1]).then_inc(comb_out, 1)
                elif name == "e1":
                    n = i * NJ + k
                    if k >= 4:
                        dve.wait_ge(e2_done, n - 3)
                    else:
                        wait(dve, dec_done, i * DEC)
                    if k % 2:
                        dve.wait_ge(hidh_act, i * (NJ // 2) + k // 2 + 1)
                    else:
                        dve.wait_ge(hid_out, n + 1)
                        dve.tensor_copy(hidh[:, k % 4, :], hid[:, k % 2, :]).then_inc(hidh_dve, 1)
                        dve.wait_ge(hidh_dve, i * (NJ // 2) + k // 2 + 1)
                    dve.tensor_tensor(hidl[:, k % 4, :], hid[:, k % 2, :], f32(hidh[:, k % 4, :]), ALU.subtract)\
                        .then_inc(hidl_out, 1)
                elif name == "z":
                    e = k
                    dve.wait_ge(e2_done, i * NJ + e * EC + EC)
                    dve.wait_ge(combb_out, i * NE + e + 1)
                    if e == 0:
                        wait(dve, accl_out, i)
                        target = acc[:, :]
                    else:
                        wait(dve, acc_out, i * (NE - 1) + max(e - 2, 0))
                        target = z[:, e % 2, :]
                    dve.tensor_tensor(target, bD[e % 3][:, :], comb_b[:, e % 2, :], ALU.mult).then_inc(z_out, 1)
                elif name == "acc":
                    dve.wait_ge(acc_out, (i + 1) * (NE - 1))
                    dve.wait_ge(logits_done, i + 1)
                    split(acc[:, :], midh[:, :], midl[:, :], acch_out, accl_out, i + 1)
                elif name == "dup":
                    dve.wait_ge(moeh_out, i + 1)
                    dve.tensor_tensor(midl[:, :], bG[:, :], f32(midh[:, :]), ALU.subtract).then_inc(moel_out, 1)
                elif name == "c2s":
                    n = i * HC + k
                    dve.wait_ge(rate_out, n + 1)
                    if k >= 4:
                        dve.wait_ge(dec_done, i * DEC + k - 3)
                    else:
                        dve.wait_ge(e2_done, i * NJ + NJ)
                    split(hid[:, k % 2, :], hidh[:, k % 4, :], hidl[:, k % 4, :], rateh_out, ratel_out, n + 1)
                elif name == "fin_stats":
                    blk = i - 1
                    if isinstance(blk, int) and blk < 0:
                        return
                    for t in range(NT):
                        dve.wait_ge(dec_out, blk * NT + t + 1)
                        dve.bn_stats(st2[:, t, :], out[:, t, :]).then_inc(fstat, 1)
                    hold(1, fstat, blk * NT + NT)
                    for t in range(NT):
                        dve.bn_aggr(mv2[:, t, :], st2[:, t, :]).then_inc(fmv, 1)
                elif name == "fin_norm":
                    blk = i - 1
                    if isinstance(blk, int) and blk < 0:
                        return
                    dve.wait_ge(frs, blk + 1)
                    dve.wait_ge(fmv, blk * NT + NT)
                    for t in range(NT):
                        dve.tensor_scalar(out[:, t, :], out[:, t, :], mv2[:, t, 0:1], rs2[:, t:t + 1],
                                          ALU.subtract, ALU.mult).then_inc(fnorm, 1)
            run(dve, step)

        @block.gpsimd
        def _(pool):
            def step(name, k, i, where, ahead, two_ahead):
                if name == "ln_stats":
                    blk = i + 2
                    pool.wait_ge(xmv, blk * NT + NT)
                    wait(pool, xnorm, blk * NT)
                    pool.tensor_tensor(ve[:, :], mv[:, :, 1], eps[:, :], ALU.add).then_inc(xve, 1)
                    pool.wait_ge(xve, blk + 1)
                    pool.tensor_tensor(rs[:, :], ve[:, :], w["half_down"][:, :], ALU.pow).then_inc(xrs, 1)
                elif name == "fin_stats":
                    blk = i - 1
                    if isinstance(blk, int) and blk < 0:
                        return
                    pool.wait_ge(fmv, blk * NT + NT)
                    wait(pool, fnorm, blk * NT)
                    pool.tensor_tensor(ve2[:, :], mv2[:, :, 1], eps4[:, :], ALU.add).then_inc(fve, 1)
                    pool.wait_ge(fve, blk + 1)
                    pool.tensor_tensor(rs2[:, :], ve2[:, :], w["half_down"][:, :], ALU.pow).then_inc(frs, 1)
                elif name == "fin_norm":
                    blk = i - 1
                    if isinstance(blk, int) and blk < 0:
                        return
                    for t in range(NT):
                        pool.wait_ge(fnorm, blk * NT + t + 1)
                        pool.tensor_tensor(out[:, t, :], out[:, t, :], w["ln_g"][:, :], ALU.mult).then_inc(scaled, 1)
                elif name == "z" and k:
                    e = k
                    pool.wait_ge(z_out, i * NE + e + 1)
                    wait(pool, acc_out, i * (NE - 1) + e - 1)
                    pool.tensor_tensor(acc[:, :], acc[:, :], z[:, e % 2, :], ALU.add).then_inc(acc_out, 1)
            pool.memset(eps[:, :], LN_EPS).then_inc(xeps, 1)
            pool.memset(eps4[:, :], 4 * LN_EPS).then_inc(xeps, 1)
            pool.wait_ge(xeps, 2)
            run(pool, step)



VW = 2 * P + 2


def run_keyvalue(nc, d, kv):
    with ExitStack() as ctx:
        b = Bench(nc, ctx, "k_")
        raw = [b.sb(f"raw{i}", [P, KC * DIM]) for i in range(2)]
        wkh, wkl = b.sb("wkh", [P, KC, DIM], F32R), b.sb("wkl", [P, KC, DIM], F32R)
        wvh, wvl = b.sb("wvh", [P, KC, DIM], F32R), b.sb("wvl", [P, KC, DIM], F32R)
        xt = [b.sb(f"xt{i}", [P, KC, BLK]) for i in range(2)]
        xh = [b.sb(f"xh{i}", [P, KC, BLK], F32R) for i in range(2)]
        xl = [b.sb(f"xl{i}", [P, KC, BLK], F32R) for i in range(2)]
        kh, kl = b.sb("kh", [P, 2, DIM], F32R), b.sb("kl", [P, 2, DIM], F32R)
        v = b.sb("v", [P, 2, KC, VW], F32R)
        onesf = b.sb("onesf", [P, 2, KC, 2])
        total = b.sb("total", [P, KC, VW])
        mask = b.sb("mask", [P, HG, HD])
        num = b.sb("num", [P, KC, P])
        numm = b.sb("numm", [P, KC, P])
        den, denh = b.sb("den", [P, KC, HG]), b.sb("denh", [P, KC, HG], F32R)
        zerof = b.sb("zerof", [P, KC * P])
        bK, bV = [b.psum(f"K{i}") for i in range(2)], [b.psum(f"V{i}") for i in range(2)]
        bA = [b.psum(f"A{g}") for g in range(KC)]

        w_in = [b.sem(f"w_in{i}") for i in range(2)]
        x_in = [b.sem(f"x_in{i}") for i in range(2)]
        wh_out, wl_out, consts, ready = (b.sem(n) for n in ("wh_out", "wl_out", "consts", "ready"))
        xh_out, xl_out, k_done, v_done, vk_done = (b.sem(n) for n in ("xh_out", "xl_out", "k_done", "v_done", "vk_done"))
        kh_out, kl_out, vh_out, vl_out = (b.sem(n) for n in ("kh_out", "kl_out", "vh_out", "vl_out"))
        summed, closed = b.sem("summed"), b.sem("closed")

        PAIRS = NB // 2
        PER_SEQ = PAIRS // BATCH
        TP = 2 * NT

        block = ctx.enter_context(nc.Block())

        @block.sync
        def _(sp):
            for k in range(2):
                sp.dma_start(raw[k][:, :], d["wkv"][k]).then_inc(w_in[k], 16)
            for h in range(2):
                sp.dma_start(xt[h][:, :, :], d["xt"][:, h * KC * BLK:(h + 1) * KC * BLK]
                             .rearrange("p (c n) -> p c n", c=KC)).then_inc(x_in[h], 16)
            with sp.Fori(1, PAIRS) as p:
                for h in range(2):
                    sp.wait_ge(xl_out, ((p - 1) * 2 + h + 1) * KC)
                    sp.dma_start(xt[h][:, :, :], d["xt"][:, bass.ds((p * 2 + h) * KC * BLK, KC * BLK)]
                                 .rearrange("p (c n) -> p c n", c=KC)).then_inc(x_in[h], 16)

        @block.gpsimd
        def _(pool):
            pool.memset(onesf[:, :, :, :], 1.0).then_inc(consts, 1)
            pool.memset(zerof[:, :], 0.0).then_inc(consts, 1)
            pool.memset(total[:, :, :], 0.0).then_inc(consts, 1)
            pool.memset(mask[:, :, :], 1.0).then_inc(consts, 1)
            pool.wait_ge(consts, 4)
            pool.affine_select(out=mask[:, :, :], in_=mask[:, :, :], compare_op=ALU.is_ge, fill=0.0, base=0,
                               pattern=[[-HD, HG], [0, HD]], channel_multiplier=1).then_inc(consts, 1)
            pool.wait_ge(consts, 5)
            pool.affine_select(out=mask[:, :, :], in_=mask[:, :, :], compare_op=ALU.is_ge, fill=0.0, base=HD - 1,
                               pattern=[[HD, HG], [0, HD]], channel_multiplier=-1).then_inc(consts, 1)

        @block.scalar
        def _(act):
            for k, t in enumerate((wkh, wvh)):
                act.wait_ge(w_in[k], 16)
                act.activation(t[:, :, :], raw[k][:, :].rearrange("p (c n) -> p c n", c=KC), ACT.Copy)\
                    .then_inc(wh_out, 1)

            def tile(n, j):
                act.wait_ge(k_done, n + 1)
                if isinstance(n, int):
                    wait(act, vk_done, n - 1)
                else:
                    act.wait_ge(vk_done, n - 1)
                act.activation(kh[:, j % 2, :], bK[j % 2][:, :], ACT.Relu).then_inc(kh_out, 1)
                act.wait_ge(v_done, n + 1)
                act.activation(v[:, j % 2, :, 0:P], bV[j % 2][:, :].rearrange("p (g f) -> p g f", g=KC), ACT.Relu)\
                    .then_inc(vh_out, 1)
            for j in range(TP):
                tile(j, j)
            with act.Fori(1, PAIRS) as p:
                for j in range(TP):
                    tile(p * TP + j, j)

        @block.tensor
        def _(pe):
            def project(n, j):
                h, t = divmod(j, NT)
                s = slice(t * P, (t + 1) * P)
                for c in range(KC):
                    a, z = c == 0, c == KC - 1
                    if c == 0:
                        wait(pe, kl_out, n - 1)
                        wait(pe, vl_out, n - 1)
                    pe.matmul(bK[j % 2][:, :], xh[h][:, c, s], wkh[:, c, :], start=a, stop=False)
                    pe.matmul(bK[j % 2][:, :], xh[h][:, c, s], wkl[:, c, :], start=False, stop=False)
                    pe.matmul(bV[j % 2][:, :], xh[h][:, c, s], wvh[:, c, :], start=a, stop=False)
                    pe.matmul(bV[j % 2][:, :], xh[h][:, c, s], wvl[:, c, :], start=False, stop=False)
                    mk = pe.matmul(bK[j % 2][:, :], xl[h][:, c, s], wkh[:, c, :], start=False, stop=z)
                    if z:
                        mk.then_inc(k_done, 1)
                    mv = pe.matmul(bV[j % 2][:, :], xl[h][:, c, s], wvh[:, c, :], start=False, stop=z)
                mv.then_inc(v_done, 1)

            def outer(n, j, p):
                pe.wait_ge(kl_out, n + 1)
                pe.wait_ge(vl_out, n + 1)
                if j == 0:
                    wait(pe, summed, p * KC)
                for g in range(KC):
                    s = slice(g * P, (g + 1) * P)
                    pe.matmul(bA[g][:, 0:VW], kh[:, j % 2, s], v[:, j % 2, g, :], start=(j == 0), stop=False)
                    m = pe.matmul(bA[g][:, 0:VW], kl[:, j % 2, s], v[:, j % 2, g, :], start=False, stop=(j == TP - 1))
                m.then_inc(vk_done, 1)

            def pair(p):
                for j in range(TP + 1):
                    if j < TP:
                        if j % NT == 0:
                            pe.wait_ge(xl_out, (p * 2 + j // NT + 1) * KC)
                        project(p * TP + j, j)
                    if j:
                        outer(p * TP + j - 1, j - 1, p)
            pe.wait_ge(wl_out, 2)
            pe.wait_ge(ready, 2)
            pair(0)
            with pe.Fori(1, PAIRS) as p:
                pair(p)

        @block.vector
        def _(dve):
            for k, (h, low) in enumerate(((wkh, wkl), (wvh, wvl))):
                dve.wait_ge(wh_out, k + 1)
                dve.tensor_tensor(low[:, :, :], raw[k][:, :].rearrange("p (c n) -> p c n", c=KC), f32(h[:, :, :]),
                                  ALU.subtract).then_inc(wl_out, 1)
            dve.wait_ge(consts, 6)
            dve.tensor_copy(v[:, :, :, 2 * P:VW], onesf[:, :, :, :]).then_inc(ready, 1)
            for s in range(BATCH):
                m = dve.tensor_copy(kv["den"][s][:, :, :], zerof[:, :].rearrange("p (c n) -> p c n", c=KC))
            m.then_inc(ready, 1)

            def split_x(p, h, c, n):
                if c == 0:
                    dve.wait_ge(x_in[h], p * 16 + 16)
                    wait(dve, v_done, (p - 1) * TP + (h + 1) * NT)
                dve.tensor_copy(xh[h][:, c, :], xt[h][:, c, :]).then_inc(xh_out, 1)
                dve.wait_ge(xh_out, n + 1)
                dve.tensor_tensor(xl[h][:, c, :], xt[h][:, c, :], f32(xh[h][:, c, :]), ALU.subtract)\
                    .then_inc(xl_out, 1)

            def tile(n, j):
                dve.wait_ge(kh_out, n + 1)
                dve.scalar_tensor_tensor(out=kl[:, j % 2, :], in0=bK[j % 2][:, :], scalar=0.0,
                                         in1=f32(kh[:, j % 2, :]), op0=ALU.max, op1=ALU.subtract).then_inc(kl_out, 1)
                dve.wait_ge(vh_out, n + 1)
                dve.scalar_tensor_tensor(out=v[:, j % 2, :, P:2 * P],
                                         in0=bV[j % 2][:, :].rearrange("p (g f) -> p g f", g=KC), scalar=0.0,
                                         in1=f32(v[:, j % 2, :, 0:P]), op0=ALU.max, op1=ALU.subtract)\
                    .then_inc(vl_out, 1)

            def pair(p, more):
                for j in range(TP):
                    tile(p * TP + j, j)
                    if more and j >= NT:
                        split_x(p + 1, 0, j - NT, (p + 1) * 2 * KC + j - NT)
                dve.wait_ge(vk_done, p * TP + TP)
                for g in range(KC):
                    dve.wait_ge(summed, p * KC + g)
                    dve.tensor_tensor(total[:, g, :], bA[g][:, 0:VW], total[:, g, :], ALU.add).then_inc(summed, 1)
                if more:
                    for c in range(KC):
                        split_x(p + 1, 1, c, (p + 1) * 2 * KC + KC + c)

            for h in range(2):
                for c in range(KC):
                    split_x(0, h, c, h * KC + c)
            done = 0
            for s in range(BATCH):
                first = s * PER_SEQ
                if s == 0:
                    pair(0, True)
                    with dve.Fori(1, PER_SEQ) as p:
                        pair(p, True)
                else:
                    with dve.Fori(first, PAIRS - 1) as p:
                        pair(p, True)
                    pair(PAIRS - 1, False)
                dve.wait_ge(summed, (first + PER_SEQ) * KC)

                def then(ins):
                    nonlocal done
                    done += 1
                    ins.then_inc(closed, 1)
                    dve.wait_ge(closed, done)
                then(dve.tensor_tensor(num[:, :, :], total[:, :, 0:P], total[:, :, P:2 * P], ALU.add))
                then(dve.tensor_tensor(numm[:, :, :], num[:, :, :],
                                       mask[:, :, :].rearrange("p a b -> p (a b)").unsqueeze(1)
                                       .broadcast_to([P, KC, P]), ALU.mult))
                then(dve.tensor_copy(kv["numh"][s][:, :, :], numm[:, :, :]))
                then(dve.tensor_tensor(kv["numl"][s][:, :, :], numm[:, :, :], f32(kv["numh"][s][:, :, :]),
                                       ALU.subtract))
                then(dve.tensor_tensor(den[:, :, :], mask[:, :, 0:1].rearrange("p a b -> p (a b)").unsqueeze(1)
                                       .broadcast_to([P, KC, HG]),
                                       total[:, :, 2 * P:2 * P + 1].broadcast_to([P, KC, HG]), ALU.mult))
                then(dve.tensor_copy(denh[:, :, :], den[:, :, :]))
                for g in range(KC):
                    a, z = g * HG, (g + 1) * HG
                    then(dve.tensor_copy(kv["den"][s][:, g, a:z], f32(denh[:, g, :])))
                    then(dve.tensor_tensor(kv["den"][s][:, g, 64 + a:64 + z], den[:, g, :], f32(denh[:, g, :]),
                                           ALU.subtract))
                then(dve.tensor_scalar(total[:, :, :], total[:, :, :], 0.0, None, ALU.mult)
                     if False else dve.memset(total[:, :, :], 0.0))



def run_attention(nc, d, kv, out_dram):
    with ExitStack() as ctx:
        b = Bench(nc, ctx, "a_")
        raw = [b.sb(f"raw{i}", [P, KC * DIM]) for i in range(2)]
        wqh, wql = b.sb("wqh", [P, KC, DIM], F32R), b.sb("wql", [P, KC, DIM], F32R)
        wph, wpl = b.sb("wph", [P, KC, DIM], F32R), b.sb("wpl", [P, KC, DIM], F32R)
        bias2, bias = b.sb("bias2", [P, 2, DIM]), b.sb("bias", [P, DIM])
        fan, fanf = b.sb("fan", [64, KC, P], F32R), b.sb("fanf", [64, KC, P])
        xt = b.sb("xt", [P, KC, BLK])
        xh, xl = b.sb("xh", [P, KC, BLK], F32R), b.sb("xl", [P, KC, BLK], F32R)
        qh, ql = b.sb("qh", [P, KC, BLK], F32R), b.sb("ql", [P, KC, BLK], F32R)
        ah, al = b.sb("ah", [P, KC, BLK], F32R), b.sb("al", [P, KC, BLK], F32R)
        at, rb = b.sb("at", [P, 2, BLK]), b.sb("rb", [P, 2, BLK])
        dlow, dsum = b.sb("dlow", [HEADS, BLK]), b.sb("dsum", [HEADS, BLK])
        rc, rc2 = b.sb("rc", [HEADS, BLK]), b.sb("rc2", [2 * HEADS, BLK], F32R)
        x, y, f = b.sb("x", [P, NT, DIM]), b.sb("y", [P, NT, DIM]), b.sb("f", [P, NT, DIM])
        bQ, bN = [b.psum(f"Q{i}") for i in range(2)], [b.psum(f"N{i}") for i in range(2)]
        bR, bDen = b.psum("R"), b.psum("Den")
        bP = [b.psum(f"P{i}") for i in range(2)]
        sem = b.sem
        w_in = [sem(f"w_in{i}") for i in range(2)]
        vec_in, xt_in, x_in, f_in, stored = sem("vec_in"), sem("xt_in"), sem("x_in"), sem("f_in"), sem("stored")
        wh_out, wl_out, consts, ready = sem("wh_out"), sem("wl_out"), sem("consts"), sem("ready")
        xh_out, xl_out, q_done, qh_out, ql_out = (sem(n) for n in ("xh_out", "xl_out", "q_done", "qh_out", "ql_out"))
        den_done, dlow_out, dsum_out, rc_out, rch_out, rcl_out = (sem(n) for n in (
            "den_done", "dlow_out", "dsum_out", "rc_out", "rch_out", "rcl_out"))
        fan_done, num_done, rb_out, at_out, ah_out, al_out = (sem(n) for n in (
            "fan_done", "num_done", "rb_out", "at_out", "ah_out", "al_out"))
        proj_done, y_out, xf_out, xfb_out = sem("proj_done"), sem("y_out"), sem("xf_out"), sem("xfb_out")

        def blocks(eng, body):
            half = NB // BATCH
            body(0, 0, True, False)
            body(1, 0, True, True)
            with eng.Fori(2, half) as i:
                body(i, 0, True, True)
            body(half, 0, True, True)
            with eng.Fori(half + 1, NB) as i:
                body(i, 1, True, True)
            body(NB, 1, False, True)

        block = ctx.enter_context(nc.Block())

        @block.sync
        def _(sp):
            for k in range(2):
                sp.dma_start(raw[k][:, :], d["wqp"][k]).then_inc(w_in[k], 16)
            sp.dma_start(bias2[:, :, :], d["bias2"][:, :, :]).then_inc(vec_in, 16)

            def body(i, s, ahead, attend):
                if ahead:
                    wait(sp, xl_out, i * KC)
                    sp.dma_start(xt[:, :, :], d["xt"][:, bass.ds(i * KC * BLK, KC * BLK)]
                                 .rearrange("p (c n) -> p c n", c=KC)).then_inc(xt_in, 16)
                if attend:
                    j = i - 1
                    wait(sp, y_out, j * NT)
                    sp.dma_start(x[:, :, :], d["x"][bass.ds(j * NT, NT), :, :].rearrange("t p c -> p t c"))\
                        .then_inc(x_in, 16)
                    wait(sp, xf_out, j * NT)
                    sp.dma_start(f[:, :, :], d["ffn"][bass.ds(j * NT, NT), :, :].rearrange("t p c -> p t c"))\
                        .then_inc(f_in, 16)
                    sp.wait_ge(y_out, j * NT + NT)
                    sp.dma_start(out_dram[bass.ds(j * NT, NT), :, :].rearrange("t p c -> p t c"), y[:, :, :])\
                        .then_inc(stored, 16)
            blocks(sp, body)
            sp.wait_ge(stored, 16 * NB)

        @block.gpsimd
        def _(pool):
            pool.memset(fanf[:, :, :], 1.0).then_inc(consts, 1)
            pool.wait_ge(consts, 1)
            n = 1
            for half in range(2):
                v = fanf[32 * half:32 * half + 32, :, :]
                for cm, st, base in ((-HD, 1, 0), (HD, -1, HD - 1)):
                    pool.wait_ge(consts, n)
                    pool.affine_select(out=v, in_=v, compare_op=ALU.is_ge, fill=0.0, base=base,
                                       pattern=[[st * P, KC], [st, P]], channel_multiplier=cm).then_inc(consts, 1)
                    n += 1
            pool.wait_ge(consts, 5)
            pool.wait_ge(vec_in, 16)
            pool.tensor_tensor(bias[:, :], bias2[:, 0, :], bias2[:, 1, :], ALU.add).then_inc(consts, 1)
            pool.wait_ge(consts, 6)

            def body(i, s, ahead, attend):
                if attend:
                    j = i - 1
                    pool.wait_ge(x_in, j * 16 + 16)
                    pool.wait_ge(f_in, j * 16 + 16)
                    for t in range(NT):
                        pool.tensor_tensor(x[:, t, :], x[:, t, :], f[:, t, :], ALU.add).then_inc(xf_out, 1)
                        pool.wait_ge(xf_out, j * NT + t + 1)
                        pool.tensor_tensor(x[:, t, :], x[:, t, :], bias[:, :], ALU.add).then_inc(xfb_out, 1)
            blocks(pool, body)

        @block.scalar
        def _(act):
            for k, t in enumerate((wqh, wph)):
                act.wait_ge(w_in[k], 16)
                act.activation(t[:, :, :], raw[k][:, :].rearrange("p (c n) -> p c n", c=KC), ACT.Copy)\
                    .then_inc(wh_out, 1)

            def body(i, s, ahead, attend):
                for m in range(KC):
                    if attend:
                        n = (i - 1) * KC + m
                        act.wait_ge(fan_done, n + 1)
                        wait(act, at_out, n - 1)
                        act.activation(rb[:, m % 2, :], bR[:, :], ACT.Copy).then_inc(rb_out, 1)
                    if ahead:
                        n = i * KC + m
                        act.wait_ge(q_done, n + 1)
                        if attend:
                            act.wait_ge(num_done, (i - 1) * KC + m + 1)
                        act.activation(qh[:, m, :], bQ[m % 2][:, :], ACT.Relu).then_inc(qh_out, 1)
                if ahead:
                    act.wait_ge(den_done, i + 1)
                    wait(act, dsum_out, i)
                    act.activation(dlow[:, :], bDen[64:64 + HEADS, :], ACT.Copy).then_inc(dlow_out, 1)
            blocks(act, body)

        @block.tensor
        def _(pe):
            pe.wait_ge(wl_out, 2)
            pe.wait_ge(ready, 1)

            def body(i, s, ahead, attend):
                for m in range(KC):
                    if attend:
                        n = (i - 1) * KC + m
                        pe.wait_ge(rcl_out, i)
                        wait(pe, rb_out, n)
                        pe.matmul(bR[:, :], fan[:, m, :], rc2[:, :], start=True, stop=True).then_inc(fan_done, 1)
                        wait(pe, at_out, n - 1)
                        pass3(pe, bN[m % 2][:, :], kv["numh"][s][:, m, :], kv["numl"][s][:, m, :],
                              qh[:, m, :], ql[:, m, :], True, True).then_inc(num_done, 1)
                    if ahead:
                        n = i * KC + m
                        if m == 0:
                            pe.wait_ge(xl_out, i * KC + KC)
                        wait(pe, ql_out, n - 1)
                        for c in range(KC):
                            o = slice(m * P, (m + 1) * P)
                            k = pass3(pe, bQ[m % 2][:, :], wqh[:, c, o], wql[:, c, o], xh[:, c, :], xl[:, c, :],
                                      c == 0, c == KC - 1)
                        k.then_inc(q_done, 1)
                if attend:
                    for t in range(NT):
                        n = (i - 1) * NT + t
                        wait(pe, y_out, n - 1)
                        for g in range(KC):
                            if t == 0:
                                pe.wait_ge(al_out, (i - 1) * KC + g + 1)
                            o = slice(t * P, (t + 1) * P)
                            pe.matmul(bP[t % 2][:, :], ah[:, g, o], wph[:, g, :], start=(g == 0), stop=False)
                            pe.matmul(bP[t % 2][:, :], ah[:, g, o], wpl[:, g, :], start=False, stop=False)
                            k = pe.matmul(bP[t % 2][:, :], al[:, g, o], wph[:, g, :], start=False, stop=(g == KC - 1))
                        k.then_inc(proj_done, 1)
                        if t == 0 and ahead:
                            denominators(i, s, attend)
                elif ahead:
                    denominators(i, s, attend)

            def denominators(i, s, attend):
                if isinstance(i, int) and i == NB // BATCH:
                    s = 1
                pe.wait_ge(ql_out, i * KC + KC)
                wait(pe, dsum_out, i)
                for g in range(KC):
                    pe.matmul(bDen[:, :], kv["den"][s][:, g, :], qh[:, g, :], start=(g == 0), stop=False)
                    k = pe.matmul(bDen[:, :], kv["den"][s][:, g, :], ql[:, g, :], start=False, stop=(g == KC - 1))
                k.then_inc(den_done, 1)
            blocks(pe, body)

        @block.vector
        def _(dve):
            for k, (h, low) in enumerate(((wqh, wql), (wph, wpl))):
                dve.wait_ge(wh_out, k + 1)
                dve.tensor_tensor(low[:, :, :], raw[k][:, :].rearrange("p (c n) -> p c n", c=KC), f32(h[:, :, :]),
                                  ALU.subtract).then_inc(wl_out, 1)
            dve.wait_ge(consts, 5)
            dve.tensor_copy(fan[:, :, :], fanf[:, :, :]).then_inc(ready, 1)

            def split_x(i):
                dve.wait_ge(xt_in, i * 16 + 16)
                wait(dve, q_done, i * KC)
                for c in range(KC):
                    dve.tensor_copy(xh[:, c, :], xt[:, c, :]).then_inc(xh_out, 1)
                    dve.wait_ge(xh_out, i * KC + c + 1)
                    dve.tensor_tensor(xl[:, c, :], xt[:, c, :], f32(xh[:, c, :]), ALU.subtract).then_inc(xl_out, 1)

            def body(i, s, ahead, attend):
                for m in range(KC):
                    if attend:
                        n = (i - 1) * KC + m
                        dve.wait_ge(rb_out, n + 1)
                        dve.wait_ge(num_done, n + 1)
                        wait(dve, al_out, n - 1)
                        dve.tensor_tensor(at[:, m % 2, :], bN[m % 2][:, :], rb[:, m % 2, :], ALU.mult)\
                            .then_inc(at_out, 1)
                        dve.wait_ge(at_out, n + 1)
                        wait(dve, proj_done, (i - 1) * NT)
                        dve.tensor_copy(ah[:, m, :], at[:, m % 2, :]).then_inc(ah_out, 1)
                        dve.wait_ge(ah_out, n + 1)
                        dve.tensor_tensor(al[:, m, :], at[:, m % 2, :], f32(ah[:, m, :]), ALU.subtract)\
                            .then_inc(al_out, 1)
                    if ahead:
                        n = i * KC + m
                        dve.wait_ge(qh_out, n + 1)
                        dve.scalar_tensor_tensor(out=ql[:, m, :], in0=bQ[m % 2][:, :], scalar=0.0,
                                                 in1=f32(qh[:, m, :]), op0=ALU.max, op1=ALU.subtract)\
                            .then_inc(ql_out, 1)
                if attend:
                    out_tile(i, 0)
                if ahead:
                    dve.wait_ge(dlow_out, i + 1)
                    wait(dve, rc_out, i)
                    dve.scalar_tensor_tensor(out=dsum[:, :], in0=bDen[0:HEADS, :], scalar=DEN_EPS, in1=dlow[:, :],
                                             op0=ALU.add, op1=ALU.add).then_inc(dsum_out, 1)
                    dve.wait_ge(dsum_out, i + 1)
                    dve.reciprocal(rc[:, :], dsum[:, :]).then_inc(rc_out, 1)
                    dve.wait_ge(rc_out, i + 1)
                    wait(dve, fan_done, i * KC)
                    dve.tensor_copy(rc2[0:HEADS, :], rc[:, :]).then_inc(rch_out, 1)
                    dve.wait_ge(rch_out, i + 1)
                    dve.tensor_tensor(rc2[HEADS:2 * HEADS, :], rc[:, :], f32(rc2[0:HEADS, :]), ALU.subtract)\
                        .then_inc(rcl_out, 1)
                if attend:
                    for t in range(1, NT):
                        out_tile(i, t)
                if ahead and not (isinstance(i, int) and i == NB - 1) and not (isinstance(i, int) and i + 1 >= NB):
                    split_next(i)

            def out_tile(i, t):
                n = (i - 1) * NT + t
                dve.wait_ge(proj_done, n + 1)
                dve.wait_ge(xfb_out, n + 1)
                if t == 0:
                    wait(dve, stored, (i - 1) * 16)
                dve.tensor_tensor(y[:, t, :], bP[t % 2][:, :], x[:, t, :], ALU.add).then_inc(y_out, 1)

            def split_next(i):
                split_x(i + 1)
            split_x(0)
            half = NB // BATCH
            body(0, 0, True, False)
            body(1, 0, True, True)
            with dve.Fori(2, half) as i:
                body(i, 0, True, True)
            body(half, 0, True, True)
            with dve.Fori(half + 1, NB - 1) as i:
                body(i, 1, True, True)
            body(NB - 1, 1, True, True)
            body(NB, 1, False, True)


def build(nc, d, out_dram):
    d = dict(d)
    d["xt"] = nc.dram_tensor("xt_scratch", [P, NB * KC * BLK], F32).ap()
    d["ffn"] = nc.dram_tensor("ffn_scratch", [TOK // P, P, DIM], F32).ap()
    with ExitStack() as ctx:
        b = Bench(nc, ctx, "w_")
        w = ffn_weights(b, nc, d)
        load_ffn(nc, d, w)
        run_ffn(nc, d, w)
    with ExitStack() as ctx:
        b = Bench(nc, ctx, "kv_")
        kv = {"numh": [b.sb(f"numh{s}", [P, KC, P], F32R) for s in range(BATCH)],
              "numl": [b.sb(f"numl{s}", [P, KC, P], F32R) for s in range(BATCH)],
              "den": [b.sb(f"den{s}", [P, KC, P], F32R) for s in range(BATCH)]}
        run_keyvalue(nc, d, kv)
        run_attention(nc, d, kv, out_dram)



def kernel(**inputs):
    import numpy as np
    import concourse.bacc as bacc
    from concourse.bass_utils import run_bass_kernel_spmd

    a = {k.removeprefix("L0_ffn_").removeprefix("L0_attn_"): np.asarray(v) for k, v in inputs.items()}

    def chunked(m):
        c = m.shape[0] // P
        return m.reshape(c, P, -1).transpose(1, 0, 2).reshape(P, -1)

    def every(v):
        return np.broadcast_to(v.reshape(1, -1), (P, v.size))

    def twice(m):
        return np.concatenate([m, m], axis=0)

    qkv_t = a["qkv_weight"].T
    host = {
        "x": a["x"].reshape(TOK // P, P, DIM),
        "enc_w": chunked(a["enc_w"]),
        "s2c_w": chunked(a["s2c_w"]),
        "e_w1": twice(a["e_w1"].transpose(1, 0, 2).reshape(MOE, NE * EH)),
        "e_w2": chunked(a["e_w2"].reshape(NE * EH, MOE)),
        "c2s_w": twice(a["c2s_w"]),
        "dec_w": chunked(a["dec_w"]),
        "r_w1": twice(np.concatenate([a["r_w1"], a["r_w1"]], axis=1)),
        "r_w2": twice(a["r_w2"]),
        "e_b2": twice(np.concatenate([a["e_b2"], a["e_b2"]], axis=1)),
        "enc_b": a["enc_b"].reshape(HC, P).T,
        "c2s_b": a["c2s_b"].reshape(HC, P).T,
        "e_b1": a["e_b1"].reshape(NJ, P).T,
        "r_b1": twice(a["r_b1"].reshape(MOE, 1)),
        "s2c_b": twice(a["s2c_b"].reshape(MOE, 1)),
        "r_b2": every(a["r_b2"]),
        "ln_g": every(a["ln_g"]),
        "dec_b": every(a["dec_b"]),
        "wkv": np.stack([chunked(qkv_t[:, DIM:2 * DIM]), chunked(qkv_t[:, 2 * DIM:3 * DIM])]),
        "wqp": np.stack([chunked(qkv_t[:, 0:DIM]), chunked(a["proj_weight"].T)]),
        "bias2": np.stack([every(a["proj_bias"]), every(a["ln_b"])], axis=1),
    }
    nc = bacc.Bacc("TRN2", target_bir_lowering=False, num_devices=1)
    arrays, d = {}, {}
    for name, v in host.items():
        v = np.ascontiguousarray(v)
        arrays[f"in_{name}"] = v
        d[name] = nc.dram_tensor(f"in_{name}", v.shape, mybir.dt.from_np(v.dtype), kind="ExternalInput").ap()
    out = nc.dram_tensor("out_y", (TOK // P, P, DIM), F32, kind="ExternalOutput").ap()
    build(nc, d, out)
    r = run_bass_kernel_spmd(nc, [arrays], core_ids=[0])
    return r.results[0]["out_y"].reshape(BATCH, SEQ, DIM)
```

```python
from contextlib import ExitStack

import concourse.bass as bass
from concourse import mybir

ALU = mybir.AluOpType
ACT = mybir.ActivationFunctionType
AX = mybir.AxisListType
F32 = mybir.dt.float32
F32R = mybir.dt.float32r

P = 128
BATCH, SEQ, DIM = 2, 4096, 512
TOK = BATCH * SEQ
BLK = 512
NB = TOK // BLK
NT = BLK // P
KC = DIM // P
HID = 1024
HC = HID // P
MOE = 64
NE = 8
EH = 512
EC = EH // P
NJ = NE * EC
HEADS, HD = 32, 16
HG = P // HD
LN_EPS = 1e-5
DEN_EPS = 1e-15


def wait(eng, sem, value):
    if isinstance(value, int) and value <= 0:
        return
    eng.wait_ge(sem, value)


def f32(ap):
    return ap.bitcast(F32)


class Bench:

    def __init__(self, nc, ctx, tag):
        self.nc, self.ctx, self.tag = nc, ctx, tag

    def sb(self, name, shape, dt=F32):
        return self.ctx.enter_context(self.nc.sbuf_tensor(self.tag + name, shape, dt))

    def psum(self, name):
        return self.ctx.enter_context(self.nc.psum_tensor(self.tag + name, [P, 512], F32))

    def sem(self, name):
        return self.ctx.enter_context(self.nc.semaphore(self.tag + name))


def pass3(pe, out, w_hi, w_lo, x_hi, x_lo, start, stop):
    pe.matmul(out, w_hi, x_hi, start=start, stop=False)
    pe.matmul(out, w_lo, x_hi, start=False, stop=False)
    return pe.matmul(out, w_hi, x_lo, start=False, stop=stop)



def ffn_weights(b, nc, d):
    w = {}
    w["enc_h"], w["enc_l"] = b.sb("enc_h", [P, KC, HID], F32R), b.sb("enc_l", [P, KC, HID], F32R)
    w["dec_h"], w["dec_l"] = b.sb("dec_h", [P, HC, DIM], F32R), b.sb("dec_l", [P, HC, DIM], F32R)
    w["s2c_h"], w["s2c_l"] = b.sb("s2c_h", [P, HC, P], F32R), b.sb("s2c_l", [P, HC, P], F32R)
    w["e1"] = b.sb("e1", [P, NE * EH], F32R)
    w["e2"] = b.sb("e2", [P, NJ, P], F32R)
    w["c2s"] = b.sb("c2s", [P, HID], F32R)
    w["r1"] = b.sb("r1", [P, P], F32R)
    w["r2"] = b.sb("r2", [P, NE], F32R)
    w["b2h"], w["b2l"] = b.sb("b2h", [2 * NE, P], F32R), b.sb("b2l", [2 * NE, P], F32R)
    w["twice"] = b.sb("twice", [P, P], F32R)
    w["pick"] = b.sb("pick", [2 * NE, NE], F32R)
    w["ident"] = b.sb("ident", [P, P], F32)
    w["rows"] = b.sb("rows", [P, BLK], F32R)
    w["pick_bias"] = b.sb("pick_bias", [P, P], F32R)
    w["enc_b"], w["c2s_b"] = b.sb("enc_b", [P, HC]), b.sb("c2s_b", [P, HC])
    w["e_b1"] = b.sb("e_b1", [P, NJ])
    w["r_b1"], w["s2c_b"] = b.sb("r_b1", [P, 1]), b.sb("s2c_b", [P, 1])
    w["r_b2"] = b.sb("r_b2", [P, NE])
    w["ln_g"] = b.sb("ln_g", [P, DIM])
    w["half_down"] = b.sb("half_down", [P, NT])
    w["probs"] = b.sb("probs", [P, NT, 2 * NE])
    w["top2"] = b.sb("top2", [P, NT, NE])
    w["comb_pad"] = b.sb("comb_pad", [P, NT, P])
    return w


def load_ffn(nc, d, w):
    with ExitStack() as ctx:
        b = Bench(nc, ctx, "fw_")
        CH = 2048
        raw = [b.sb(f"raw{i}", [P, CH]) for i in range(4)]
        small = b.sb("small", [P, 4 * P])
        ones = b.sb("ones", [P, P], F32R)
        onesf = b.sb("onesf", [P, P])
        twicef = b.sb("twicef", [P, P])
        pickf = b.sb("pickf", [2 * NE, NE])
        pbf = b.sb("pbf", [P, P])
        dec_b = b.sb("dec_b", [P, DIM])
        bias = b.sb("bias", [P, DIM])
        sums = b.psum("sums")
        row = b.psum("row")
        arrived = [b.sem(f"arrived{i}") for i in range(4)]
        small_in, vectors_in = b.sem("small_in"), b.sem("vectors_in")
        hi_done, lo_done = b.sem("hi_done"), b.sem("lo_done")
        consts, const_copied, summed, biased = (b.sem(n) for n in ("consts", "const_copied", "summed", "biased"))

        def flat(t):
            return t[:, :, :].rearrange("p a b -> p (a b)")
        enc_h, enc_l, dec_h, dec_l = (flat(w[n]) for n in ("enc_h", "enc_l", "dec_h", "dec_l"))
        chunks = []
        for c in range(2):
            s = slice(c * CH, (c + 1) * CH)
            chunks.append((d["enc_w"][:, s], CH, [(enc_h[:, s], enc_l[:, s], 0)]))
        chunks.append((d["s2c_w"][:, :], HC * MOE, [(w["s2c_h"][:, :, 0:MOE], w["s2c_l"][:, :, 0:MOE], 0),
                                                    (w["s2c_h"][:, :, MOE:P], w["s2c_l"][:, :, MOE:P], 0)]))
        for c in range(2):
            s = slice(c * CH, (c + 1) * CH)
            chunks.append((d["e_w1"][:, s], CH, [(w["e1"][:, s], None, MOE)]))
        chunks.append((d["e_w2"][:, :], CH, [(w["e2"][:, :, 0:MOE], w["e2"][:, :, MOE:P], 0)]))
        chunks.append((d["c2s_w"][:, :], HID, [(w["c2s"][:, :], None, MOE)]))
        for c in range(2):
            s = slice(c * CH, (c + 1) * CH)
            chunks.append((d["dec_w"][:, s], CH, [(dec_h[:, s], dec_l[:, s], 0)]))
        jobs = [(n, src, size, t) for n, (src, size, ts) in enumerate(chunks) for t in ts]
        hi_of = {}
        for k, (n, _, _, _) in enumerate(jobs):
            hi_of[n] = k + 1

        block = ctx.enter_context(nc.Block())

        @block.sync
        def _(sp):
            for n, (src, size, _) in enumerate(chunks):
                if n >= 4:
                    sp.wait_ge(lo_done, hi_of[n - 4])
                sp.dma_start(raw[n % 4][:, 0:size], src).then_inc(arrived[n % 4], 16)

        @block.gpsimd
        def _(pool):
            pool.dma_start(small[:, 0:P], d["r_w1"][:, :]).then_inc(small_in, 16)
            pool.dma_start(small[:, P:P + NE], d["r_w2"][:, :]).then_inc(small_in, 16)
            pool.dma_start(small[0:2 * NE, 2 * P:3 * P], d["e_b2"][:, :]).then_inc(small_in, 16)
            for k, name in (("enc_b", "enc_b"), ("c2s_b", "c2s_b"), ("e_b1", "e_b1"), ("r_b1", "r_b1"),
                            ("s2c_b", "s2c_b"), ("r_b2", "r_b2"), ("ln_g", "ln_g")):
                pool.dma_start(w[k][:, :], d[name][:, :]).then_inc(vectors_in, 16)
            pool.dma_start(dec_b[:, :], d["dec_b"][:, :]).then_inc(vectors_in, 16)
            pool.memset(w["ident"][:, :], 0.0).then_inc(consts, 1)
            pool.memset(twicef[:, :], 0.0).then_inc(consts, 1)
            pool.memset(pickf[:, :], 0.0).then_inc(consts, 1)
            pool.memset(onesf[:, :], 1.0).then_inc(consts, 1)
            pool.memset(pbf[:, :], 0.0).then_inc(consts, 1)
            pool.memset(w["half_down"][:, :], -0.5).then_inc(consts, 1)
            pool.memset(w["probs"][:, :, :], -1.0).then_inc(consts, 1)
            pool.memset(w["top2"][:, :, :], -1.0).then_inc(consts, 1)
            pool.memset(w["comb_pad"][:, :, :], 0.0).then_inc(consts, 1)
            pool.wait_ge(consts, 9)

            def diagonal(t, base, n):
                pool.wait_ge(consts, n)
                pool.affine_select(out=t, in_=t, compare_op=ALU.not_equal, fill=1.0, base=base,
                                   pattern=[[-1, t.shape[1]]], channel_multiplier=1).then_inc(consts, 1)
            diagonal(w["ident"][:, :], 0, 9)
            for k, base in enumerate((0, MOE, -MOE)):
                diagonal(twicef[:, :], base, 10 + k)
            for k, base in enumerate((0, -NE)):
                diagonal(pickf[:, :], base, 13 + k)
            for k, r in enumerate((64, 96)):
                pool.memset(pbf[r:r + 1, :], 1.0).then_inc(consts, 1)

        @block.scalar
        def _(act):
            for k, (n, _, size, (hi, _, _)) in enumerate(jobs):
                act.wait_ge(arrived[n % 4], 16 * (n // 4 + 1))
                src = raw[n % 4][:, 0:size]
                if len(hi.shape) == 3:
                    src = src.rearrange("p (a b) -> p a b", b=hi.shape[2])
                act.activation(hi, src, ACT.Copy).then_inc(hi_done, 1)

        @block.vector
        def _(dve):
            dve.wait_ge(consts, 17)
            dve.tensor_copy(ones[:, :], onesf[:, :]).then_inc(const_copied, 1)
            dve.tensor_copy(w["twice"][:, :], twicef[:, :]).then_inc(const_copied, 1)
            dve.tensor_copy(w["pick"][:, :], pickf[:, :]).then_inc(const_copied, 1)
            dve.tensor_copy(w["pick_bias"][:, :], pbf[:, :]).then_inc(const_copied, 1)
            dve.wait_ge(small_in, 48)
            dve.tensor_copy(w["r1"][:, :], small[:, 0:P]).then_inc(const_copied, 1)
            dve.tensor_copy(w["r2"][:, :], small[:, P:P + NE]).then_inc(const_copied, 1)
            dve.tensor_copy(w["b2h"][:, :], small[0:2 * NE, 2 * P:3 * P]).then_inc(const_copied, 1)
            dve.wait_ge(const_copied, 7)
            dve.tensor_tensor(w["r1"][MOE:P, :], small[MOE:P, 0:P], f32(w["r1"][MOE:P, :]),
                              ALU.subtract).then_inc(const_copied, 1)
            dve.tensor_tensor(w["r2"][MOE:P, :], small[MOE:P, P:P + NE], f32(w["r2"][MOE:P, :]),
                              ALU.subtract).then_inc(const_copied, 1)
            dve.tensor_tensor(w["b2l"][:, :], small[0:2 * NE, 2 * P:3 * P], f32(w["b2h"][:, :]),
                              ALU.subtract).then_inc(const_copied, 1)
            dve.wait_ge(vectors_in, 16 * 8)
            dve.tensor_scalar(w["enc_b"][:, :], w["enc_b"][:, :], 0.5, None, ALU.mult).then_inc(const_copied, 1)
            dve.tensor_scalar(w["c2s_b"][:, :], w["c2s_b"][:, :], 0.5, None, ALU.mult).then_inc(const_copied, 1)
            for k, (n, _, size, (hi, lo, r)) in enumerate(jobs):
                dve.wait_ge(hi_done, k + 1)
                if lo is None:
                    lo, hi = hi[r:, :], hi[r:, :]
                src = raw[n % 4][r:, 0:size]
                if len(hi.shape) == 3:
                    src = src.rearrange("p (a b) -> p a b", b=hi.shape[2])
                dve.tensor_tensor(lo, src, f32(hi), ALU.subtract).then_inc(lo_done, 1)
            dve.wait_ge(summed, 1)
            dve.scalar_tensor_tensor(out=w["s2c_b"][:, :], in0=sums[:, 0:1], scalar=0.5, in1=w["s2c_b"][:, :],
                                     op0=ALU.mult, op1=ALU.add).then_inc(biased, 1)
            dve.wait_ge(summed, 2)
            dve.scalar_tensor_tensor(out=bias[:, :], in0=dec_b[:, :], scalar=2.0, in1=row[:, :],
                                     op0=ALU.mult, op1=ALU.add).then_inc(biased, 1)
            dve.wait_ge(biased, 2)
            dve.tensor_copy(w["rows"][64:P, :], bias[64:P, :]).then_inc(biased, 1)
            dve.wait_ge(biased, 3)
            dve.tensor_tensor(w["rows"][96:P, :], bias[96:P, :], f32(w["rows"][96:P, :]),
                              ALU.subtract).then_inc(biased, 1)
            dve.wait_ge(biased, 4)

        @block.tensor
        def _(pe):
            pe.wait_ge(lo_done, len(jobs))
            pe.wait_ge(const_copied, 1)
            for k in range(HC):
                pe.matmul(sums[:, 0:2], w["s2c_h"][:, k, :], ones[:, 0:2], start=(k == 0), stop=False)
                m = pe.matmul(sums[:, 0:2], w["s2c_l"][:, k, :], ones[:, 0:2], start=False, stop=(k == HC - 1))
            m.then_inc(summed, 1)
            for k in range(HC):
                pe.matmul(row[:, :], ones[:, :], w["dec_h"][:, k, :], start=(k == 0), stop=False)
                m = pe.matmul(row[:, :], ones[:, :], w["dec_l"][:, k, :], start=False, stop=(k == HC - 1))
            m.then_inc(summed, 1)


def ffn_steps():
    at = {}

    def put(j, *steps):
        at.setdefault(j, []).extend(steps)
    for q in range(4):
        put(2 * q, ("route", q))
    put(8, ("comb_t", 0))
    put(9, ("spread", 0), ("z", 0))
    put(10, ("spread", 1), ("z", 1))
    for e in range(2, NE):
        put(4 * e + (1 if e > 2 else 3), ("spread", e))
        put(4 * e + 3, ("z", e))
    for m, j in enumerate((0, 3, 6, 9, 13, 17, 22, 27)):
        if m >= 2:
            put(j, ("s2c", m - 2))
        put(j, ("enc", m))
    for t in range(NT):
        put(12 + t, ("fin_stats", t))
        put(19 + t, ("ln_stats", t))
    put(18, ("fin_norm", 0))
    put(25, ("ln_norm", 0))
    steps = [("rt1", 0)] + [("e1", j) for j in range(4)] + [("logits", 0)]
    for j in range(NJ):
        steps.append(("e2", j))
        if j + 4 < NJ:
            steps.append(("e1", j + 4))
        steps += at.get(j, [])
    steps += [("s2c", 6), ("turn", 0), ("acc", 0), ("turn", 1), ("turn", 2), ("dup", 0), ("s2c", 7), ("turn", 3),
              ("c2s", 0), ("dec_bias", 0), ("c2s", 1)]
    for k in range(HC):
        steps.append(("dec", k))
        if k + 2 < HC:
            steps.append(("c2s", k + 2))
    return steps


def ffn_prologue_steps():
    steps = [("ln_stats", t) for t in range(NT)] + [("ln_norm", 0)] + [("turn", c) for c in range(KC)]
    for m in range(HC + 2):
        if m < HC:
            steps.append(("enc", m))
        if m == 4:
            steps += [("ln_stats", 10 + t) for t in range(NT)] + [("ln_norm", 10)]
        if m >= 2:
            steps.append(("s2c", m - 2))
    return steps + [("turn", 10 + c) for c in range(KC)]


def run_ffn(nc, d, w):
    with ExitStack() as ctx:
        b = Bench(nc, ctx, "f_")
        x = b.sb("x", [P, NT, DIM])
        xt = b.sb("xt", [P, 2, BLK])
        xh, xl = b.sb("xh", [P, KC, BLK], F32R), b.sb("xl", [P, KC, BLK], F32R)
        sp_t, sph, spl = b.sb("sp_t", [P, 2, BLK]), b.sb("sph", [P, 2, BLK], F32R), b.sb("spl", [P, 2, BLK], F32R)
        hid, hidh, hidl = b.sb("hid", [P, 2, BLK]), b.sb("hidh", [P, 4, BLK], F32R), b.sb("hidl", [P, 4, BLK], F32R)
        cont, conth, contl = b.sb("cont", [P, BLK]), b.sb("conth", [P, BLK], F32R), b.sb("contl", [P, BLK], F32R)
        midh, midl = b.sb("midh", [P, BLK], F32R), b.sb("midl", [P, BLK], F32R)
        comb_b = b.sb("comb_b", [P, 2, BLK])
        z, acc = b.sb("z", [P, 2, BLK]), b.sb("acc", [P, BLK])
        out = b.sb("out", [P, NT, DIM])
        st, mv = b.sb("st", [P, NT, 6]), b.sb("mv", [P, NT, 2])
        ve, rs = b.sb("ve", [P, NT]), b.sb("rs", [P, NT])
        st2, mv2 = b.sb("st2", [P, NT, 6]), b.sb("mv2", [P, NT, 2])
        ve2, rs2 = b.sb("ve2", [P, NT]), b.sb("rs2", [P, NT])
        lg, lgm, ex = b.sb("lg", [P, NT, NE]), b.sb("lgm", [P, NT, NE]), b.sb("ex", [P, NT, NE])
        top, left = b.sb("top", [P, NT, NE]), b.sb("left", [P, NT, 2 * NE])
        picked, comb = b.sb("picked", [P, NT, NE]), b.sb("comb", [P, NT, NE])
        comb_r = b.sb("comb_r", [P, NT, NE], F32R)
        s4 = b.sb("s4", [P, 5, NT])
        held = b.sb("held", [P, 4])
        eps, eps4 = b.sb("eps", [P, NT]), b.sb("eps4", [P, NT])

        bE, bD = [b.psum(f"E{i}") for i in range(2)], [b.psum(f"D{i}") for i in range(4)]
        bS, bG = b.psum("S"), b.psum("G")

        names = {}

        def sem(name):
            names[name] = b.sem(name)
            return names[name]

        x_in, out_stored = sem("x_in"), sem("out_stored")
        xt_stored = [sem("xt_stored0"), sem("xt_stored1")]
        turned, enc_done, s2c_done, rt1_done, logits_done = (sem(n) for n in (
            "turned", "enc_done", "s2c_done", "rt1_done", "logits_done"))
        combt_done, spread_done, e1_done, e2_done, dup_done, c2s_done, dec_done = (sem(n) for n in (
            "combt_done", "spread_done", "e1_done", "e2_done", "dup_done", "c2s_done", "dec_done"))
        xt_out, sp_out, rate_out, cont_out, rh_out, exp_out = (sem(n) for n in (
            "xt_out", "sp_out", "rate_out", "cont_out", "rh_out", "exp_out"))
        combrow_out, combb_out, hid_out, hidh_act, moeh_out, dec_out = (sem(n) for n in (
            "combrow_out", "combb_out", "hid_out", "hidh_act", "moeh_out", "dec_out"))
        xstat, xmv, xnorm, xh_out, xl_out, sph_out, spl_out = (sem(n) for n in (
            "xstat", "xmv", "xnorm", "xh_out", "xl_out", "sph_out", "spl_out"))
        hidh_dve, hidl_out, rateh_out, ratel_out, conth_out, contl_out = (sem(n) for n in (
            "hidh_dve", "hidl_out", "rateh_out", "ratel_out", "conth_out", "contl_out"))
        rhh_out, rhl_out, route, z_out, acch_out, accl_out, moel_out = (sem(n) for n in (
            "rhh_out", "rhl_out", "route", "z_out", "acch_out", "accl_out", "moel_out"))
        last_out = sem("last_out")
        fstat, fmv, fnorm = sem("fstat"), sem("fmv"), sem("fnorm")
        xeps = sem("xeps")
        xve, xrs, acc_out, fve, frs, scaled = (sem(n) for n in ("xve", "xrs", "acc_out", "fve", "frs", "scaled"))

        def prior_on_e(order):
            e_uses = [s for s in order if s[0] in ("enc", "e1", "turn")]
            return {s: (k % 2, e_uses[k - 2] if k >= 2 else None) for k, s in enumerate(e_uses)}

        steps = ffn_steps()
        uses_full = prior_on_e(steps)
        n_full = [s for s in steps if s[0] in ("enc", "e1", "turn")]
        assert len(n_full) % 2 == 0 and len([s for s in n_full if s[0] != "turn"]) % 2 == 0

        block = ctx.enter_context(nc.Block())

        def run(eng, step, idle=()):
            for name, k in ffn_prologue_steps():
                if name in ("turn", "ln_stats", "ln_norm"):
                    step(name, k % 10, -2 if k < 10 else -1, "first", True, True)
                else:
                    step(name, k, -1, "first", True, True)

            def body(i, where, ahead, two_ahead):
                for name, k in steps:
                    if name in ("enc", "s2c") and not ahead:
                        continue
                    if name in ("turn", "ln_stats", "ln_norm") and not two_ahead:
                        continue
                    step(name, k, i, where, ahead, two_ahead)

            body(0, "peeled", True, True)
            with eng.Fori(1, NB - 2) as i:
                body(i, "loop", True, True)
            body(NB - 2, "peeled", True, False)
            body(NB - 1, "peeled", False, False)
            for name, k in [("fin_stats", t) for t in range(NT)] + [("fin_norm", 0)]:
                step(name, k, NB, "peeled", False, False)

        def e_bank(name, k, where, ahead, two_ahead):
            if where == "first":
                return bE[k % 2]
            order = [s for s in steps if s[0] in ("enc", "e1", "turn")]
            if not ahead:
                order = [s for s in order if s[0] != "enc"]
            if not two_ahead:
                order = [s for s in order if s[0] != "turn"]
            return bE[order.index((name, k)) % 2]

        def wait_e_bank(pe, name, k, i, where, ahead, two_ahead):
            def read(s, blk_i):
                n, q = s
                if n == "enc":
                    wait(pe, sp_out, (blk_i + 1) * HC + q + 1)
                elif n == "turn":
                    wait(pe, xt_out, (blk_i + 2) * KC + q + 1)
                else:
                    wait(pe, hid_out, blk_i * NJ + q + 1)
            if where == "first":
                if name == "turn" and k < 2 and isinstance(i, int) and i == -2:
                    return
                if name == "turn":
                    read(("turn", k - 2) if k >= 2 else ("enc", HC - 2 + k), -2 if i == -2 else -1)
                else:
                    read(("enc", k - 2), -1) if k >= 2 else read(("turn", KC - 2 + k), -2)
                return
            order = [s for s in steps if s[0] in ("enc", "e1", "turn")]
            before = list(order)
            if not ahead:
                order = [s for s in order if s[0] != "enc"]
            if not two_ahead:
                order = [s for s in order if s[0] != "turn"]
            n = order.index((name, k))
            if n >= 2:
                return read(order[n - 2], i)
            if isinstance(i, int) and i == 0:
                return read(("turn", KC - 2 + n), -1)
            if isinstance(i, int) and i == NB - 1:
                before = [s for s in before if s[0] != "turn"]
            return read(before[n - 2], i - 1)

        @block.sync
        def _(sp):
            def load_x(blk):
                wait(sp, turned, blk * KC)
                sp.dma_start(x[:, :, :], d["x"][bass.ds(blk * NT, NT), :, :].rearrange("t p c -> p t c"))\
                    .then_inc(x_in, 16)

            def store_xt(blk, c):
                sp.wait_ge(xt_out, blk * KC + c + 1)
                sp.dma_start(d["xt"][:, bass.ds(blk * KC * BLK + c * BLK, BLK)],
                             xt[:, c % 2, :]).then_inc(xt_stored[c % 2], 16)

            def step(name, k, i, where, ahead, two_ahead):
                if name == "ln_stats" and k == 0 and where == "first" or name == "rt1" and two_ahead:
                    load_x(i + 2)
                if name == "turn":
                    store_xt(i + 2, k)
                if name == "fin_norm":
                    blk = i - 1
                    if isinstance(blk, int) and blk < 0:
                        return
                    sp.wait_ge(scaled, blk * NT + NT)
                    sp.dma_start(d["ffn"][bass.ds(blk * NT, NT), :, :].rearrange("t p c -> p t c"),
                                 out[:, :, :]).then_inc(out_stored, 16)
            run(sp, step)
            sp.wait_ge(out_stored, 16 * NB)
            for s in xt_stored:
                sp.wait_ge(s, 16 * NB * KC // 2)

        @block.tensor
        def _(pe):
            def step(name, k, i, where, ahead, two_ahead):
                if name == "turn":
                    blk = i + 2
                    pe.wait_ge(xnorm, blk * NT + NT)
                    wait_e_bank(pe, name, k, i, where, ahead, two_ahead)
                    bank = e_bank(name, k, where, ahead, two_ahead)
                    for t in range(NT):
                        m = pe.transpose(bank[:, t * P:(t + 1) * P], x[:, t, k * P:(k + 1) * P], w["ident"][:, :])
                    m.then_inc(turned, 1)
                elif name == "enc":
                    blk = i + 1
                    pe.wait_ge(xl_out, blk * KC + KC)
                    wait_e_bank(pe, name, k, i, where, ahead, two_ahead)
                    bank = e_bank(name, k, where, ahead, two_ahead)
                    for c in range(KC):
                        s = slice(k * P, (k + 1) * P)
                        m = pass3(pe, bank[:, :], w["enc_h"][:, c, s], w["enc_l"][:, c, s], xh[:, c, :], xl[:, c, :],
                                  c == 0, c == KC - 1)
                    m.then_inc(enc_done, 1)
                elif name == "s2c":
                    blk = i + 1
                    pe.wait_ge(spl_out, blk * HC + k + 1)
                    if k == 0:
                        wait(pe, cont_out, blk)
                    pass3(pe, bS[:, :], w["s2c_h"][:, k, :], w["s2c_l"][:, k, :], sph[:, k % 2, :], spl[:, k % 2, :],
                          k == 0, k == HC - 1).then_inc(s2c_done, 1)
                elif name == "rt1":
                    pe.wait_ge(contl_out, i + 1)
                    wait(pe, rate_out, i * HC)
                    pe.matmul(bG[:, :], w["r1"][:, :], conth[:, :], start=True, stop=False)
                    pe.matmul(bG[:, :], w["r1"][:, :], contl[:, :], start=False, stop=True).then_inc(rt1_done, 1)
                elif name == "logits":
                    pe.wait_ge(rhl_out, i + 1)
                    for t in range(NT):
                        s = slice(t * P, (t + 1) * P)
                        pe.matmul(bG[:, t * NE:(t + 1) * NE], midh[:, s], w["r2"][:, :], start=True, stop=False)
                        m = pe.matmul(bG[:, t * NE:(t + 1) * NE], midl[:, s], w["r2"][:, :], start=False, stop=True)
                    m.then_inc(logits_done, 1)
                elif name == "comb_t":
                    pe.wait_ge(route, i * 16 + 16)
                    for t in range(NT):
                        m = pe.transpose(bG[:, t * P:(t + 1) * P], w["comb_pad"][:, t, :], w["ident"][:, :])
                    m.then_inc(combt_done, 1)
                elif name == "spread":
                    pe.wait_ge(combrow_out, i + 1)
                    if k == 0:
                        wait(pe, dec_out, i * NT)
                    else:
                        pe.wait_ge(combb_out, i * NE + k)
                    pe.matmul(bD[3][:, :], w["pick"][:, k:k + 1].broadcast_to([2 * NE, P]), w["rows"][0:2 * NE, :],
                              start=True, stop=True).then_inc(spread_done, 1)
                elif name == "e1":
                    wait_e_bank(pe, name, k, i, where, ahead, two_ahead)
                    bank = e_bank(name, k, where, ahead, two_ahead)
                    s = slice(k * P, (k + 1) * P)
                    pe.matmul(bank[:, :], w["e1"][:, s], conth[:, :], start=True, stop=False)
                    pe.matmul(bank[:, :], w["e1"][:, s], contl[:, :], start=False, stop=True).then_inc(e1_done, 1)
                elif name == "e2":
                    e, q = divmod(k, EC)
                    pe.wait_ge(hidl_out, i * NJ + k + 1)
                    if q == 0 and e < 3:
                        wait(pe, dec_out, (i - 1) * NT + e + 1)
                    elif q == 0:
                        pe.wait_ge(z_out, i * NE + e - 2)
                    pe.matmul(bD[e % 3][:, :], w["e2"][:, k, :], hidh[:, k % 4, :], start=(q == 0), stop=False)
                    pe.matmul(bD[e % 3][:, :], w["e2"][:, k, :], hidl[:, k % 4, :], start=False,
                              stop=(q == EC - 1)).then_inc(e2_done, 1)
                elif name == "dup":
                    pe.wait_ge(accl_out, i + 1)
                    pe.matmul(bG[:, :], w["twice"][:, :], midh[:, :], start=True, stop=False)
                    pe.matmul(bG[:, :], w["twice"][:, :], midl[:, :], start=False, stop=False)
                    pe.matmul(bG[:, :], w["b2h"][:, :], w["rows"][0:2 * NE, :], start=False, stop=False)
                    pe.matmul(bG[:, :], w["b2l"][:, :], w["rows"][0:2 * NE, :], start=False, stop=True)\
                        .then_inc(dup_done, 1)
                elif name == "c2s":
                    pe.wait_ge(moel_out, i + 1)
                    if k:
                        pe.wait_ge(rate_out, i * HC + k)
                    s = slice(k * P, (k + 1) * P)
                    pe.matmul(bG[:, :], w["c2s"][:, s], midh[:, :], start=True, stop=False)
                    pe.matmul(bG[:, :], w["c2s"][:, s], midl[:, :], start=False, stop=True).then_inc(c2s_done, 1)
                elif name == "dec_bias":
                    pe.wait_ge(z_out, i * NE + NE)
                    pe.wait_ge(combb_out, i * NE + NE)
                    for t in range(NT):
                        pe.matmul(bD[t][:, :], w["pick_bias"][64:P, :], w["rows"][64:P, :], start=True, stop=False)
                elif name == "dec":
                    pe.wait_ge(ratel_out, i * HC + k + 1)
                    for t in range(NT):
                        s = slice(t * P, (t + 1) * P)
                        last = k == HC - 1
                        pe.matmul(bD[t][:, :], hidh[:, k % 4, s], w["dec_h"][:, k, :], start=False, stop=False)
                        pe.matmul(bD[t][:, :], hidh[:, k % 4, s], w["dec_l"][:, k, :], start=False, stop=False)
                        m = pe.matmul(bD[t][:, :], hidl[:, k % 4, s], w["dec_h"][:, k, :], start=False, stop=last)
                        if last:
                            m.then_inc(dec_done, 1)
                    if not last:
                        m.then_inc(dec_done, 1)
            run(pe, step)

        DEC = HC - 1 + NT

        @block.scalar
        def _(act):
            def step(name, k, i, where, ahead, two_ahead):
                if name == "turn":
                    blk = i + 2
                    n = blk * KC + k
                    act.wait_ge(turned, n + 1)
                    if not (isinstance(n, int) and n < 2):
                        act.wait_ge(xl_out, n - 1)
                        act.wait_ge(xt_stored[k % 2], (blk * KC // 2 + k // 2) * 16)
                    act.activation(xt[:, k % 2, :], e_bank(name, k, where, ahead, two_ahead)[:, :], ACT.Copy)\
                        .then_inc(xt_out, 1)
                elif name == "enc":
                    n = (i + 1) * HC + k
                    act.wait_ge(enc_done, n + 1)
                    wait(act, spl_out, n - 1)
                    act.activation(sp_t[:, k % 2, :], e_bank(name, k, where, ahead, two_ahead)[:, :], ACT.Tanh,
                                   bias=w["enc_b"][:, k:k + 1], scale=0.5).then_inc(sp_out, 1)
                elif name == "s2c" and k == HC - 1:
                    blk = i + 1
                    act.wait_ge(s2c_done, blk * HC + HC)
                    wait(act, rhl_out, blk)
                    act.activation(cont[:, :], bS[:, :], ACT.Identity, bias=w["s2c_b"][:, :], scale=0.5)\
                        .then_inc(cont_out, 1)
                elif name == "rt1":
                    act.wait_ge(rt1_done, i + 1)
                    act.wait_ge(contl_out, i + 1)
                    act.activation(cont[:, :], bG[:, :], ACT.Relu, bias=w["r_b1"][:, :]).then_inc(rh_out, 1)
                elif name == "route" and k == 0:
                    act.wait_ge(route, i * 16 + 3)
                    act.activation(ex[:, :, :], lgm[:, :, :], ACT.Exp).then_inc(exp_out, 1)
                elif name == "comb_t":
                    act.wait_ge(combt_done, i + 1)
                    wait(act, dup_done, i)
                    act.activation(w["rows"][0:2 * NE, :], bG[0:2 * NE, :], ACT.Copy).then_inc(combrow_out, 1)
                elif name == "spread":
                    n = i * NE + k
                    act.wait_ge(spread_done, n + 1)
                    wait(act, z_out, n - 1)
                    act.activation(comb_b[:, k % 2, :], bD[3][:, :], ACT.Copy).then_inc(combb_out, 1)
                elif name == "e1":
                    n = i * NJ + k
                    act.wait_ge(e1_done, n + 1)
                    if k >= 2:
                        act.wait_ge(hidl_out, n - 1)
                    else:
                        wait(act, ratel_out, (i - 1) * HC + HC - 1 + k)
                    act.activation(hid[:, k % 2, :], e_bank(name, k, where, ahead, two_ahead)[:, :], ACT.Relu,
                                   bias=w["e_b1"][:, k:k + 1]).then_inc(hid_out, 1)
                    if k % 2:
                        act.wait_ge(hid_out, n + 1)
                        if k >= 4:
                            act.wait_ge(e2_done, n - 3)
                        else:
                            wait(act, dec_done, i * DEC)
                        act.activation(hidh[:, k % 4, :], hid[:, k % 2, :], ACT.Copy).then_inc(hidh_act, 1)
                elif name == "dup":
                    act.wait_ge(dup_done, i + 1)
                    act.activation(midh[:, :], bG[:, :], ACT.Copy).then_inc(moeh_out, 1)
                elif name == "c2s":
                    n = i * HC + k
                    act.wait_ge(c2s_done, n + 1)
                    if k >= 2:
                        act.wait_ge(ratel_out, n - 1)
                    else:
                        act.wait_ge(hidl_out, i * NJ + NJ - 1 + k)
                        if k % 2:
                            act.wait_ge(hidh_act, i * (NJ // 2) + NJ // 2)
                    act.activation(hid[:, k % 2, :], bG[:, :], ACT.Tanh, bias=w["c2s_b"][:, k:k + 1], scale=0.5)\
                        .then_inc(rate_out, 1)
                elif name == "dec" and k == HC - 1:
                    wait(act, out_stored, i * 16)
                    for t in range(NT):
                        act.wait_ge(dec_done, i * DEC + HC + t)
                        act.activation(out[:, t, :], bD[t][:, :], ACT.Tanh, scale=0.25).then_inc(dec_out, 1)
            run(act, step)

        @block.vector
        def _(dve):
            def hold(k, sem, value):
                dve.wait_ge(sem, value)
                dve.memset(held[:, k:k + 1], 0.0)

            def split(src, hi, lo, hi_sem, lo_sem, n):
                dve.tensor_copy(hi, src).then_inc(hi_sem, 1)
                dve.wait_ge(hi_sem, n)
                dve.tensor_tensor(lo, src, f32(hi), ALU.subtract).then_inc(lo_sem, 1)

            def step(name, k, i, where, ahead, two_ahead):
                if name == "ln_stats":
                    blk = i + 2
                    dve.wait_ge(x_in, blk * 16 + 16)
                    dve.bn_stats(st[:, k, :], x[:, k, :]).then_inc(xstat, 1)
                    if k == NT - 1:
                        hold(0, xstat, blk * NT + NT)
                        for t in range(NT):
                            dve.bn_aggr(mv[:, t, :], st[:, t, :]).then_inc(xmv, 1)
                elif name == "ln_norm":
                    blk = i + 2
                    dve.wait_ge(xrs, blk + 1)
                    dve.wait_ge(xmv, blk * NT + NT)
                    for t in range(NT):
                        dve.tensor_scalar(x[:, t, :], x[:, t, :], mv[:, t, 0:1], rs[:, t:t + 1],
                                          ALU.subtract, ALU.mult).then_inc(xnorm, 1)
                elif name == "turn":
                    blk = i + 2
                    n = blk * KC + k
                    dve.wait_ge(xt_out, n + 1)
                    wait(dve, enc_done, (i + 2) * HC)
                    split(xt[:, k % 2, :], xh[:, k, :], xl[:, k, :], xh_out, xl_out, n + 1)
                elif name == "enc":
                    n = (i + 1) * HC + k
                    dve.wait_ge(sp_out, n + 1)
                    wait(dve, s2c_done, n - 1)
                    split(sp_t[:, k % 2, :], sph[:, k % 2, :], spl[:, k % 2, :], sph_out, spl_out, n + 1)
                elif name == "s2c" and k == HC - 1:
                    blk = i + 1
                    dve.wait_ge(cont_out, blk + 1)
                    wait(dve, e1_done, blk * NJ)
                    split(cont[:, :], conth[:, :], contl[:, :], conth_out, contl_out, blk + 1)
                elif name == "rt1":
                    dve.wait_ge(rh_out, i + 1)
                    wait(dve, c2s_done, i * HC)
                    split(cont[:, :], midh[:, :], midl[:, :], rhh_out, rhl_out, i + 1)
                elif name == "route":
                    r = i * 16
                    wide = [P, NT, NE]

                    def over(q):
                        return s4[:, q, :].unsqueeze(2).broadcast_to(wide)

                    def after(n, ins):
                        ins.then_inc(route, 1)
                        dve.wait_ge(route, r + n)
                    if k == 0:
                        dve.wait_ge(logits_done, i + 1)
                        after(1, dve.tensor_tensor(lg[:, :, :], bG[:, 0:NT * NE].rearrange("p (t e) -> p t e", e=NE),
                                                   w["r_b2"][:, :].unsqueeze(1).broadcast_to(wide), ALU.add))
                        after(2, dve.tensor_reduce(s4[:, 0, :], lg[:, :, :], AX.X, ALU.max))
                        dve.tensor_tensor(lgm[:, :, :], lg[:, :, :], over(0), ALU.subtract).then_inc(route, 1)
                    elif k == 1:
                        dve.wait_ge(exp_out, i + 1)
                        after(4, dve.tensor_reduce(s4[:, 1, :], ex[:, :, :], AX.X, ALU.add))
                        after(5, dve.reciprocal(s4[:, 2, :], s4[:, 1, :]))
                        dve.tensor_tensor(w["probs"][:, :, 0:NE], ex[:, :, :], over(2), ALU.mult).then_inc(route, 1)
                    elif k == 2:
                        hold(2, route, r + 6)
                        for t in range(NT):
                            m = dve.max(top[:, t, :], w["probs"][:, t, 0:NE])
                        after(7, m)
                        dve.tensor_copy(w["top2"][:, :, 0:2], top[:, :, 0:2]).then_inc(route, 1)
                        hold(3, route, r + 8)
                        for t in range(NT):
                            m = dve.match_replace(left[:, t, :], w["top2"][:, t, :], w["probs"][:, t, :], -2.0)
                        m.then_inc(route, 1)
                    elif k == 3:
                        dve.wait_ge(route, r + 9)
                        after(10, dve.scalar_tensor_tensor(
                            out=picked[:, :, :], in0=left[:, :, 0:NE], scalar=0.0,
                            in1=w["probs"][:, :, 0:NE], op0=ALU.is_lt, op1=ALU.mult))
                        after(11, dve.tensor_reduce(s4[:, 3, :], picked[:, :, :], AX.X, ALU.add))
                        after(12, dve.reciprocal(s4[:, 4, :], s4[:, 3, :]))
                        after(13, dve.tensor_tensor(comb[:, :, :], picked[:, :, :], over(4), ALU.mult))
                        after(14, dve.tensor_copy(comb_r[:, :, :], comb[:, :, :]))
                        wait(dve, combt_done, i)
                        dve.tensor_copy(w["comb_pad"][:, :, 0:NE], f32(comb_r[:, :, :])).then_inc(route, 1)
                        dve.tensor_tensor(w["comb_pad"][:, :, NE:2 * NE], comb[:, :, :], f32(comb_r[:, :, :]),
                                          ALU.subtract).then_inc(route, 1)
                elif name == "e1":
                    n = i * NJ + k
                    if k >= 4:
                        dve.wait_ge(e2_done, n - 3)
                    else:
                        wait(dve, dec_done, i * DEC)
                    if k % 2:
                        dve.wait_ge(hidh_act, i * (NJ // 2) + k // 2 + 1)
                    else:
                        dve.wait_ge(hid_out, n + 1)
                        dve.tensor_copy(hidh[:, k % 4, :], hid[:, k % 2, :]).then_inc(hidh_dve, 1)
                        dve.wait_ge(hidh_dve, i * (NJ // 2) + k // 2 + 1)
                    dve.tensor_tensor(hidl[:, k % 4, :], hid[:, k % 2, :], f32(hidh[:, k % 4, :]), ALU.subtract)\
                        .then_inc(hidl_out, 1)
                elif name == "z":
                    e = k
                    dve.wait_ge(e2_done, i * NJ + e * EC + EC)
                    dve.wait_ge(combb_out, i * NE + e + 1)
                    if e == 0:
                        wait(dve, accl_out, i)
                        target = acc[:, :]
                    else:
                        wait(dve, acc_out, i * (NE - 2) + max(e - 2, 0))
                        target = z[:, e % 2, :]
                    dve.tensor_tensor(target, bD[e % 3][:, :], comb_b[:, e % 2, :], ALU.mult).then_inc(z_out, 1)
                elif name == "acc":
                    dve.wait_ge(acc_out, (i + 1) * (NE - 2))
                    dve.wait_ge(z_out, (i + 1) * NE)
                    dve.tensor_tensor(acc[:, :], acc[:, :], z[:, (NE - 1) % 2, :], ALU.add).then_inc(last_out, 1)
                    dve.wait_ge(last_out, i + 1)
                    dve.wait_ge(logits_done, i + 1)
                    split(acc[:, :], midh[:, :], midl[:, :], acch_out, accl_out, i + 1)
                elif name == "dup":
                    dve.wait_ge(moeh_out, i + 1)
                    dve.tensor_tensor(midl[:, :], bG[:, :], f32(midh[:, :]), ALU.subtract).then_inc(moel_out, 1)
                elif name == "c2s":
                    n = i * HC + k
                    dve.wait_ge(rate_out, n + 1)
                    if k >= 4:
                        dve.wait_ge(dec_done, i * DEC + k - 3)
                    else:
                        dve.wait_ge(e2_done, i * NJ + NJ)
                    split(hid[:, k % 2, :], hidh[:, k % 4, :], hidl[:, k % 4, :], rateh_out, ratel_out, n + 1)
                elif name == "fin_stats":
                    blk = i - 1
                    if isinstance(blk, int) and blk < 0:
                        return
                    dve.wait_ge(dec_out, blk * NT + k + 1)
                    dve.bn_stats(st2[:, k, :], out[:, k, :]).then_inc(fstat, 1)
                    if k == NT - 1:
                        hold(1, fstat, blk * NT + NT)
                        for t in range(NT):
                            dve.bn_aggr(mv2[:, t, :], st2[:, t, :]).then_inc(fmv, 1)
                elif name == "fin_norm":
                    blk = i - 1
                    if isinstance(blk, int) and blk < 0:
                        return
                    dve.wait_ge(frs, blk + 1)
                    dve.wait_ge(fmv, blk * NT + NT)
                    for t in range(NT):
                        dve.tensor_scalar(out[:, t, :], out[:, t, :], mv2[:, t, 0:1], rs2[:, t:t + 1],
                                          ALU.subtract, ALU.mult).then_inc(fnorm, 1)
            run(dve, step)

        @block.gpsimd
        def _(pool):
            def step(name, k, i, where, ahead, two_ahead):
                if name == "ln_stats" and k == NT - 1:
                    blk = i + 2
                    pool.wait_ge(xmv, blk * NT + NT)
                    wait(pool, xnorm, blk * NT)
                    pool.tensor_tensor(ve[:, :], mv[:, :, 1], eps[:, :], ALU.add).then_inc(xve, 1)
                    pool.wait_ge(xve, blk + 1)
                    pool.tensor_tensor(rs[:, :], ve[:, :], w["half_down"][:, :], ALU.pow).then_inc(xrs, 1)
                elif name == "fin_stats" and k == NT - 1:
                    blk = i - 1
                    if isinstance(blk, int) and blk < 0:
                        return
                    pool.wait_ge(fmv, blk * NT + NT)
                    wait(pool, fnorm, blk * NT)
                    pool.tensor_tensor(ve2[:, :], mv2[:, :, 1], eps4[:, :], ALU.add).then_inc(fve, 1)
                    pool.wait_ge(fve, blk + 1)
                    pool.tensor_tensor(rs2[:, :], ve2[:, :], w["half_down"][:, :], ALU.pow).then_inc(frs, 1)
                elif name == "fin_norm":
                    blk = i - 1
                    if isinstance(blk, int) and blk < 0:
                        return
                    for t in range(NT):
                        pool.wait_ge(fnorm, blk * NT + t + 1)
                        pool.tensor_tensor(out[:, t, :], out[:, t, :], w["ln_g"][:, :], ALU.mult).then_inc(scaled, 1)
                elif name == "z" and 0 < k < NE - 1:
                    e = k
                    pool.wait_ge(z_out, i * NE + e + 1)
                    wait(pool, acc_out, i * (NE - 2) + e - 1)
                    pool.tensor_tensor(acc[:, :], acc[:, :], z[:, e % 2, :], ALU.add).then_inc(acc_out, 1)
            pool.memset(eps[:, :], LN_EPS).then_inc(xeps, 1)
            pool.memset(eps4[:, :], 4 * LN_EPS).then_inc(xeps, 1)
            pool.wait_ge(xeps, 2)
            run(pool, step)



VW = 2 * P + 2


def run_keyvalue(nc, d, kv):
    with ExitStack() as ctx:
        b = Bench(nc, ctx, "k_")
        raw = [b.sb(f"raw{i}", [P, KC * DIM]) for i in range(2)]
        wkh, wkl = b.sb("wkh", [P, KC, DIM], F32R), b.sb("wkl", [P, KC, DIM], F32R)
        wvh, wvl = b.sb("wvh", [P, KC, DIM], F32R), b.sb("wvl", [P, KC, DIM], F32R)
        xt = [b.sb(f"xt{i}", [P, KC, BLK]) for i in range(2)]
        xh = [b.sb(f"xh{i}", [P, KC, BLK], F32R) for i in range(2)]
        xl = [b.sb(f"xl{i}", [P, KC, BLK], F32R) for i in range(2)]
        kh, kl = b.sb("kh", [P, 2, DIM], F32R), b.sb("kl", [P, 2, DIM], F32R)
        v = b.sb("v", [P, 2, KC, VW], F32R)
        onesf = b.sb("onesf", [P, 2, KC, 2])
        total = b.sb("total", [P, KC, VW])
        mask = b.sb("mask", [P, HG, HD])
        num = b.sb("num", [P, KC, P])
        numm = b.sb("numm", [P, KC, P])
        den, denh = b.sb("den", [P, KC, HG]), b.sb("denh", [P, KC, HG], F32R)
        zerof = b.sb("zerof", [P, KC * P])
        bK, bV = [b.psum(f"K{i}") for i in range(2)], [b.psum(f"V{i}") for i in range(2)]
        bA = [b.psum(f"A{g}") for g in range(KC)]

        w_in = [b.sem(f"w_in{i}") for i in range(2)]
        x_in = [b.sem(f"x_in{i}") for i in range(2)]
        wh_out, wl_out, consts, ready = (b.sem(n) for n in ("wh_out", "wl_out", "consts", "ready"))
        xh_out, xl_out, k_done, v_done, vk_done = (b.sem(n) for n in ("xh_out", "xl_out", "k_done", "v_done", "vk_done"))
        kh_out, kl_out, vh_out, vl_out = (b.sem(n) for n in ("kh_out", "kl_out", "vh_out", "vl_out"))
        summed, closed = b.sem("summed"), b.sem("closed")

        PAIRS = NB // 2
        PER_SEQ = PAIRS // BATCH
        TP = 2 * NT

        block = ctx.enter_context(nc.Block())

        @block.sync
        def _(sp):
            for k in range(2):
                sp.dma_start(raw[k][:, :], d["wkv"][k]).then_inc(w_in[k], 16)
            for h in range(2):
                sp.dma_start(xt[h][:, :, :], d["xt"][:, h * KC * BLK:(h + 1) * KC * BLK]
                             .rearrange("p (c n) -> p c n", c=KC)).then_inc(x_in[h], 16)
            with sp.Fori(1, PAIRS) as p:
                for h in range(2):
                    sp.wait_ge(xl_out, ((p - 1) * 2 + h + 1) * KC)
                    sp.dma_start(xt[h][:, :, :], d["xt"][:, bass.ds((p * 2 + h) * KC * BLK, KC * BLK)]
                                 .rearrange("p (c n) -> p c n", c=KC)).then_inc(x_in[h], 16)

        @block.gpsimd
        def _(pool):
            pool.memset(onesf[:, :, :, :], 1.0).then_inc(consts, 1)
            pool.memset(zerof[:, :], 0.0).then_inc(consts, 1)
            pool.memset(total[:, :, :], 0.0).then_inc(consts, 1)
            pool.memset(mask[:, :, :], 1.0).then_inc(consts, 1)
            pool.wait_ge(consts, 4)
            pool.affine_select(out=mask[:, :, :], in_=mask[:, :, :], compare_op=ALU.is_ge, fill=0.0, base=0,
                               pattern=[[-HD, HG], [0, HD]], channel_multiplier=1).then_inc(consts, 1)
            pool.wait_ge(consts, 5)
            pool.affine_select(out=mask[:, :, :], in_=mask[:, :, :], compare_op=ALU.is_ge, fill=0.0, base=HD - 1,
                               pattern=[[HD, HG], [0, HD]], channel_multiplier=-1).then_inc(consts, 1)

        @block.scalar
        def _(act):
            for k, t in enumerate((wkh, wvh)):
                act.wait_ge(w_in[k], 16)
                act.activation(t[:, :, :], raw[k][:, :].rearrange("p (c n) -> p c n", c=KC), ACT.Copy)\
                    .then_inc(wh_out, 1)

            def tile(n, j):
                act.wait_ge(k_done, n + 1)
                if isinstance(n, int):
                    wait(act, vk_done, n - 1)
                else:
                    act.wait_ge(vk_done, n - 1)
                act.activation(kh[:, j % 2, :], bK[j % 2][:, :], ACT.Relu).then_inc(kh_out, 1)
                act.wait_ge(v_done, n + 1)
                act.activation(v[:, j % 2, :, 0:P], bV[j % 2][:, :].rearrange("p (g f) -> p g f", g=KC), ACT.Relu)\
                    .then_inc(vh_out, 1)
            for j in range(TP):
                tile(j, j)
            with act.Fori(1, PAIRS) as p:
                for j in range(TP):
                    tile(p * TP + j, j)

        @block.tensor
        def _(pe):
            def project(n, j):
                h, t = divmod(j, NT)
                s = slice(t * P, (t + 1) * P)
                for c in range(KC):
                    a, z = c == 0, c == KC - 1
                    if c == 0:
                        wait(pe, kl_out, n - 1)
                        wait(pe, vl_out, n - 1)
                    pe.matmul(bK[j % 2][:, :], xh[h][:, c, s], wkh[:, c, :], start=a, stop=False)
                    pe.matmul(bK[j % 2][:, :], xh[h][:, c, s], wkl[:, c, :], start=False, stop=False)
                    pe.matmul(bV[j % 2][:, :], xh[h][:, c, s], wvh[:, c, :], start=a, stop=False)
                    pe.matmul(bV[j % 2][:, :], xh[h][:, c, s], wvl[:, c, :], start=False, stop=False)
                    mk = pe.matmul(bK[j % 2][:, :], xl[h][:, c, s], wkh[:, c, :], start=False, stop=z)
                    if z:
                        mk.then_inc(k_done, 1)
                    mv = pe.matmul(bV[j % 2][:, :], xl[h][:, c, s], wvh[:, c, :], start=False, stop=z)
                mv.then_inc(v_done, 1)

            def outer(n, j, p):
                pe.wait_ge(kl_out, n + 1)
                pe.wait_ge(vl_out, n + 1)
                if j == 0:
                    wait(pe, summed, p * KC)
                for g in range(KC):
                    s = slice(g * P, (g + 1) * P)
                    pe.matmul(bA[g][:, 0:VW], kh[:, j % 2, s], v[:, j % 2, g, :], start=(j == 0), stop=False)
                    m = pe.matmul(bA[g][:, 0:VW], kl[:, j % 2, s], v[:, j % 2, g, :], start=False, stop=(j == TP - 1))
                m.then_inc(vk_done, 1)

            def pair(p):
                for j in range(TP + 1):
                    if j < TP:
                        if j % NT == 0:
                            pe.wait_ge(xl_out, (p * 2 + j // NT + 1) * KC)
                        project(p * TP + j, j)
                    if j:
                        outer(p * TP + j - 1, j - 1, p)
            pe.wait_ge(wl_out, 2)
            pe.wait_ge(ready, 2)
            pair(0)
            with pe.Fori(1, PAIRS) as p:
                pair(p)

        @block.vector
        def _(dve):
            for k, (h, low) in enumerate(((wkh, wkl), (wvh, wvl))):
                dve.wait_ge(wh_out, k + 1)
                dve.tensor_tensor(low[:, :, :], raw[k][:, :].rearrange("p (c n) -> p c n", c=KC), f32(h[:, :, :]),
                                  ALU.subtract).then_inc(wl_out, 1)
            dve.wait_ge(consts, 6)
            dve.tensor_copy(v[:, :, :, 2 * P:VW], onesf[:, :, :, :]).then_inc(ready, 1)
            for s in range(BATCH):
                m = dve.tensor_copy(kv["den"][s][:, :, :], zerof[:, :].rearrange("p (c n) -> p c n", c=KC))
            m.then_inc(ready, 1)

            def split_x(p, h, c, n):
                if c == 0:
                    dve.wait_ge(x_in[h], p * 16 + 16)
                    wait(dve, v_done, (p - 1) * TP + (h + 1) * NT)
                dve.tensor_copy(xh[h][:, c, :], xt[h][:, c, :]).then_inc(xh_out, 1)
                dve.wait_ge(xh_out, n + 1)
                dve.tensor_tensor(xl[h][:, c, :], xt[h][:, c, :], f32(xh[h][:, c, :]), ALU.subtract)\
                    .then_inc(xl_out, 1)

            def tile(n, j):
                dve.wait_ge(kh_out, n + 1)
                dve.scalar_tensor_tensor(out=kl[:, j % 2, :], in0=bK[j % 2][:, :], scalar=0.0,
                                         in1=f32(kh[:, j % 2, :]), op0=ALU.max, op1=ALU.subtract).then_inc(kl_out, 1)
                dve.wait_ge(vh_out, n + 1)
                dve.scalar_tensor_tensor(out=v[:, j % 2, :, P:2 * P],
                                         in0=bV[j % 2][:, :].rearrange("p (g f) -> p g f", g=KC), scalar=0.0,
                                         in1=f32(v[:, j % 2, :, 0:P]), op0=ALU.max, op1=ALU.subtract)\
                    .then_inc(vl_out, 1)

            def pair(p, more):
                for j in range(TP):
                    tile(p * TP + j, j)
                    if more and j >= NT:
                        split_x(p + 1, 0, j - NT, (p + 1) * 2 * KC + j - NT)
                dve.wait_ge(vk_done, p * TP + TP)
                for g in range(KC):
                    dve.wait_ge(summed, p * KC + g)
                    dve.tensor_tensor(total[:, g, :], bA[g][:, 0:VW], total[:, g, :], ALU.add).then_inc(summed, 1)
                if more:
                    for c in range(KC):
                        split_x(p + 1, 1, c, (p + 1) * 2 * KC + KC + c)

            for h in range(2):
                for c in range(KC):
                    split_x(0, h, c, h * KC + c)
            done = 0
            for s in range(BATCH):
                first = s * PER_SEQ
                if s == 0:
                    pair(0, True)
                    with dve.Fori(1, PER_SEQ) as p:
                        pair(p, True)
                else:
                    with dve.Fori(first, PAIRS - 1) as p:
                        pair(p, True)
                    pair(PAIRS - 1, False)
                dve.wait_ge(summed, (first + PER_SEQ) * KC)

                def then(ins):
                    nonlocal done
                    done += 1
                    ins.then_inc(closed, 1)
                    dve.wait_ge(closed, done)
                then(dve.tensor_tensor(num[:, :, :], total[:, :, 0:P], total[:, :, P:2 * P], ALU.add))
                then(dve.tensor_tensor(numm[:, :, :], num[:, :, :],
                                       mask[:, :, :].rearrange("p a b -> p (a b)").unsqueeze(1)
                                       .broadcast_to([P, KC, P]), ALU.mult))
                then(dve.tensor_copy(kv["numh"][s][:, :, :], numm[:, :, :]))
                then(dve.tensor_tensor(kv["numl"][s][:, :, :], numm[:, :, :], f32(kv["numh"][s][:, :, :]),
                                       ALU.subtract))
                then(dve.tensor_tensor(den[:, :, :], mask[:, :, 0:1].rearrange("p a b -> p (a b)").unsqueeze(1)
                                       .broadcast_to([P, KC, HG]),
                                       total[:, :, 2 * P:2 * P + 1].broadcast_to([P, KC, HG]), ALU.mult))
                then(dve.tensor_copy(denh[:, :, :], den[:, :, :]))
                for g in range(KC):
                    a, z = g * HG, (g + 1) * HG
                    then(dve.tensor_copy(kv["den"][s][:, g, a:z], f32(denh[:, g, :])))
                    then(dve.tensor_tensor(kv["den"][s][:, g, 64 + a:64 + z], den[:, g, :], f32(denh[:, g, :]),
                                           ALU.subtract))
                then(dve.memset(total[:, :, :], 0.0))



def run_attention(nc, d, kv, out_dram):
    with ExitStack() as ctx:
        b = Bench(nc, ctx, "a_")
        raw = [b.sb(f"raw{i}", [P, KC * DIM]) for i in range(2)]
        wqh, wql = b.sb("wqh", [P, KC, DIM], F32R), b.sb("wql", [P, KC, DIM], F32R)
        wph, wpl = b.sb("wph", [P, KC, DIM], F32R), b.sb("wpl", [P, KC, DIM], F32R)
        bias2, bias = b.sb("bias2", [P, 2, DIM]), b.sb("bias", [P, DIM])
        fan, fanf = b.sb("fan", [64, KC, P], F32R), b.sb("fanf", [64, KC, P])
        xt = b.sb("xt", [P, KC, BLK])
        xh, xl = b.sb("xh", [P, KC, BLK], F32R), b.sb("xl", [P, KC, BLK], F32R)
        qh, ql = b.sb("qh", [P, KC, BLK], F32R), b.sb("ql", [P, KC, BLK], F32R)
        ah, al = b.sb("ah", [P, KC, BLK], F32R), b.sb("al", [P, KC, BLK], F32R)
        at, rb = b.sb("at", [P, 2, BLK]), b.sb("rb", [P, 2, BLK])
        dlow, dsum = b.sb("dlow", [HEADS, BLK]), b.sb("dsum", [HEADS, BLK])
        rc, rc2 = b.sb("rc", [HEADS, BLK]), b.sb("rc2", [2 * HEADS, BLK], F32R)
        x, y, f = b.sb("x", [P, NT, DIM]), b.sb("y", [P, NT, DIM]), b.sb("f", [P, NT, DIM])
        bQ, bN = [b.psum(f"Q{i}") for i in range(2)], [b.psum(f"N{i}") for i in range(2)]
        bR, bDen = b.psum("R"), b.psum("Den")
        bP = [b.psum(f"P{i}") for i in range(2)]
        sem = b.sem
        w_in = [sem(f"w_in{i}") for i in range(2)]
        vec_in, xt_in, f_in = sem("vec_in"), sem("xt_in"), sem("f_in")
        x_in = [sem(f"x_in{t}") for t in range(NT)]
        stored = [sem(f"stored{t}") for t in range(NT)]
        wh_out, wl_out, consts, ready = sem("wh_out"), sem("wl_out"), sem("consts"), sem("ready")
        xh_out, xl_out, q_done, qh_out, ql_out = (sem(n) for n in ("xh_out", "xl_out", "q_done", "qh_out", "ql_out"))
        den_done, dlow_out, dsum_out, rc_out, rch_out, rcl_out = (sem(n) for n in (
            "den_done", "dlow_out", "dsum_out", "rc_out", "rch_out", "rcl_out"))
        fan_done, num_done, rb_out, at_out, ah_out, al_out = (sem(n) for n in (
            "fan_done", "num_done", "rb_out", "at_out", "ah_out", "al_out"))
        proj_done, y_out, xf_out, xfb_out = sem("proj_done"), sem("y_out"), sem("xf_out"), sem("xfb_out")

        def blocks(eng, body):
            half = NB // BATCH
            body(0, 0, attend=False)
            body(1, 0)
            with eng.Fori(2, half) as i:
                body(i, 0)
            body(half, 0)
            with eng.Fori(half + 1, NB - 1) as i:
                body(i, 1)
            body(NB - 1, 1, more=False)
            body(NB, 1, more=False, ahead=False)

        block = ctx.enter_context(nc.Block())

        @block.sync
        def _(sp):
            def load_xt(i):
                sp.dma_start(xt[:, :, :], d["xt"][:, bass.ds(i * KC * BLK, KC * BLK)]
                             .rearrange("p (c n) -> p c n", c=KC)).then_inc(xt_in, 16)

            def load_x(j, t):
                sp.dma_start(x[:, t, :], d["x"][bass.ds(j * NT + t, 1), :, :].rearrange("t p c -> (t p) c"))\
                    .then_inc(x_in[t], 16)

            def load_f(j):
                sp.dma_start(f[:, :, :], d["ffn"][bass.ds(j * NT, NT), :, :].rearrange("t p c -> p t c"))\
                    .then_inc(f_in, 16)

            sp.dma_start(raw[0][:, :], d["wqp"][0]).then_inc(w_in[0], 16)
            load_xt(0)
            sp.dma_start(raw[1][:, :], d["wqp"][1]).then_inc(w_in[1], 16)
            sp.dma_start(bias2[:, :, :], d["bias2"][:, :, :]).then_inc(vec_in, 16)
            for t in range(NT):
                load_x(0, t)
            load_f(0)

            def body(i, s, ahead=True, attend=True, more=True):
                if more:
                    sp.wait_ge(xl_out, i * KC + KC)
                    load_xt(i + 1)
                if attend:
                    j = i - 1
                    if ahead:
                        sp.wait_ge(xf_out, j * NT + NT)
                        load_f(j + 1)
                    for t in range(NT):
                        sp.wait_ge(y_out, j * NT + t + 1)
                        sp.dma_start(out_dram[bass.ds(j * NT + t, 1), :, :].rearrange("t p c -> (t p) c"),
                                     y[:, t, :]).then_inc(stored[t], 16)
                        if ahead:
                            load_x(j + 1, t)
            blocks(sp, body)
            for t in range(NT):
                sp.wait_ge(stored[t], 16 * NB)

        @block.gpsimd
        def _(pool):
            pool.memset(fanf[:, :, :], 1.0).then_inc(consts, 1)
            n = 1
            for half in range(2):
                v = fanf[32 * half:32 * half + 32, :, :]
                for cm, st, base in ((-HD, 1, 0), (HD, -1, HD - 1)):
                    pool.wait_ge(consts, n)
                    pool.affine_select(out=v, in_=v, compare_op=ALU.is_ge, fill=0.0, base=base,
                                       pattern=[[st * P, KC], [st, P]], channel_multiplier=cm).then_inc(consts, 1)
                    n += 1
            pool.wait_ge(consts, 5)
            pool.wait_ge(vec_in, 16)
            pool.tensor_tensor(bias[:, :], bias2[:, 0, :], bias2[:, 1, :], ALU.add).then_inc(consts, 1)
            pool.wait_ge(consts, 6)

            def body(i, s, ahead=True, attend=True, more=True):
                if attend:
                    j = i - 1
                    pool.wait_ge(f_in, j * 16 + 16)
                    for t in range(NT):
                        pool.wait_ge(x_in[t], j * 16 + 16)
                        pool.tensor_tensor(x[:, t, :], x[:, t, :], f[:, t, :], ALU.add).then_inc(xf_out, 1)
                        pool.wait_ge(xf_out, j * NT + t + 1)
                        pool.tensor_tensor(x[:, t, :], x[:, t, :], bias[:, :], ALU.add).then_inc(xfb_out, 1)
            blocks(pool, body)

        @block.scalar
        def _(act):
            def split_x(i):
                act.wait_ge(xt_in, i * 16 + 16)
                wait(act, q_done, i * KC)
                for c in range(KC):
                    act.activation(xh[:, c, :], xt[:, c, :], ACT.Copy).then_inc(xh_out, 1)

            for k, t in enumerate((wqh, wph)):
                act.wait_ge(w_in[k], 16)
                act.activation(t[:, :, :], raw[k][:, :].rearrange("p (c n) -> p c n", c=KC), ACT.Copy)\
                    .then_inc(wh_out, 1)
                if k == 0:
                    split_x(0)

            def body(i, s, ahead=True, attend=True, more=True):
                for m in range(KC):
                    if attend:
                        n = (i - 1) * KC + m
                        act.wait_ge(fan_done, n + 1)
                        wait(act, at_out, n - 1)
                        act.activation(rb[:, m % 2, :], bR[:, :], ACT.Copy).then_inc(rb_out, 1)
                    if ahead:
                        n = i * KC + m
                        act.wait_ge(q_done, n + 1)
                        if attend:
                            act.wait_ge(num_done, (i - 1) * KC + m + 1)
                        act.activation(qh[:, m, :], bQ[m % 2][:, :], ACT.Relu).then_inc(qh_out, 1)
                    if attend:
                        n = (i - 1) * KC + m
                        act.wait_ge(at_out, n + 1)
                        wait(act, proj_done, (i - 1) * NT)
                        act.activation(ah[:, m, :], at[:, m % 2, :], ACT.Copy).then_inc(ah_out, 1)
                if more:
                    split_x(i + 1)
                if ahead:
                    act.wait_ge(den_done, i + 1)
                    wait(act, dsum_out, i)
                    act.activation(dlow[:, :], bDen[64:64 + HEADS, :], ACT.Copy).then_inc(dlow_out, 1)
                    act.wait_ge(rc_out, 2 * i + 2)
                    wait(act, fan_done, i * KC)
                    act.activation(rc2[0:HEADS, :], rc[:, :], ACT.Copy).then_inc(rch_out, 1)
            blocks(act, body)

        @block.tensor
        def _(pe):
            def attention(i, m, s):
                n = (i - 1) * KC + m
                pe.wait_ge(rcl_out, i)
                wait(pe, rb_out, n)
                pe.matmul(bR[:, :], fan[:, m, :], rc2[:, :], start=True, stop=True).then_inc(fan_done, 1)
                wait(pe, at_out, n - 1)
                pass3(pe, bN[m % 2][:, :], kv["numh"][s][:, m, :], kv["numl"][s][:, m, :],
                      qh[:, m, :], ql[:, m, :], True, True).then_inc(num_done, 1)

            def query(i, m):
                n = i * KC + m
                wait(pe, ql_out, n - 1)
                for c in range(KC):
                    if m == 0:
                        pe.wait_ge(xl_out, i * KC + c + 1)
                    o = slice(m * P, (m + 1) * P)
                    k = pass3(pe, bQ[m % 2][:, :], wqh[:, c, o], wql[:, c, o], xh[:, c, :], xl[:, c, :],
                              c == 0, c == KC - 1)
                k.then_inc(q_done, 1)

            def denominators(i, s):
                if isinstance(i, int) and i == NB // BATCH:
                    s = 1
                pe.wait_ge(ql_out, i * KC + KC)
                wait(pe, dsum_out, i)
                for g in range(KC):
                    pe.matmul(bDen[:, :], kv["den"][s][:, g, :], qh[:, g, :], start=(g == 0), stop=False)
                    k = pe.matmul(bDen[:, :], kv["den"][s][:, g, :], ql[:, g, :], start=False, stop=(g == KC - 1))
                k.then_inc(den_done, 1)

            def body(i, s, ahead=True, attend=True, more=True):
                if isinstance(i, int) and i == 1:
                    pe.wait_ge(wl_out, 2)
                    pe.wait_ge(ready, 1)
                for m in range(KC):
                    if ahead:
                        query(i, m)
                    if attend:
                        attention(i, m, s)
                if attend:
                    for t in range(NT):
                        n = (i - 1) * NT + t
                        wait(pe, y_out, n - 1)
                        for g in range(KC):
                            if t == 0:
                                pe.wait_ge(al_out, (i - 1) * KC + g + 1)
                            o = slice(t * P, (t + 1) * P)
                            pe.matmul(bP[t % 2][:, :], ah[:, g, o], wph[:, g, :], start=(g == 0), stop=False)
                            pe.matmul(bP[t % 2][:, :], ah[:, g, o], wpl[:, g, :], start=False, stop=False)
                            k = pe.matmul(bP[t % 2][:, :], al[:, g, o], wph[:, g, :], start=False, stop=(g == KC - 1))
                        k.then_inc(proj_done, 1)
                        if t == 0 and ahead:
                            denominators(i, s)
                else:
                    denominators(i, s)

            pe.wait_ge(wl_out, 1)
            blocks(pe, body)

        @block.vector
        def _(dve):
            def split_low(k, h, low):
                dve.wait_ge(wh_out, k + 1)
                dve.tensor_tensor(low[:, :, :], raw[k][:, :].rearrange("p (c n) -> p c n", c=KC), f32(h[:, :, :]),
                                  ALU.subtract).then_inc(wl_out, 1)

            def split_x(i, c):
                dve.wait_ge(xh_out, i * KC + c + 1)
                dve.tensor_tensor(xl[:, c, :], xt[:, c, :], f32(xh[:, c, :]), ALU.subtract).then_inc(xl_out, 1)

            def out_tile(i, t):
                j = i - 1
                dve.wait_ge(proj_done, j * NT + t + 1)
                dve.wait_ge(xfb_out, j * NT + t + 1)
                wait(dve, stored[t], j * 16)
                dve.tensor_tensor(y[:, t, :], bP[t % 2][:, :], x[:, t, :], ALU.add).then_inc(y_out, 1)

            def reciprocals(i, half):
                o = slice(half * BLK // 2, (half + 1) * BLK // 2)
                dve.reciprocal(rc[:, o], dsum[:, o]).then_inc(rc_out, 1)

            def body(i, s, ahead=True, attend=True, more=True):
                for m in range(KC):
                    if attend:
                        n = (i - 1) * KC + m
                        dve.wait_ge(rb_out, n + 1)
                        dve.wait_ge(num_done, n + 1)
                        wait(dve, al_out, n - 1)
                        dve.tensor_tensor(at[:, m % 2, :], bN[m % 2][:, :], rb[:, m % 2, :], ALU.mult)\
                            .then_inc(at_out, 1)
                    if ahead:
                        n = i * KC + m
                        dve.wait_ge(qh_out, n + 1)
                        dve.scalar_tensor_tensor(out=ql[:, m, :], in0=bQ[m % 2][:, :], scalar=0.0,
                                                 in1=f32(qh[:, m, :]), op0=ALU.max, op1=ALU.subtract)\
                            .then_inc(ql_out, 1)
                    if attend:
                        n = (i - 1) * KC + m
                        dve.wait_ge(ah_out, n + 1)
                        dve.tensor_tensor(al[:, m, :], at[:, m % 2, :], f32(ah[:, m, :]), ALU.subtract)\
                            .then_inc(al_out, 1)
                if more:
                    split_x(i + 1, 0)
                    split_x(i + 1, 1)
                if attend:
                    out_tile(i, 0)
                if more:
                    split_x(i + 1, 2)
                if ahead:
                    dve.wait_ge(dlow_out, i + 1)
                    wait(dve, rc_out, 2 * i)
                    dve.scalar_tensor_tensor(out=dsum[:, :], in0=bDen[0:HEADS, :], scalar=DEN_EPS, in1=dlow[:, :],
                                             op0=ALU.add, op1=ALU.add).then_inc(dsum_out, 1)
                    dve.wait_ge(dsum_out, i + 1)
                    wait(dve, rcl_out, i)
                    reciprocals(i, 0)
                if attend:
                    out_tile(i, 1)
                if ahead:
                    reciprocals(i, 1)
                if attend:
                    out_tile(i, 2)
                if more:
                    split_x(i + 1, 3)
                if ahead:
                    dve.wait_ge(rch_out, i + 1)
                    dve.tensor_tensor(rc2[HEADS:2 * HEADS, :], rc[:, :], f32(rc2[0:HEADS, :]), ALU.subtract)\
                        .then_inc(rcl_out, 1)
                if attend:
                    out_tile(i, 3)

            split_low(0, wqh, wql)
            for c in range(KC):
                split_x(0, c)
            split_low(1, wph, wpl)
            dve.wait_ge(consts, 5)
            dve.tensor_copy(fan[:, :, :], fanf[:, :, :]).then_inc(ready, 1)
            blocks(dve, body)


def build(nc, d, out_dram):
    d = dict(d)
    d["xt"] = nc.dram_tensor("xt_scratch", [P, NB * KC * BLK], F32).ap()
    d["ffn"] = nc.dram_tensor("ffn_scratch", [TOK // P, P, DIM], F32).ap()
    with ExitStack() as ctx:
        b = Bench(nc, ctx, "w_")
        w = ffn_weights(b, nc, d)
        load_ffn(nc, d, w)
        run_ffn(nc, d, w)
    with ExitStack() as ctx:
        b = Bench(nc, ctx, "kv_")
        kv = {"numh": [b.sb(f"numh{s}", [P, KC, P], F32R) for s in range(BATCH)],
              "numl": [b.sb(f"numl{s}", [P, KC, P], F32R) for s in range(BATCH)],
              "den": [b.sb(f"den{s}", [P, KC, P], F32R) for s in range(BATCH)]}
        run_keyvalue(nc, d, kv)
        run_attention(nc, d, kv, out_dram)



def kernel(**inputs):
    import numpy as np
    import concourse.bacc as bacc
    from concourse.bass_utils import run_bass_kernel_spmd

    a = {k.removeprefix("L0_ffn_").removeprefix("L0_attn_"): np.asarray(v) for k, v in inputs.items()}

    def chunked(m):
        c = m.shape[0] // P
        return m.reshape(c, P, -1).transpose(1, 0, 2).reshape(P, -1)

    def every(v):
        return np.broadcast_to(v.reshape(1, -1), (P, v.size))

    def twice(m):
        return np.concatenate([m, m], axis=0)

    qkv_t = a["qkv_weight"].T
    host = {
        "x": a["x"].reshape(TOK // P, P, DIM),
        "enc_w": chunked(a["enc_w"]),
        "s2c_w": chunked(a["s2c_w"]),
        "e_w1": twice(a["e_w1"].transpose(1, 0, 2).reshape(MOE, NE * EH)),
        "e_w2": chunked(a["e_w2"].reshape(NE * EH, MOE)),
        "c2s_w": twice(a["c2s_w"]),
        "dec_w": chunked(a["dec_w"]),
        "r_w1": twice(np.concatenate([a["r_w1"], a["r_w1"]], axis=1)),
        "r_w2": twice(a["r_w2"]),
        "e_b2": twice(np.concatenate([a["e_b2"], a["e_b2"]], axis=1)),
        "enc_b": a["enc_b"].reshape(HC, P).T,
        "c2s_b": a["c2s_b"].reshape(HC, P).T,
        "e_b1": a["e_b1"].reshape(NJ, P).T,
        "r_b1": twice(a["r_b1"].reshape(MOE, 1)),
        "s2c_b": twice(a["s2c_b"].reshape(MOE, 1)),
        "r_b2": every(a["r_b2"]),
        "ln_g": every(a["ln_g"]),
        "dec_b": every(a["dec_b"]),
        "wkv": np.stack([chunked(qkv_t[:, DIM:2 * DIM]), chunked(qkv_t[:, 2 * DIM:3 * DIM])]),
        "wqp": np.stack([chunked(qkv_t[:, 0:DIM]), chunked(a["proj_weight"].T)]),
        "bias2": np.stack([every(a["proj_bias"]), every(a["ln_b"])], axis=1),
    }
    nc = bacc.Bacc("TRN2", target_bir_lowering=False, num_devices=1)
    arrays, d = {}, {}
    for name, v in host.items():
        v = np.ascontiguousarray(v)
        arrays[f"in_{name}"] = v
        d[name] = nc.dram_tensor(f"in_{name}", v.shape, mybir.dt.from_np(v.dtype), kind="ExternalInput").ap()
    out = nc.dram_tensor("out_y", (TOK // P, P, DIM), F32, kind="ExternalOutput").ap()
    build(nc, d, out)
    r = run_bass_kernel_spmd(nc, [arrays], core_ids=[0])
    return r.results[0]["out_y"].reshape(BATCH, SEQ, DIM)
```

```python
from contextlib import ExitStack

import concourse.bass as bass
from concourse import mybir

ALU = mybir.AluOpType
ACT = mybir.ActivationFunctionType
AX = mybir.AxisListType
F32 = mybir.dt.float32
F32R = mybir.dt.float32r

P = 128
BATCH, SEQ, DIM = 2, 4096, 512
TOK = BATCH * SEQ
BLK = 512
NB = TOK // BLK
NT = BLK // P
KC = DIM // P
HID = 1024
HC = HID // P
MOE = 64
NE = 8
EH = 512
EC = EH // P
NJ = NE * EC
HEADS, HD = 32, 16
HG = P // HD
LN_EPS = 1e-5
DEN_EPS = 1e-15
DEC_ORDER = (2, 0, 1, 3)
COLUMNS = (("enc_b", HC), ("c2s_b", HC), ("e_b1", NJ), ("r_b1", 1), ("s2c_b", 1), ("r_b2", NE))
COLS = sum(n for _, n in COLUMNS)
SMALL = P + NE + P


def wait(eng, sem, value):
    if isinstance(value, int) and value <= 0:
        return
    eng.wait_ge(sem, value)


def f32(ap):
    return ap.bitcast(F32)


class Bench:

    def __init__(self, nc, ctx, tag):
        self.nc, self.ctx, self.tag = nc, ctx, tag

    def sb(self, name, shape, dt=F32):
        return self.ctx.enter_context(self.nc.sbuf_tensor(self.tag + name, shape, dt))

    def first_use(self, name, shape):
        with self.nc.sbuf_tensor(self.tag + name, shape, F32) as t:
            return t

    def psum(self, name):
        return self.ctx.enter_context(self.nc.psum_tensor(self.tag + name, [P, 512], F32))

    def sem(self, name):
        return self.ctx.enter_context(self.nc.semaphore(self.tag + name))


def pass3(pe, out, w_hi, w_lo, x_hi, x_lo, start, stop):
    pe.matmul(out, w_hi, x_hi, start=start, stop=False)
    pe.matmul(out, w_lo, x_hi, start=False, stop=False)
    return pe.matmul(out, w_hi, x_lo, start=False, stop=stop)



class Branch:

    def __init__(self, nc, b, d):
        self.out = b.sb("out", [P, NT, DIM])
        self.gain = b.sb("ln_g", [P, DIM])
        self.half_down = b.sb("half_down", [P, NT])
        self.st, self.mv = b.sb("st2", [P, NT, 6]), b.sb("mv2", [P, NT, 2])
        self.ve, self.rs = b.sb("ve2", [P, NT]), b.sb("rs2", [P, NT])
        self.eps4, self.held = b.sb("eps4", [P, NT]), b.sb("held", [P, NT])
        self.dram = d["ffn"]
        self.dec_out, self.fstat, self.fmv, self.fve, self.frs, self.fnorm, self.scaled, self.stored = (
            b.sem(n) for n in ("dec_out", "fstat", "fmv", "fve", "frs", "fnorm", "scaled", "out_stored"))

    def hold(self, dve, k, sem, value):
        dve.wait_ge(sem, value)
        dve.memset(self.held[:, k:k + 1], 0.0)

    def stats_dve(self, dve, blk, k):
        dve.wait_ge(self.dec_out, blk * NT + DEC_ORDER.index(k) + 1)
        dve.bn_stats(self.st[:, k, :], self.out[:, k, :]).then_inc(self.fstat, 1)
        if k == NT - 1:
            self.hold(dve, 1, self.fstat, blk * NT + NT)
            for t in range(NT):
                dve.bn_aggr(self.mv[:, t, :], self.st[:, t, :]).then_inc(self.fmv, 1)

    def stats_pool(self, pool, blk):
        pool.wait_ge(self.fmv, blk * NT + NT)
        wait(pool, self.fnorm, blk * NT)
        pool.tensor_tensor(self.ve[:, :], self.mv[:, :, 1], self.eps4[:, :], ALU.add).then_inc(self.fve, 1)
        pool.wait_ge(self.fve, blk + 1)
        pool.tensor_tensor(self.rs[:, :], self.ve[:, :], self.half_down[:, :], ALU.pow).then_inc(self.frs, 1)

    def norm_dve(self, dve, blk, k):
        dve.wait_ge(self.frs, blk + 1)
        dve.wait_ge(self.fmv, blk * NT + NT)
        dve.tensor_scalar(self.out[:, k, :], self.out[:, k, :], self.mv[:, k, 0:1], self.rs[:, k:k + 1],
                          ALU.subtract, ALU.mult).then_inc(self.fnorm, 1)

    def scale_pool(self, pool, blk, k):
        pool.wait_ge(self.fnorm, blk * NT + k + 1)
        pool.tensor_tensor(self.out[:, k, :], self.out[:, k, :], self.gain[:, :], ALU.mult).then_inc(self.scaled, 1)

    def store(self, sp, blk):
        sp.wait_ge(self.scaled, blk * NT + NT)
        sp.dma_start(self.dram[bass.ds(blk * NT, NT), :, :].rearrange("t p c -> p t c"), self.out[:, :, :])\
            .then_inc(self.stored, 16)


def ffn_weights(b, branch):
    w = {}
    w["e1_raw"] = b.first_use("e1_raw", [P, NE * EH])
    w["e1"] = b.sb("e1", [P, NE * EH], F32R)
    w["enc_h"] = b.sb("enc_h", [P, KC, HID], F32R)
    w["enc_raw"] = b.first_use("enc_raw", [P, KC, HID])
    w["enc_l"] = b.sb("enc_l", [P, KC, HID], F32R)
    w["dec_h"] = b.sb("dec_h", [P, HC, DIM], F32R)
    w["dec_raw"] = b.first_use("dec_raw", [P, HC, DIM])
    w["dec_l"] = b.sb("dec_l", [P, HC, DIM], F32R)
    w["s2c_h"] = b.sb("s2c_h", [P, HC, P], F32R)
    w["s2c_raw"] = b.first_use("s2c_raw", [P, HC, P])
    w["s2c_l"] = b.sb("s2c_l", [P, HC, P], F32R)
    w["e2"] = b.sb("e2", [P, NJ, P], F32R)
    w["c2s_raw"] = b.first_use("c2s_raw", [P, HID])
    w["c2s"] = b.sb("c2s", [P, HID], F32R)
    w["r1"] = b.sb("r1", [P, P], F32R)
    w["r2"] = b.sb("r2", [P, NE], F32R)
    w["b2h"], w["b2l"] = b.sb("b2h", [2 * NE, P], F32R), b.sb("b2l", [2 * NE, P], F32R)
    w["twice"] = b.sb("twice", [P, P], F32R)
    w["pick"] = b.sb("pick", [2 * NE, NE], F32R)
    w["ident"] = b.sb("ident", [P, P], F32)
    w["ones"] = b.sb("ones", [P, 2], F32R)
    w["x"] = b.sb("x", [P, NT, DIM])
    w["rows"] = b.sb("rows", [P, BLK], F32R)
    w["pick_bias"] = b.sb("pick_bias", [P, P], F32R)
    w["cols"] = b.sb("cols", [P, COLS])
    w["ln_g"], w["half_down"] = branch.gain, branch.half_down
    at = 0
    for name, n in COLUMNS:
        w[name] = w["cols"][:, at:at + n]
        at += n
    w["probs"] = b.sb("probs", [P, NT, 2 * NE])
    w["top2"] = b.sb("top2", [P, NT, NE])
    w["comb_pad"] = b.sb("comb_pad", [P, NT, P])
    w["x_in"], w["s2c_in"] = b.sem("x_in"), b.sem("s2c_in")
    w["enc_in"] = [b.sem(f"enc_in{c}") for c in range(KC)]
    return w


def load_x(sp, d, w, blk):
    sp.dma_start(w["x"][:, :, :], d["x"][bass.ds(blk * NT, NT), :, :].rearrange("t p c -> p t c"))\
        .then_inc(w["x_in"], 16)


def ffn_constants(nc, d, w):
    with ExitStack() as ctx:
        b = Bench(nc, ctx, "fw_")
        small = b.sb("small", [P, SMALL])
        onesf, twicef = b.sb("onesf", [P, 2]), b.sb("twicef", [P, P])
        pickf, pbf = b.sb("pickf", [2 * NE, NE]), b.sb("pbf", [P, P])
        small_in, cols_in, gain_in = b.sem("small_in"), b.sem("cols_in"), b.sem("gain_in")
        consts, drawn, const_copied = b.sem("consts"), b.sem("drawn"), b.sem("const_copied")
        r_w1, r_w2, e_b2 = small[:, 0:P], small[:, P:P + NE], small[0:2 * NE, P + NE:2 * P + NE]

        block = ctx.enter_context(nc.Block())

        @block.sync
        def _(sp):
            load_x(sp, d, w, 0)
            sp.wait_ge(w["x_in"], 16)
            for c in range(KC):
                sp.dma_start(w["enc_raw"][:, c, :], d["enc_w"][:, c * HID:(c + 1) * HID]).then_inc(w["enc_in"][c], 16)
            sp.dma_start(w["s2c_raw"][:, :, :], d["s2c_w"][:, :].rearrange("p (c n) -> p c n", c=HC))\
                .then_inc(w["s2c_in"], 16)

        @block.gpsimd
        def _(pool):
            pool.dma_start(small[:, :], d["small"][:, :]).then_inc(small_in, 16)
            pool.dma_start(w["cols"][:, :], d["cols"][:, :]).then_inc(cols_in, 16)
            pool.dma_start(w["ln_g"][:, :], d["ln_g"][:, :]).then_inc(gain_in, 16)

            n = 0

            def diagonal(t, base):
                nonlocal n
                wait(pool, drawn, n)
                pool.affine_select(out=t, in_=t, compare_op=ALU.not_equal, fill=1.0, base=base,
                                   pattern=[[-1, t.shape[1]]], channel_multiplier=1).then_inc(drawn, 1)
                n += 1
            pool.wait_ge(consts, 3)
            diagonal(w["ident"][:, :], 0)
            for base in (0, MOE, -MOE):
                diagonal(twicef[:, :], base)
            for base in (0, -NE):
                diagonal(pickf[:, :], base)
            pool.wait_ge(gain_in, 16)

        @block.vector
        def _(dve):
            dve.memset(w["ident"][:, :], 0.0).then_inc(consts, 1)
            dve.memset(twicef[:, :], 0.0).then_inc(consts, 1)
            dve.memset(pickf[:, :], 0.0).then_inc(consts, 1)
            dve.memset(pbf[:, :], 0.0).then_inc(consts, 1)
            dve.memset(onesf[:, :], 1.0).then_inc(consts, 1)
            dve.memset(w["half_down"][:, :], -0.5).then_inc(consts, 1)
            dve.memset(w["probs"][:, :, :], -1.0).then_inc(consts, 1)
            dve.memset(w["top2"][:, :, :], -1.0).then_inc(consts, 1)
            dve.memset(w["comb_pad"][:, :, :], 0.0).then_inc(consts, 1)
            dve.wait_ge(consts, 9)
            for r in (64, 96):
                dve.memset(pbf[r:r + 1, :], 1.0).then_inc(consts, 1)
            dve.wait_ge(consts, 11)
            dve.tensor_copy(w["pick_bias"][:, :], pbf[:, :]).then_inc(const_copied, 1)
            dve.tensor_copy(w["ones"][:, :], onesf[:, :]).then_inc(const_copied, 1)
            dve.wait_ge(small_in, 16)
            dve.tensor_copy(w["r1"][:, :], r_w1).then_inc(const_copied, 1)
            dve.tensor_copy(w["r2"][:, :], r_w2).then_inc(const_copied, 1)
            dve.tensor_copy(w["b2h"][:, :], e_b2).then_inc(const_copied, 1)
            dve.wait_ge(const_copied, 5)
            dve.tensor_tensor(w["r1"][MOE:P, :], r_w1[MOE:P, :], f32(w["r1"][MOE:P, :]),
                              ALU.subtract).then_inc(const_copied, 1)
            dve.tensor_tensor(w["r2"][MOE:P, :], r_w2[MOE:P, :], f32(w["r2"][MOE:P, :]),
                              ALU.subtract).then_inc(const_copied, 1)
            dve.tensor_tensor(w["b2l"][:, :], e_b2, f32(w["b2h"][:, :]), ALU.subtract).then_inc(const_copied, 1)
            dve.wait_ge(cols_in, 16)
            dve.tensor_scalar(w["enc_b"], w["enc_b"], 0.5, None, ALU.mult).then_inc(const_copied, 1)
            dve.tensor_scalar(w["c2s_b"], w["c2s_b"], 0.5, None, ALU.mult).then_inc(const_copied, 1)
            dve.wait_ge(drawn, 6)
            dve.tensor_copy(w["twice"][:, :], twicef[:, :]).then_inc(const_copied, 1)
            dve.tensor_copy(w["pick"][:, :], pickf[:, :]).then_inc(const_copied, 1)
            dve.wait_ge(const_copied, 12)


AHEAD = ("enc_part", "enc", "s2c", "cont")
TWO_AHEAD = ("load_x", "ln_stats", "ln_norm", "turn", "xt", "xsplit")
BEHIND = ("dec_end", "fin_stats", "fin_norm")
LAG = 4


def ffn_steps():
    at = {}

    def put(j, *steps):
        at.setdefault(j, []).extend(steps)
    for q in range(1, 4):
        put(q - 1, ("route", q))
    put(1, ("dec_end", 1))
    put(5, ("dec_end", 3))
    for e, (j_spread, j_z) in enumerate(((8, 9), (10, 11), (12, 13), (14, 15), (17, 19), (21, 23), (25, 27), (29, 31))):
        put(j_spread, ("spread", e))
        put(j_z, ("z", e))
    for t in range(NT):
        put(10 + t, ("fin_stats", t))
        put(15 + t, ("fin_norm", t))
        put(19 + t, ("ln_stats", t))
        put(24 + t, ("ln_norm", t))
    for m in range(1, HC - 1):
        j = (m - 1) * (KC + 1)
        for c in range(KC):
            put(j + c, ("enc_part", m * KC + c))
        put(j + KC - 1, ("enc", m))
        put(j + KC, ("s2c", m - 1))
    put(5, ("comb_t", 0))
    put(NJ - 2, ("enc_part", (HC - 1) * KC))
    steps = [("load_x", 0), ("dec_end", 2), ("rt1", 0), ("e1", 0), ("dec_end", 0), ("e1", 1), ("enc_part", 0),
             ("enc_part", 1), ("logits", 0), ("e1", 2), ("enc_part", 2), ("e1", 3), ("enc_part", 3), ("enc", 0),
             ("route", 0)]
    for j in range(NJ):
        steps.append(("e2", j))
        if j + LAG < NJ:
            steps.append(("e1", j + LAG))
        steps += at.get(j, [])
    parts = HC * KC
    steps += [("enc_part", parts - 3), ("acc", 0), ("enc_part", parts - 2), ("s2c", HC - 2), ("turn", 0), ("xt", 0),
              ("turn", 1), ("dup", 0), ("enc_part", parts - 1), ("xt", 1), ("turn", 2), ("xsplit", 0), ("c2s", 0),
              ("enc", HC - 1), ("dec_bias", 0), ("dec_bias", 1), ("dec_bias", 3), ("turn", 3), ("c2s", 1), ("xt", 2),
              ("dec_bias", 2), ("xsplit", 1)]
    behind_dec = {0: [("s2c", HC - 1), ("xt", 3), ("xsplit", 2)], 1: [("xsplit", 3)], 2: [("cont", 0)]}
    for k in range(HC):
        steps.append(("dec", k))
        if k + 2 < HC:
            steps.append(("c2s", k + 2))
        steps += behind_dec.get(k, [])
    for name, number in (("enc_part", parts), ("enc", HC), ("s2c", HC), ("e1", NJ), ("dec_end", NT)):
        assert [k for n, k in steps if n == name] == (list(DEC_ORDER) if name == "dec_end" else list(range(number)))
    return steps


SPLITS = ([("enc", c) for c in range(KC)] + [("s2c", 0)] + [("e1", q) for q in range(4)] + [("e2", q) for q in range(2)]
          + [("c2s", 0)] + [("dec", q) for q in range(4)])


def ffn_prologue_steps():
    def norm(i):
        return [("ln_stats", t, i) for t in range(NT)] + [("ln_norm", t, i) for t in range(NT)]

    def turns(i, *between):
        steps = []
        for c in range(KC):
            steps += [("turn", c, i), ("xt", c, i)] + [(*b, i) for b in between[c:c + 1]] + [("xsplit", c, i)]
        return steps

    def splits(*names):
        return [("split_w", n, -1) for n, (name, _) in enumerate(SPLITS) if name in names]
    enc, s2c, e1, e2, c2s, dec = (splits(name) for name in ("enc", "s2c", "e1", "e2", "c2s", "dec"))
    stats, normed = norm(-1)[:NT], norm(-1)[NT:]
    steps = norm(-2) + turns(-2, *[s[:2] for s in enc]) + [("load_x", 0, -1), ("load_rest", 0, -1)]
    behind = [s2c + e1[0:1], e1[1:3], e1[3:4] + [("s2c_sum", 0, -1)], stats + e2[0:1], normed + e2[1:2], c2s + dec[0:1],
              dec[1:3], dec[3:4]]
    for m in range(HC):
        steps += [("enc_part", m * KC + c, -1) for c in range(KC)] + [("enc", m, -1)] + behind[m]
        if m >= 2:
            steps.append(("s2c", m - 2, -1))
    return steps + [("s2c", HC - 2, -1)] + turns(-1) + [("s2c", HC - 1, -1), ("cont", 0, -1), ("dec_sum", 0, -1)]


def run_ffn(nc, d, w, branch, ahead):
    with ExitStack() as ctx:
        b = Bench(nc, ctx, "f_")
        x = w["x"]
        xt = b.sb("xt", [P, 2, BLK])
        xh, xl = b.sb("xh", [P, KC, BLK], F32R), b.sb("xl", [P, KC, BLK], F32R)
        sp_t, sph, spl = b.sb("sp_t", [P, 2, BLK]), b.sb("sph", [P, 2, BLK], F32R), b.sb("spl", [P, 2, BLK], F32R)
        hid, hidh = b.sb("hid", [P, 2, BLK]), b.sb("hidh", [P, 4, BLK], F32R)
        e2_raw = b.first_use("e2_raw", [P, NJ, MOE])
        hidl = b.sb("hidl", [P, 4, BLK], F32R)
        cont, conth, contl = b.sb("cont", [P, BLK]), b.sb("conth", [P, BLK], F32R), b.sb("contl", [P, BLK], F32R)
        midh, midl = b.sb("midh", [P, BLK], F32R), b.sb("midl", [P, BLK], F32R)
        comb_b = b.sb("comb_b", [P, 2, BLK])
        z, acc = b.sb("z", [P, 2, BLK]), b.sb("acc", [P, BLK])
        out = branch.out
        st, mv = b.sb("st", [P, NT, 6]), b.sb("mv", [P, NT, 2])
        ve, rs = b.sb("ve", [P, NT]), b.sb("rs", [P, NT])
        lg, lgm, ex = b.sb("lg", [P, NT, NE]), b.sb("lgm", [P, NT, NE]), b.sb("ex", [P, NT, NE])
        top, left = b.sb("top", [P, NT, NE]), b.sb("left", [P, NT, 2 * NE])
        picked, comb = b.sb("picked", [P, NT, NE]), b.sb("comb", [P, NT, NE])
        comb_r = b.sb("comb_r", [P, NT, NE], F32R)
        s4 = b.sb("s4", [P, 5, NT])
        eps, eps4 = b.sb("eps", [P, NT]), branch.eps4

        bE, bD = [b.psum(f"E{i}") for i in range(2)], [b.psum(f"D{i}") for i in range(4)]
        bS, bG = b.psum("S"), b.psum("G")
        bX = [bD[0], bD[1], bG]

        sem = b.sem

        x_in, out_stored, dec_out = w["x_in"], branch.stored, branch.dec_out
        w_in = {("enc", c): w["enc_in"][c] for c in range(KC)}
        w_in[("s2c", 0)] = w["s2c_in"]
        for name, q in SPLITS:
            if (name, q) not in w_in:
                w_in[(name, q)] = sem(f"{name}_in{q}")
        dec_b_in, wh_out, wl_out, summed, biased = (sem(n) for n in (
            "dec_b_in", "wh_out", "wl_out", "summed", "biased"))
        xt_stored = [sem("xt_stored0"), sem("xt_stored1")]
        turned, enc_done, s2c_done, rt1_done, logits_done = (sem(n) for n in (
            "turned", "enc_done", "s2c_done", "rt1_done", "logits_done"))
        combt_done, spread_done, e1_done, e2_done, dup_done, c2s_done, dec_done = (sem(n) for n in (
            "combt_done", "spread_done", "e1_done", "e2_done", "dup_done", "c2s_done", "dec_done"))
        xt_out, sp_out, rate_out, cont_out, rh_out, exp_out = (sem(n) for n in (
            "xt_out", "sp_out", "rate_out", "cont_out", "rh_out", "exp_out"))
        combrow_out, combb_out, hid_out, hidh_act, moeh_out = (sem(n) for n in (
            "combrow_out", "combb_out", "hid_out", "hidh_act", "moeh_out"))
        xstat, xmv, xnorm, xh_out, xl_out, sph_out, spl_out = (sem(n) for n in (
            "xstat", "xmv", "xnorm", "xh_out", "xl_out", "sph_out", "spl_out"))
        hidh_dve, hidl_out, rateh_out, ratel_out, conth_out, contl_out = (sem(n) for n in (
            "hidh_dve", "hidl_out", "rateh_out", "ratel_out", "conth_out", "contl_out"))
        rhh_out, rhl_out, route, z_out, acch_out, accl_out, moel_out = (sem(n) for n in (
            "rhh_out", "rhl_out", "route", "z_out", "acch_out", "accl_out", "moel_out"))
        last_out = sem("last_out")
        xeps = sem("xeps")
        xve, xrs, acc_out = sem("xve"), sem("xrs"), sem("acc_out")

        def split_of(name, q):
            if name == "enc":
                return w["enc_raw"][:, q, :], w["enc_h"][:, q, :], w["enc_l"][:, q, :]
            if name == "s2c":
                return w["s2c_raw"][:, :, :], w["s2c_h"][:, :, :], w["s2c_l"][:, :, :]
            if name == "e2":
                s = slice(q * NJ // 2, (q + 1) * NJ // 2)
                return e2_raw[:, s, :], w["e2"][:, s, 0:MOE], w["e2"][:, s, MOE:P]
            if name == "dec":
                s = slice(2 * q, 2 * q + 2)
                return w["dec_raw"][:, s, :], w["dec_h"][:, s, :], w["dec_l"][:, s, :]
            s = slice(q * 1024, (q + 1) * 1024)
            return w[name + "_raw"][:, s], w[name][:, s]

        def rounded(n):
            s = slice(n % 2 * 2, n % 2 * 2 + 2)
            return hidh[MOE:P, s, :].rearrange("p a b -> p (a b)")

        steps = ffn_steps()
        block = ctx.enter_context(nc.Block())

        def walk(eng, step):
            before = []
            uses = 0
            for name, k, i in ffn_prologue_steps():
                if name != "turn":
                    step(name, k, i, (k % 2,) if name == "xt" else None)
                    continue
                step(name, k, i, (uses % 2, before[-2] if uses >= 2 else None))
                before.append((name, k, i))
                uses += 1
            before = [(name, k) for name, k, _ in before[-2:]]

            def body(i, last=0):
                nonlocal before
                here = [s for s in steps if not (last >= 1 and s[0] in TWO_AHEAD or last >= 2 and s[0] in AHEAD)]
                on_e = [s for s in here if s[0] in ("e1", "turn")]
                had = [(*s, i - 1) for s in before] + [(*s, i) for s in on_e]
                for name, k in here:
                    if name in BEHIND and isinstance(i, int) and i == 0:
                        continue
                    e = None
                    if name in ("e1", "turn"):
                        n = on_e.index((name, k))
                        e = (n % 2, had[n])
                    elif name == "xt":
                        e = (on_e.index(("turn", k)) % 2,)
                    step(name, k, i, e)
                assert len(on_e) % 2 == 0
                before = on_e[-2:]

            body(0)
            with eng.Fori(1, NB - 2) as i:
                body(i)
            body(NB - 2, 1)
            body(NB - 1, 2)
            for t in DEC_ORDER:
                step("dec_end", t, NB, None)

        def first(i):
            return isinstance(i, int) and i < 0

        def enc_bank(m, i):
            return bD[2 + m % 2] if first(i) else bD[2]

        DEC = HC - 1 + NT

        @block.sync
        def _(sp):
            def load(name, q, source):
                sp.dma_start(split_of(name, q)[0], source).then_inc(w_in[(name, q)], 16)

            def columns(name, q, n):
                return d[name][:, q * n:(q + 1) * n]

            def store_xt(blk, c):
                sp.wait_ge(xt_out, blk * KC + c + 1)
                sp.dma_start(d["xt"][:, bass.ds(blk * KC * BLK + c * BLK, BLK)],
                             xt[:, c % 2, :]).then_inc(xt_stored[c % 2], 16)

            def step(name, k, i, e):
                if name == "load_x":
                    sp.wait_ge(turned, (i + 2) * KC)
                    load_x(sp, d, w, i + 2)
                if name == "load_rest":
                    for q in range(2):
                        load("e2", q, columns("e_w2", q, 1024).rearrange("p (j n) -> p j n", n=MOE))
                    load("c2s", 0, d["c2s_w"][:, :])
                    sp.dma_start(comb_b[:, 0, :], d["dec_b"][:, :]).then_inc(dec_b_in, 16)
                    for q in range(4):
                        load("dec", q, columns("dec_w", q, 1024).rearrange("p (c n) -> p c n", n=DIM))
                if name == "xt":
                    store_xt(i + 2, k)
                if name == "fin_norm" and k == NT - 1:
                    branch.store(sp, i - 1)
                if name == "e1" and k == NJ - 1 and isinstance(i, int) and i == NB - 1:
                    sp.wait_ge(enc_done, NB * HC)
                    for h in range(2):
                        sp.wait_ge(xt_stored[h], 16 * NB * KC // 2)
                    sp.dma_start(ahead["xt"][:, 0:KC * BLK], d["xt"][:, 0:KC * BLK]).then_inc(ahead["xt_in"][0], 16)
                    sp.wait_ge(e1_done, NB * NJ)
                    for h in range(2):
                        sp.dma_start(ahead["wkv"][h], d["wkv"][h]).then_inc(ahead["wkv_in"][h], 16)
                    sp.dma_start(ahead["xt"][:, KC * BLK:2 * KC * BLK], d["xt"][:, KC * BLK:2 * KC * BLK])\
                        .then_inc(ahead["xt_in"][1], 16)
            for q in range(4):
                load("e1", q, columns("e_w1", q, 1024))
            walk(sp, step)
            for s in xt_stored:
                sp.wait_ge(s, 16 * NB * KC // 2)

        @block.tensor
        def _(pe):
            def take_e(e):
                bank, had = e
                if had is not None:
                    name, k, i = had
                    if name == "turn":
                        pe.wait_ge(xt_out, (i + 2) * KC + k + 1)
                    else:
                        pe.wait_ge(hid_out, i * NJ + k + 1)
                return bE[bank]

            def step(name, k, i, e):
                if name == "turn":
                    blk = i + 2
                    pe.wait_ge(xnorm, blk * NT + NT)
                    bank = take_e(e)
                    for t in range(NT):
                        m = pe.transpose(bank[:, t * P:(t + 1) * P], x[:, t, k * P:(k + 1) * P], w["ident"][:, :])
                    m.then_inc(turned, 1)
                elif name == "enc_part":
                    blk = i + 1
                    m, c = divmod(k, KC)
                    if m == 0:
                        pe.wait_ge(xl_out, blk * KC + c + 1)
                        if first(i):
                            pe.wait_ge(wl_out, c + 1)
                    bank = enc_bank(m, i)
                    if c == 0:
                        wait(pe, sp_out, blk * HC + m - (1 if first(i) else 0))
                        if m == 0:
                            wait(pe, dec_out, (i - 1) * NT + 1)
                    s = slice(m * P, (m + 1) * P)
                    mm = pass3(pe, bank[:, :], w["enc_h"][:, c, s], w["enc_l"][:, c, s], xh[:, c, :], xl[:, c, :],
                               c == 0, c == KC - 1)
                    if c == KC - 1:
                        mm.then_inc(enc_done, 1)
                elif name == "s2c_sum":
                    pe.wait_ge(wl_out, SPLITS.index(("s2c", 0)) + 1)
                    for c in range(HC):
                        pe.matmul(bG[:, 0:2], w["s2c_h"][:, c, :], w["ones"][:, 0:2], start=(c == 0), stop=False)
                        m = pe.matmul(bG[:, 0:2], w["s2c_l"][:, c, :], w["ones"][:, 0:2], start=False,
                                      stop=(c == HC - 1))
                    m.then_inc(summed, 1)
                elif name == "dec_sum":
                    pe.wait_ge(wl_out, len(SPLITS))
                    pe.wait_ge(cont_out, 1)
                    for c in range(HC):
                        pe.matmul(bS[:, :], w["ones"][:, 0:1].broadcast_to([P, P]), w["dec_h"][:, c, :], start=(c == 0), stop=False)
                        m = pe.matmul(bS[:, :], w["ones"][:, 0:1].broadcast_to([P, P]), w["dec_l"][:, c, :], start=False,
                                      stop=(c == HC - 1))
                    m.then_inc(summed, 1)
                elif name == "s2c":
                    blk = i + 1
                    if k == 0 and isinstance(i, int) and i == 0:
                        pe.wait_ge(biased, 2)
                    pe.wait_ge(spl_out, blk * HC + k + 1)
                    if k == 0:
                        wait(pe, cont_out, blk)
                    pass3(pe, bS[:, :], w["s2c_h"][:, k, :], w["s2c_l"][:, k, :], sph[:, k % 2, :], spl[:, k % 2, :],
                          k == 0, k == HC - 1).then_inc(s2c_done, 1)
                elif name == "rt1":
                    pe.wait_ge(contl_out, i + 1)
                    wait(pe, rate_out, i * HC)
                    pe.matmul(bG[:, :], w["r1"][:, :], conth[:, :], start=True, stop=False)
                    pe.matmul(bG[:, :], w["r1"][:, :], contl[:, :], start=False, stop=True).then_inc(rt1_done, 1)
                elif name == "logits":
                    pe.wait_ge(rhl_out, i + 1)
                    for t in range(NT):
                        s = slice(t * P, (t + 1) * P)
                        pe.matmul(bG[:, t * NE:(t + 1) * NE], midh[:, s], w["r2"][:, :], start=True, stop=False)
                        m = pe.matmul(bG[:, t * NE:(t + 1) * NE], midl[:, s], w["r2"][:, :], start=False, stop=True)
                    m.then_inc(logits_done, 1)
                elif name == "comb_t":
                    pe.wait_ge(route, i * 16 + 16)
                    for t in range(NT):
                        m = pe.transpose(bG[:, t * P:(t + 1) * P], w["comb_pad"][:, t, :], w["ident"][:, :])
                    m.then_inc(combt_done, 1)
                elif name == "spread":
                    pe.wait_ge(combrow_out, i + 1)
                    if k == 0:
                        wait(pe, dec_out, i * NT)
                    else:
                        pe.wait_ge(combb_out, i * NE + k)
                    pe.matmul(bD[3][:, :], w["pick"][:, k:k + 1].broadcast_to([2 * NE, P]), w["rows"][0:2 * NE, :],
                              start=True, stop=True).then_inc(spread_done, 1)
                elif name == "e1":
                    bank = take_e(e)
                    s = slice(k * P, (k + 1) * P)
                    pe.matmul(bank[:, :], w["e1"][:, s], conth[:, :], start=True, stop=False)
                    pe.matmul(bank[:, :], w["e1"][:, s], contl[:, :], start=False, stop=True).then_inc(e1_done, 1)
                elif name == "e2":
                    expert, q = divmod(k, EC)
                    pe.wait_ge(hidl_out, i * NJ + k + 1)
                    if q == 0 and expert < 2:
                        wait(pe, dec_out, (i - 1) * NT + expert + 2)
                    elif q == 0 and expert > 2:
                        pe.wait_ge(z_out, i * NE + expert - 2)
                    elif q == 0:
                        pe.wait_ge(combrow_out, i + 1)
                    pe.matmul(bX[expert % 3][:, :], w["e2"][:, k, :], hidh[:, k % 4, :], start=(q == 0), stop=False)
                    pe.matmul(bX[expert % 3][:, :], w["e2"][:, k, :], hidl[:, k % 4, :], start=False,
                              stop=(q == EC - 1)).then_inc(e2_done, 1)
                elif name == "dup":
                    pe.wait_ge(z_out, i * NE + NE)
                    pe.matmul(bG[:, :], w["b2h"][:, :], w["rows"][0:2 * NE, :], start=True, stop=False)
                    pe.matmul(bG[:, :], w["b2l"][:, :], w["rows"][0:2 * NE, :], start=False, stop=False)
                    pe.wait_ge(accl_out, i + 1)
                    pe.matmul(bG[:, :], w["twice"][:, :], midh[:, :], start=False, stop=False)
                    pe.matmul(bG[:, :], w["twice"][:, :], midl[:, :], start=False, stop=True)\
                        .then_inc(dup_done, 1)
                elif name == "c2s":
                    pe.wait_ge(moel_out, i + 1)
                    if k:
                        pe.wait_ge(rate_out, i * HC + k)
                    s = slice(k * P, (k + 1) * P)
                    pe.matmul(bG[:, :], w["c2s"][:, s], midh[:, :], start=True, stop=False)
                    pe.matmul(bG[:, :], w["c2s"][:, s], midl[:, :], start=False, stop=True).then_inc(c2s_done, 1)
                elif name == "dec_bias":
                    if k == 0:
                        if isinstance(i, int) and i == 0:
                            pe.wait_ge(biased, 4)
                        pe.wait_ge(z_out, i * NE + NE)
                    elif k == 2 and not (isinstance(i, int) and i == NB - 1):
                        pe.wait_ge(sp_out, (i + 2) * HC)
                    elif k == 3:
                        pe.wait_ge(combb_out, i * NE + NE)
                    pe.matmul(bD[k][:, :], w["pick_bias"][64:P, :], w["rows"][64:P, :], start=True, stop=False)
                elif name == "dec":
                    pe.wait_ge(ratel_out, i * HC + k + 1)
                    for t in DEC_ORDER:
                        s = slice(t * P, (t + 1) * P)
                        last = k == HC - 1
                        pe.matmul(bD[t][:, :], hidh[:, k % 4, s], w["dec_h"][:, k, :], start=False, stop=False)
                        pe.matmul(bD[t][:, :], hidh[:, k % 4, s], w["dec_l"][:, k, :], start=False, stop=False)
                        m = pe.matmul(bD[t][:, :], hidl[:, k % 4, s], w["dec_h"][:, k, :], start=False, stop=last)
                        if last:
                            m.then_inc(dec_done, 1)
                    if not last:
                        m.then_inc(dec_done, 1)
            walk(pe, step)

        @block.scalar
        def _(act):
            def step(name, k, i, e):
                if name == "split_w":
                    act.wait_ge(w_in[SPLITS[k]], 16)
                    raw, hi, *lo = split_of(*SPLITS[k])
                    if lo:
                        act.activation(hi, raw, ACT.Copy).then_inc(wh_out, 1)
                    else:
                        wait(act, wl_out, k - 1)
                        act.activation(rounded(k), raw[MOE:P, :], ACT.Copy)
                        act.activation(hi[0:MOE, :], raw[0:MOE, :], ACT.Copy).then_inc(wh_out, 1)
                elif name == "dec_sum":
                    act.wait_ge(wl_out, len(SPLITS))
                elif name == "xt":
                    blk = i + 2
                    n = blk * KC + k
                    act.wait_ge(turned, n + 1)
                    if not (isinstance(n, int) and n < 2):
                        act.wait_ge(xl_out, n - 1)
                        act.wait_ge(xt_stored[k % 2], (blk * KC // 2 + k // 2) * 16)
                    act.activation(xt[:, k % 2, :], bE[e[0]][:, :], ACT.Copy).then_inc(xt_out, 1)
                elif name == "enc":
                    n = (i + 1) * HC + k
                    act.wait_ge(enc_done, n + 1)
                    wait(act, spl_out, n - 1)
                    act.activation(sp_t[:, k % 2, :], enc_bank(k, i)[:, :], ACT.Tanh,
                                   bias=w["enc_b"][:, k:k + 1], scale=0.5).then_inc(sp_out, 1)
                    act.wait_ge(sp_out, n + 1)
                    wait(act, s2c_done, n - 1)
                    act.activation(sph[:, k % 2, :], sp_t[:, k % 2, :], ACT.Copy).then_inc(sph_out, 1)
                elif name == "cont":
                    blk = i + 1
                    act.wait_ge(s2c_done, blk * HC + HC)
                    if first(i):
                        act.wait_ge(biased, 1)
                    wait(act, rhl_out, blk)
                    act.activation(cont[:, :], bS[:, :], ACT.Identity, bias=w["s2c_b"], scale=0.5)\
                        .then_inc(cont_out, 1)
                elif name == "rt1":
                    act.wait_ge(rt1_done, i + 1)
                    act.wait_ge(contl_out, i + 1)
                    act.activation(cont[:, :], bG[:, :], ACT.Relu, bias=w["r_b1"]).then_inc(rh_out, 1)
                elif name == "route" and k == 0:
                    act.wait_ge(route, i * 16 + 3)
                    act.activation(ex[:, :, :], lgm[:, :, :], ACT.Exp).then_inc(exp_out, 1)
                elif name == "comb_t":
                    act.wait_ge(combt_done, i + 1)
                    if isinstance(i, int) and i == 0:
                        act.wait_ge(biased, 4)
                    wait(act, dup_done, i)
                    act.activation(w["rows"][0:2 * NE, :], bG[0:2 * NE, :], ACT.Copy).then_inc(combrow_out, 1)
                elif name == "spread":
                    n = i * NE + k
                    act.wait_ge(spread_done, n + 1)
                    wait(act, z_out, n - 1)
                    act.activation(comb_b[:, k % 2, :], bD[3][:, :], ACT.Copy).then_inc(combb_out, 1)
                elif name == "e1":
                    n = i * NJ + k
                    act.wait_ge(e1_done, n + 1)
                    if k >= 2:
                        act.wait_ge(hidl_out, n - 1)
                    else:
                        wait(act, ratel_out, (i - 1) * HC + HC - 1 + k)
                    act.activation(hid[:, k % 2, :], bE[e[0]][:, :], ACT.Relu,
                                   bias=w["e_b1"][:, k:k + 1]).then_inc(hid_out, 1)
                    if k % 2:
                        act.wait_ge(hid_out, n + 1)
                        if k >= 4:
                            act.wait_ge(e2_done, n - 3)
                        else:
                            wait(act, dec_done, i * DEC)
                        act.activation(hidh[:, k % 4, :], hid[:, k % 2, :], ACT.Copy).then_inc(hidh_act, 1)
                elif name == "dup":
                    act.wait_ge(dup_done, i + 1)
                    act.activation(midh[:, :], bG[:, :], ACT.Copy).then_inc(moeh_out, 1)
                elif name == "c2s":
                    n = i * HC + k
                    act.wait_ge(c2s_done, n + 1)
                    if k >= 2:
                        act.wait_ge(ratel_out, n - 1)
                    else:
                        act.wait_ge(hidl_out, i * NJ + NJ - 1 + k)
                        if k % 2:
                            act.wait_ge(hidh_act, i * (NJ // 2) + NJ // 2)
                    act.activation(hid[:, k % 2, :], bG[:, :], ACT.Tanh, bias=w["c2s_b"][:, k:k + 1], scale=0.5)\
                        .then_inc(rate_out, 1)
                elif name == "dec_end":
                    blk = i - 1
                    n = DEC_ORDER.index(k)
                    if n == 0:
                        wait(act, out_stored, blk * 16)
                    act.wait_ge(dec_done, blk * DEC + HC + n)
                    act.activation(out[:, k, :], bD[k][:, :], ACT.Tanh, scale=0.25).then_inc(dec_out, 1)
            walk(act, step)

        @block.vector
        def _(dve):
            def hold(k, sem, value):
                branch.hold(dve, k, sem, value)

            def split(src, hi, lo, hi_sem, lo_sem, n):
                dve.tensor_copy(hi, src).then_inc(hi_sem, 1)
                dve.wait_ge(hi_sem, n)
                dve.tensor_tensor(lo, src, f32(hi), ALU.subtract).then_inc(lo_sem, 1)

            def step(name, k, i, e):
                if name == "split_w":
                    dve.wait_ge(wh_out, k + 1)
                    raw, hi, *lo = split_of(*SPLITS[k])
                    if lo:
                        dve.tensor_tensor(lo[0], raw, f32(hi), ALU.subtract).then_inc(wl_out, 1)
                    else:
                        dve.tensor_tensor(hi[MOE:P, :], raw[MOE:P, :], f32(rounded(k)), ALU.subtract)\
                            .then_inc(wl_out, 1)
                elif name == "s2c_sum":
                    dve.wait_ge(summed, 1)
                    dve.scalar_tensor_tensor(out=w["s2c_b"], in0=bG[:, 0:1], scalar=0.5, in1=w["s2c_b"],
                                             op0=ALU.mult, op1=ALU.add).then_inc(biased, 1)
                elif name == "dec_sum":
                    dve.wait_ge(summed, 2)
                    dve.wait_ge(dec_b_in, 16)
                    dve.scalar_tensor_tensor(out=z[:, 0, :], in0=comb_b[:, 0, :], scalar=2.0, in1=bS[:, :],
                                             op0=ALU.mult, op1=ALU.add).then_inc(biased, 1)
                    dve.wait_ge(biased, 2)
                    dve.tensor_copy(w["rows"][64:P, :], z[64:P, 0, :]).then_inc(biased, 1)
                    dve.wait_ge(biased, 3)
                    dve.tensor_tensor(w["rows"][96:P, :], z[96:P, 0, :], f32(w["rows"][96:P, :]),
                                      ALU.subtract).then_inc(biased, 1)
                elif name == "ln_stats":
                    blk = i + 2
                    dve.wait_ge(x_in, blk * 16 + 16)
                    dve.bn_stats(st[:, k, :], x[:, k, :]).then_inc(xstat, 1)
                    if k == NT - 1:
                        hold(0, xstat, blk * NT + NT)
                        for t in range(NT):
                            dve.bn_aggr(mv[:, t, :], st[:, t, :]).then_inc(xmv, 1)
                elif name == "ln_norm":
                    blk = i + 2
                    dve.wait_ge(xrs, blk + 1)
                    dve.wait_ge(xmv, blk * NT + NT)
                    dve.tensor_scalar(x[:, k, :], x[:, k, :], mv[:, k, 0:1], rs[:, k:k + 1],
                                      ALU.subtract, ALU.mult).then_inc(xnorm, 1)
                elif name == "xsplit":
                    blk = i + 2
                    n = blk * KC + k
                    dve.wait_ge(xt_out, n + 1)
                    wait(dve, enc_done, (i + 2) * HC)
                    split(xt[:, k % 2, :], xh[:, k, :], xl[:, k, :], xh_out, xl_out, n + 1)
                elif name == "enc":
                    n = (i + 1) * HC + k
                    dve.wait_ge(sph_out, n + 1)
                    wait(dve, s2c_done, n - 1)
                    dve.tensor_tensor(spl[:, k % 2, :], sp_t[:, k % 2, :], f32(sph[:, k % 2, :]), ALU.subtract)\
                        .then_inc(spl_out, 1)
                elif name == "cont":
                    blk = i + 1
                    dve.wait_ge(cont_out, blk + 1)
                    wait(dve, e1_done, blk * NJ)
                    split(cont[:, :], conth[:, :], contl[:, :], conth_out, contl_out, blk + 1)
                elif name == "rt1":
                    dve.wait_ge(rh_out, i + 1)
                    wait(dve, c2s_done, i * HC)
                    split(cont[:, :], midh[:, :], midl[:, :], rhh_out, rhl_out, i + 1)
                elif name == "route":
                    r = i * 16
                    wide = [P, NT, NE]

                    def over(q):
                        return s4[:, q, :].unsqueeze(2).broadcast_to(wide)

                    def after(n, ins):
                        ins.then_inc(route, 1)
                        dve.wait_ge(route, r + n)
                    if k == 0:
                        dve.wait_ge(logits_done, i + 1)
                        after(1, dve.tensor_tensor(lg[:, :, :], bG[:, 0:NT * NE].rearrange("p (t e) -> p t e", e=NE),
                                                   w["r_b2"].unsqueeze(1).broadcast_to(wide), ALU.add))
                        after(2, dve.tensor_reduce(s4[:, 0, :], lg[:, :, :], AX.X, ALU.max))
                        dve.tensor_tensor(lgm[:, :, :], lg[:, :, :], over(0), ALU.subtract).then_inc(route, 1)
                    elif k == 1:
                        dve.wait_ge(exp_out, i + 1)
                        after(4, dve.tensor_reduce(s4[:, 1, :], ex[:, :, :], AX.X, ALU.add))
                        after(5, dve.reciprocal(s4[:, 2, :], s4[:, 1, :]))
                        dve.tensor_tensor(w["probs"][:, :, 0:NE], ex[:, :, :], over(2), ALU.mult).then_inc(route, 1)
                    elif k == 2:
                        hold(2, route, r + 6)
                        for t in range(NT):
                            m = dve.max(top[:, t, :], w["probs"][:, t, 0:NE])
                        after(7, m)
                        dve.tensor_copy(w["top2"][:, :, 0:2], top[:, :, 0:2]).then_inc(route, 1)
                        hold(3, route, r + 8)
                        for t in range(NT):
                            m = dve.match_replace(left[:, t, :], w["top2"][:, t, :], w["probs"][:, t, :], -2.0)
                        m.then_inc(route, 1)
                    elif k == 3:
                        dve.wait_ge(route, r + 9)
                        after(10, dve.scalar_tensor_tensor(
                            out=picked[:, :, :], in0=left[:, :, 0:NE], scalar=0.0,
                            in1=w["probs"][:, :, 0:NE], op0=ALU.is_lt, op1=ALU.mult))
                        after(11, dve.tensor_reduce(s4[:, 3, :], picked[:, :, :], AX.X, ALU.add))
                        after(12, dve.reciprocal(s4[:, 4, :], s4[:, 3, :]))
                        after(13, dve.tensor_tensor(comb[:, :, :], picked[:, :, :], over(4), ALU.mult))
                        after(14, dve.tensor_copy(comb_r[:, :, :], comb[:, :, :]))
                        wait(dve, combt_done, i)
                        dve.tensor_copy(w["comb_pad"][:, :, 0:NE], f32(comb_r[:, :, :])).then_inc(route, 1)
                        dve.tensor_tensor(w["comb_pad"][:, :, NE:2 * NE], comb[:, :, :], f32(comb_r[:, :, :]),
                                          ALU.subtract).then_inc(route, 1)
                elif name == "e1":
                    n = i * NJ + k
                    if k >= 4:
                        dve.wait_ge(e2_done, n - 3)
                    else:
                        wait(dve, dec_done, i * DEC)
                    if k % 2:
                        dve.wait_ge(hidh_act, i * (NJ // 2) + k // 2 + 1)
                    else:
                        dve.wait_ge(hid_out, n + 1)
                        dve.tensor_copy(hidh[:, k % 4, :], hid[:, k % 2, :]).then_inc(hidh_dve, 1)
                        dve.wait_ge(hidh_dve, i * (NJ // 2) + k // 2 + 1)
                    dve.tensor_tensor(hidl[:, k % 4, :], hid[:, k % 2, :], f32(hidh[:, k % 4, :]), ALU.subtract)\
                        .then_inc(hidl_out, 1)
                elif name == "z":
                    e = k
                    dve.wait_ge(e2_done, i * NJ + e * EC + EC)
                    dve.wait_ge(combb_out, i * NE + e + 1)
                    if e == 0:
                        wait(dve, accl_out, i)
                        target = acc[:, :]
                    else:
                        wait(dve, acc_out, i * (NE - 2) + max(e - 2, 0))
                        target = z[:, e % 2, :]
                    dve.tensor_tensor(target, bX[e % 3][:, :], comb_b[:, e % 2, :], ALU.mult).then_inc(z_out, 1)
                elif name == "acc":
                    dve.wait_ge(acc_out, (i + 1) * (NE - 2))
                    dve.wait_ge(z_out, (i + 1) * NE)
                    dve.tensor_tensor(acc[:, :], acc[:, :], z[:, (NE - 1) % 2, :], ALU.add).then_inc(last_out, 1)
                    dve.wait_ge(last_out, i + 1)
                    dve.wait_ge(logits_done, i + 1)
                    split(acc[:, :], midh[:, :], midl[:, :], acch_out, accl_out, i + 1)
                elif name == "dup":
                    dve.wait_ge(moeh_out, i + 1)
                    dve.tensor_tensor(midl[:, :], bG[:, :], f32(midh[:, :]), ALU.subtract).then_inc(moel_out, 1)
                elif name == "c2s":
                    n = i * HC + k
                    dve.wait_ge(rate_out, n + 1)
                    if k >= 4:
                        dve.wait_ge(dec_done, i * DEC + k - 3)
                    else:
                        dve.wait_ge(e2_done, i * NJ + NJ)
                    split(hid[:, k % 2, :], hidh[:, k % 4, :], hidl[:, k % 4, :], rateh_out, ratel_out, n + 1)
                elif name == "fin_stats":
                    branch.stats_dve(dve, i - 1, k)
                elif name == "fin_norm":
                    branch.norm_dve(dve, i - 1, k)
            walk(dve, step)

        @block.gpsimd
        def _(pool):
            def step(name, k, i, e):
                if name == "ln_stats" and k == NT - 1:
                    blk = i + 2
                    pool.wait_ge(xmv, blk * NT + NT)
                    wait(pool, xnorm, blk * NT)
                    pool.tensor_tensor(ve[:, :], mv[:, :, 1], eps[:, :], ALU.add).then_inc(xve, 1)
                    pool.wait_ge(xve, blk + 1)
                    pool.tensor_tensor(rs[:, :], ve[:, :], w["half_down"][:, :], ALU.pow).then_inc(xrs, 1)
                elif name == "fin_stats" and k == NT - 1:
                    branch.stats_pool(pool, i - 1)
                elif name == "fin_norm":
                    branch.scale_pool(pool, i - 1, k)
                elif name == "z" and 0 < k < NE - 1:
                    e = k
                    pool.wait_ge(z_out, i * NE + e + 1)
                    wait(pool, acc_out, i * (NE - 2) + e - 1)
                    pool.tensor_tensor(acc[:, :], acc[:, :], z[:, e % 2, :], ALU.add).then_inc(acc_out, 1)
            pool.memset(eps[:, :], LN_EPS).then_inc(xeps, 1)
            pool.memset(eps4[:, :], 4 * LN_EPS).then_inc(xeps, 1)
            pool.wait_ge(xeps, 2)
            walk(pool, step)



VW = 2 * P + 2


def close_sequence(dve, kv, s):
    total, mask, num, numm, den, denh = (kv[n] for n in ("total", "mask", "num", "numm", "dent", "denth"))
    numh, numl, stationary = kv["numh"][s], kv["numl"][s], kv["den"][s]
    done = s * (6 + 2 * KC)

    def then(ins):
        nonlocal done
        done += 1
        ins.then_inc(kv["closed"], 1)
        dve.wait_ge(kv["closed"], done)
    then(dve.tensor_tensor(num[:, :, :], total[:, :, 0:P], total[:, :, P:2 * P], ALU.add))
    then(dve.tensor_tensor(numm[:, :, :], num[:, :, :],
                           mask[:, :, :].rearrange("p a b -> p (a b)").unsqueeze(1).broadcast_to([P, KC, P]),
                           ALU.mult))
    then(dve.tensor_copy(numh[:, :, :], numm[:, :, :]))
    then(dve.tensor_tensor(numl[:, :, :], numm[:, :, :], f32(numh[:, :, :]), ALU.subtract))
    then(dve.tensor_tensor(den[:, :, :], mask[:, :, 0:1].rearrange("p a b -> p (a b)").unsqueeze(1)
                           .broadcast_to([P, KC, HG]),
                           total[:, :, 2 * P:2 * P + 1].broadcast_to([P, KC, HG]), ALU.mult))
    then(dve.tensor_copy(denh[:, :, :], den[:, :, :]))
    for g in range(KC):
        a, z = g * HG, (g + 1) * HG
        then(dve.tensor_copy(stationary[:, g, a:z], f32(denh[:, g, :])))
        then(dve.tensor_tensor(stationary[:, g, 64 + a:64 + z], den[:, g, :], f32(denh[:, g, :]), ALU.subtract))


def run_keyvalue(nc, d, kv, att, branch, ahead):
    with ExitStack() as ctx:
        b = Bench(nc, ctx, "k_")
        raw = [ahead["wkv"][i].rearrange("p (c n) -> p c n", c=KC) for i in range(2)]
        wkh, wkl = b.sb("wkh", [P, KC, DIM], F32R), b.sb("wkl", [P, KC, DIM], F32R)
        wvh, wvl = b.sb("wvh", [P, KC, DIM], F32R), b.sb("wvl", [P, KC, DIM], F32R)
        xt = [ahead["xt"][:, i * KC * BLK:(i + 1) * KC * BLK].rearrange("p (c n) -> p c n", c=KC) for i in range(2)]
        xh = [b.sb(f"xh{i}", [P, KC, BLK], F32R) for i in range(2)]
        xl = [b.sb(f"xl{i}", [P, KC, BLK], F32R) for i in range(2)]
        aw = [b.sb(f"aw{i}", [P, KC, DIM]) for i in range(2)]
        kh, kl = b.sb("kh", [P, 2, DIM], F32R), b.sb("kl", [P, 2, DIM], F32R)
        v = b.sb("v", [P, 2, KC, VW], F32R)
        onesf = b.sb("onesf", [P, 2, KC, 2])
        total, mask = kv["total"], kv["mask"]
        zerof = b.sb("zerof", [P, KC * P])
        bK, bV = [b.psum(f"K{i}") for i in range(2)], [b.psum(f"V{i}") for i in range(2)]
        bA = [b.psum(f"A{g}") for g in range(KC)]

        w_in, x_in = ahead["wkv_in"], ahead["xt_in"]
        aw_in = [b.sem(f"aw_in{i}") for i in range(2)]
        awh_out, awl_out = b.sem("awh_out"), b.sem("awl_out")
        wh_out, wl_out, consts, ready = (b.sem(n) for n in ("wh_out", "wl_out", "consts", "ready"))
        xh_out, xl_out, k_done, v_done, vk_done = (b.sem(n) for n in ("xh_out", "xl_out", "k_done", "v_done", "vk_done"))
        kh_out, kl_out, vh_out, vl_out = (b.sem(n) for n in ("kh_out", "kl_out", "vh_out", "vl_out"))
        summed, cleared = b.sem("summed"), b.sem("cleared")

        PAIRS = NB // 2
        PER_SEQ = PAIRS // BATCH
        TP = 2 * NT

        block = ctx.enter_context(nc.Block())

        @block.sync
        def _(sp):
            for k in range(2):
                sp.dma_start(aw[k][:, :, :], d["wqp"][k].rearrange("p (c n) -> p c n", c=KC))\
                    .then_inc(aw_in[k], 16)
            with sp.Fori(1, PAIRS) as p:
                for h in range(2):
                    sp.wait_ge(xl_out, ((p - 1) * 2 + h + 1) * KC)
                    sp.dma_start(xt[h][:, :, :], d["xt"][:, bass.ds((p * 2 + h) * KC * BLK, KC * BLK)]
                                 .rearrange("p (c n) -> p c n", c=KC)).then_inc(x_in[h], 16)
            sp.dma_start(att["xt"][:, :, :], d["xt"][:, 0:KC * BLK].rearrange("p (c n) -> p c n", c=KC))\
                .then_inc(att["xt_in"], 16)
            branch.store(sp, NB - 1)
            sp.wait_ge(branch.stored, 16 * NB)

        @block.gpsimd
        def _(pool):
            pool.memset(onesf[:, :, :, :], 1.0).then_inc(consts, 1)
            pool.memset(zerof[:, :], 0.0).then_inc(consts, 1)
            pool.memset(total[:, :, :], 0.0).then_inc(consts, 1)
            pool.memset(mask[:, :, :], 1.0).then_inc(consts, 1)
            pool.wait_ge(consts, 4)
            pool.affine_select(out=mask[:, :, :], in_=mask[:, :, :], compare_op=ALU.is_ge, fill=0.0, base=0,
                               pattern=[[-HD, HG], [0, HD]], channel_multiplier=1).then_inc(consts, 1)
            pool.wait_ge(consts, 5)
            pool.affine_select(out=mask[:, :, :], in_=mask[:, :, :], compare_op=ALU.is_ge, fill=0.0, base=HD - 1,
                               pattern=[[HD, HG], [0, HD]], channel_multiplier=-1).then_inc(consts, 1)
            branch.stats_pool(pool, NB - 1)
            for t in range(NT):
                branch.scale_pool(pool, NB - 1, t)

        @block.scalar
        def _(act):
            for c in range(KC):
                for k, t in enumerate((wkh, wvh)):
                    act.wait_ge(w_in[k], 16)
                    act.activation(t[:, c, :], raw[k][:, c, :], ACT.Copy).then_inc(wh_out, 1)

            def tile(n, j):
                act.wait_ge(k_done, n + 1)
                if isinstance(n, int):
                    wait(act, vk_done, n - 1)
                else:
                    act.wait_ge(vk_done, n - 1)
                act.activation(kh[:, j % 2, :], bK[j % 2][:, :], ACT.Relu).then_inc(kh_out, 1)
                act.wait_ge(v_done, n + 1)
                act.activation(v[:, j % 2, :, 0:P], bV[j % 2][:, :].rearrange("p (g f) -> p g f", g=KC), ACT.Relu)\
                    .then_inc(vh_out, 1)
            for j in range(TP):
                tile(j, j)
                k, c = divmod(j, KC)
                act.wait_ge(aw_in[k], 16)
                act.activation(att["w"][k][0][:, c, :], aw[k][:, c, :], ACT.Copy).then_inc(awh_out, 1)
            with act.Fori(1, PAIRS) as p:
                for j in range(TP):
                    tile(p * TP + j, j)

        @block.tensor
        def _(pe):
            def project(n, j):
                h, t = divmod(j, NT)
                s = slice(t * P, (t + 1) * P)
                for c in range(KC):
                    a, z = c == 0, c == KC - 1
                    if isinstance(n, int) and n == 0:
                        pe.wait_ge(xl_out, c + 1)
                        pe.wait_ge(wl_out, 2 * c + 2)
                    if c == 0:
                        wait(pe, kl_out, n - 1)
                        wait(pe, vl_out, n - 1)
                    pe.matmul(bK[j % 2][:, :], xh[h][:, c, s], wkh[:, c, :], start=a, stop=False)
                    pe.matmul(bK[j % 2][:, :], xh[h][:, c, s], wkl[:, c, :], start=False, stop=False)
                    pe.matmul(bV[j % 2][:, :], xh[h][:, c, s], wvh[:, c, :], start=a, stop=False)
                    pe.matmul(bV[j % 2][:, :], xh[h][:, c, s], wvl[:, c, :], start=False, stop=False)
                    mk = pe.matmul(bK[j % 2][:, :], xl[h][:, c, s], wkh[:, c, :], start=False, stop=z)
                    if z:
                        mk.then_inc(k_done, 1)
                    mv = pe.matmul(bV[j % 2][:, :], xl[h][:, c, s], wvh[:, c, :], start=False, stop=z)
                mv.then_inc(v_done, 1)

            def outer(n, j, p):
                if isinstance(n, int) and n == 0:
                    pe.wait_ge(ready, 2)
                pe.wait_ge(kl_out, n + 1)
                pe.wait_ge(vl_out, n + 1)
                if j == 0:
                    wait(pe, summed, p * KC)
                for g in range(KC):
                    s = slice(g * P, (g + 1) * P)
                    pe.matmul(bA[g][:, 0:VW], kh[:, j % 2, s], v[:, j % 2, g, :], start=(j == 0), stop=False)
                    m = pe.matmul(bA[g][:, 0:VW], kl[:, j % 2, s], v[:, j % 2, g, :], start=False, stop=(j == TP - 1))
                m.then_inc(vk_done, 1)

            def pair(p):
                for j in range(TP + 1):
                    if j < TP:
                        if j % NT == 0 and not (j == 0 and isinstance(p, int)):
                            pe.wait_ge(xl_out, (p * 2 + j // NT + 1) * KC)
                        project(p * TP + j, j)
                    if j:
                        outer(p * TP + j - 1, j - 1, p)
            pair(0)
            with pe.Fori(1, PAIRS) as p:
                pair(p)

        @block.vector
        def _(dve):

            def split_x(p, h, c, n):
                if c == 0:
                    dve.wait_ge(x_in[h], p * 16 + 16)
                    wait(dve, v_done, (p - 1) * TP + (h + 1) * NT)
                dve.tensor_copy(xh[h][:, c, :], xt[h][:, c, :]).then_inc(xh_out, 1)
                dve.wait_ge(xh_out, n + 1)
                dve.tensor_tensor(xl[h][:, c, :], xt[h][:, c, :], f32(xh[h][:, c, :]), ALU.subtract)\
                    .then_inc(xl_out, 1)

            def tile(n, j):
                dve.wait_ge(kh_out, n + 1)
                dve.scalar_tensor_tensor(out=kl[:, j % 2, :], in0=bK[j % 2][:, :], scalar=0.0,
                                         in1=f32(kh[:, j % 2, :]), op0=ALU.max, op1=ALU.subtract).then_inc(kl_out, 1)
                dve.wait_ge(vh_out, n + 1)
                dve.scalar_tensor_tensor(out=v[:, j % 2, :, P:2 * P],
                                         in0=bV[j % 2][:, :].rearrange("p (g f) -> p g f", g=KC), scalar=0.0,
                                         in1=f32(v[:, j % 2, :, 0:P]), op0=ALU.max, op1=ALU.subtract)\
                    .then_inc(vl_out, 1)

            def pair(p, more):
                for j in range(TP):
                    if j < NT:
                        split_x(p, 1, j, p * 2 * KC + KC + j)
                    elif more:
                        split_x(p + 1, 0, j - NT, (p + 1) * 2 * KC + j - NT)
                    tile(p * TP + j, j)
                    if isinstance(p, int) and p == 0:
                        k, c = divmod(j, KC)
                        dve.wait_ge(awh_out, j + 1)
                        high, low = att["w"][k]
                        dve.tensor_tensor(low[:, c, :], aw[k][:, c, :], f32(high[:, c, :]), ALU.subtract)\
                            .then_inc(awl_out, 1)
                        if j < NT:
                            branch.stats_dve(dve, NB - 1, j)
                        elif j == NT:
                            for t in range(NT):
                                branch.norm_dve(dve, NB - 1, t)
                dve.wait_ge(vk_done, p * TP + TP)
                for g in range(KC):
                    dve.wait_ge(summed, p * KC + g)
                    dve.tensor_tensor(total[:, g, :], bA[g][:, 0:VW], total[:, g, :], ALU.add).then_inc(summed, 1)

            for c in range(KC):
                split_x(0, 0, c, c)
                for k, (high, low) in enumerate(((wkh, wkl), (wvh, wvl))):
                    dve.wait_ge(wh_out, 2 * c + k + 1)
                    dve.tensor_tensor(low[:, c, :], raw[k][:, c, :], f32(high[:, c, :]), ALU.subtract)\
                        .then_inc(wl_out, 1)
            dve.wait_ge(consts, 6)
            dve.tensor_copy(v[:, :, :, 2 * P:VW], onesf[:, :, :, :]).then_inc(ready, 1)
            for s in range(BATCH):
                m = dve.tensor_copy(kv["den"][s][:, :, :], zerof[:, :].rearrange("p (c n) -> p c n", c=KC))
            m.then_inc(ready, 1)
            for s in range(BATCH):
                first = s * PER_SEQ
                if s == 0:
                    pair(0, True)
                    with dve.Fori(1, PER_SEQ) as p:
                        pair(p, True)
                else:
                    with dve.Fori(first, PAIRS - 1) as p:
                        pair(p, True)
                    pair(PAIRS - 1, False)
                if s == 0:
                    dve.wait_ge(summed, PER_SEQ * KC)
                    close_sequence(dve, kv, 0)
                    dve.memset(total[:, :, :], 0.0).then_inc(cleared, 1)
                    dve.wait_ge(cleared, 1)



def run_attention(nc, d, kv, att, out_dram):
    with ExitStack() as ctx:
        b = Bench(nc, ctx, "a_")
        (wqh, wql), (wph, wpl) = att["w"]
        bias2, bias = b.sb("bias2", [P, 2, DIM]), b.sb("bias", [P, DIM])
        fan, fanf = b.sb("fan", [64, KC, P], F32R), b.sb("fanf", [64, KC, P])
        xt = att["xt"]
        xh, xl = b.sb("xh", [P, KC, BLK], F32R), b.sb("xl", [P, KC, BLK], F32R)
        qh, ql = b.sb("qh", [P, KC, BLK], F32R), b.sb("ql", [P, KC, BLK], F32R)
        ah, al = b.sb("ah", [P, KC, BLK], F32R), b.sb("al", [P, KC, BLK], F32R)
        at, rb = b.sb("at", [P, 2, BLK]), b.sb("rb", [P, 2, BLK])
        dlow, dsum = b.sb("dlow", [HEADS, BLK]), b.sb("dsum", [HEADS, BLK])
        rc, rc2 = b.sb("rc", [HEADS, BLK]), b.sb("rc2", [2 * HEADS, BLK], F32R)
        x, y, f = b.sb("x", [P, NT, DIM]), b.sb("y", [P, NT, DIM]), b.sb("f", [P, NT, DIM])
        bQ, bN = [b.psum(f"Q{i}") for i in range(2)], [b.psum(f"N{i}") for i in range(2)]
        bR, bDen = b.psum("R"), b.psum("Den")
        bP = [b.psum(f"P{i}") for i in range(2)]
        sem = b.sem
        vec_in, xt_in, f_in = sem("vec_in"), att["xt_in"], sem("f_in")
        x_in = [sem(f"x_in{t}") for t in range(NT)]
        stored = [sem(f"stored{t}") for t in range(NT)]
        consts, ready = sem("consts"), sem("ready")
        xh_out, xl_out, q_done, qh_out, ql_out = (sem(n) for n in ("xh_out", "xl_out", "q_done", "qh_out", "ql_out"))
        den_done, dlow_out, dsum_out, rc_out, rch_out, rcl_out = (sem(n) for n in (
            "den_done", "dlow_out", "dsum_out", "rc_out", "rch_out", "rcl_out"))
        fan_done, num_done, rb_out, at_out, ah_out, al_out = (sem(n) for n in (
            "fan_done", "num_done", "rb_out", "at_out", "ah_out", "al_out"))
        proj_done, y_out, xf_out, xfb_out = sem("proj_done"), sem("y_out"), sem("xf_out"), sem("xfb_out")

        def blocks(eng, body):
            half = NB // BATCH
            body(0, 0, attend=False)
            body(1, 0)
            with eng.Fori(2, half) as i:
                body(i, 0)
            body(half, 0)
            with eng.Fori(half + 1, NB - 1) as i:
                body(i, 1)
            body(NB - 1, 1, more=False)
            body(NB, 1, more=False, ahead=False)

        block = ctx.enter_context(nc.Block())

        @block.sync
        def _(sp):
            def load_xt(i):
                sp.dma_start(xt[:, :, :], d["xt"][:, bass.ds(i * KC * BLK, KC * BLK)]
                             .rearrange("p (c n) -> p c n", c=KC)).then_inc(xt_in, 16)

            def load_x(j, t):
                sp.dma_start(x[:, t, :], d["x"][bass.ds(j * NT + t, 1), :, :].rearrange("t p c -> (t p) c"))\
                    .then_inc(x_in[t], 16)

            def load_f(j):
                sp.dma_start(f[:, :, :], d["ffn"][bass.ds(j * NT, NT), :, :].rearrange("t p c -> p t c"))\
                    .then_inc(f_in, 16)

            sp.dma_start(bias2[:, :, :], d["bias2"][:, :, :]).then_inc(vec_in, 16)
            for t in range(NT):
                load_x(0, t)
            load_f(0)

            def body(i, s, ahead=True, attend=True, more=True):
                if more:
                    sp.wait_ge(xl_out, i * KC + KC)
                    load_xt(i + 1)
                if attend:
                    j = i - 1
                    if ahead:
                        sp.wait_ge(xf_out, j * NT + NT)
                        load_f(j + 1)
                    for t in range(NT):
                        sp.wait_ge(y_out, j * NT + t + 1)
                        sp.dma_start(out_dram[bass.ds(j * NT + t, 1), :, :].rearrange("t p c -> (t p) c"),
                                     y[:, t, :]).then_inc(stored[t], 16)
                        if ahead:
                            load_x(j + 1, t)
            blocks(sp, body)
            for t in range(NT):
                sp.wait_ge(stored[t], 16 * NB)

        @block.gpsimd
        def _(pool):
            pool.memset(fanf[:, :, :], 1.0).then_inc(consts, 1)
            n = 1
            for half in range(2):
                v = fanf[32 * half:32 * half + 32, :, :]
                for cm, st, base in ((-HD, 1, 0), (HD, -1, HD - 1)):
                    pool.wait_ge(consts, n)
                    pool.affine_select(out=v, in_=v, compare_op=ALU.is_ge, fill=0.0, base=base,
                                       pattern=[[st * P, KC], [st, P]], channel_multiplier=cm).then_inc(consts, 1)
                    n += 1
            pool.wait_ge(consts, 5)
            pool.wait_ge(vec_in, 16)
            pool.tensor_tensor(bias[:, :], bias2[:, 0, :], bias2[:, 1, :], ALU.add).then_inc(consts, 1)
            pool.wait_ge(consts, 6)

            def body(i, s, ahead=True, attend=True, more=True):
                if attend:
                    j = i - 1
                    pool.wait_ge(f_in, j * 16 + 16)
                    for t in range(NT):
                        pool.wait_ge(x_in[t], j * 16 + 16)
                        pool.tensor_tensor(x[:, t, :], x[:, t, :], f[:, t, :], ALU.add).then_inc(xf_out, 1)
                        pool.wait_ge(xf_out, j * NT + t + 1)
                        pool.tensor_tensor(x[:, t, :], x[:, t, :], bias[:, :], ALU.add).then_inc(xfb_out, 1)
            blocks(pool, body)

        @block.scalar
        def _(act):
            def split_x(i):
                act.wait_ge(xt_in, i * 16 + 16)
                wait(act, q_done, i * KC)
                for c in range(KC):
                    act.activation(xh[:, c, :], xt[:, c, :], ACT.Copy).then_inc(xh_out, 1)

            split_x(0)

            def body(i, s, ahead=True, attend=True, more=True):
                for m in range(KC):
                    if attend:
                        n = (i - 1) * KC + m
                        act.wait_ge(fan_done, n + 1)
                        wait(act, at_out, n - 1)
                        act.activation(rb[:, m % 2, :], bR[:, :], ACT.Copy).then_inc(rb_out, 1)
                    if ahead:
                        n = i * KC + m
                        act.wait_ge(q_done, n + 1)
                        if attend:
                            act.wait_ge(num_done, (i - 1) * KC + m + 1)
                        act.activation(qh[:, m, :], bQ[m % 2][:, :], ACT.Relu).then_inc(qh_out, 1)
                    if attend:
                        n = (i - 1) * KC + m
                        act.wait_ge(at_out, n + 1)
                        wait(act, proj_done, (i - 1) * NT)
                        act.activation(ah[:, m, :], at[:, m % 2, :], ACT.Copy).then_inc(ah_out, 1)
                if more:
                    split_x(i + 1)
                if ahead:
                    act.wait_ge(den_done, i + 1)
                    wait(act, dsum_out, i)
                    act.activation(dlow[:, :], bDen[64:64 + HEADS, :], ACT.Copy).then_inc(dlow_out, 1)
                    act.wait_ge(rc_out, 2 * i + 2)
                    wait(act, fan_done, i * KC)
                    act.activation(rc2[0:HEADS, :], rc[:, :], ACT.Copy).then_inc(rch_out, 1)
            blocks(act, body)

        @block.tensor
        def _(pe):
            def attention(i, m, s):
                n = (i - 1) * KC + m
                pe.wait_ge(rcl_out, i)
                wait(pe, rb_out, n)
                pe.matmul(bR[:, :], fan[:, m, :], rc2[:, :], start=True, stop=True).then_inc(fan_done, 1)
                wait(pe, at_out, n - 1)
                pass3(pe, bN[m % 2][:, :], kv["numh"][s][:, m, :], kv["numl"][s][:, m, :],
                      qh[:, m, :], ql[:, m, :], True, True).then_inc(num_done, 1)

            def query(i, m):
                n = i * KC + m
                wait(pe, ql_out, n - 1)
                for c in range(KC):
                    if m == 0:
                        pe.wait_ge(xl_out, i * KC + c + 1)
                    o = slice(m * P, (m + 1) * P)
                    k = pass3(pe, bQ[m % 2][:, :], wqh[:, c, o], wql[:, c, o], xh[:, c, :], xl[:, c, :],
                              c == 0, c == KC - 1)
                k.then_inc(q_done, 1)

            def denominators(i, s):
                if isinstance(i, int) and i == NB // BATCH:
                    s = 1
                pe.wait_ge(ql_out, i * KC + KC)
                wait(pe, dsum_out, i)
                if isinstance(i, int) and i == 0:
                    pe.wait_ge(kv["closed"], BATCH * (6 + 2 * KC))
                for g in range(KC):
                    pe.matmul(bDen[:, :], kv["den"][s][:, g, :], qh[:, g, :], start=(g == 0), stop=False)
                    k = pe.matmul(bDen[:, :], kv["den"][s][:, g, :], ql[:, g, :], start=False, stop=(g == KC - 1))
                k.then_inc(den_done, 1)

            def body(i, s, ahead=True, attend=True, more=True):
                if isinstance(i, int) and i == 1:
                    pe.wait_ge(ready, 1)
                for m in range(KC):
                    if ahead:
                        query(i, m)
                    if attend:
                        attention(i, m, s)
                if attend:
                    for t in range(NT):
                        n = (i - 1) * NT + t
                        wait(pe, y_out, n - 1)
                        for g in range(KC):
                            if t == 0:
                                pe.wait_ge(al_out, (i - 1) * KC + g + 1)
                            o = slice(t * P, (t + 1) * P)
                            pe.matmul(bP[t % 2][:, :], ah[:, g, o], wph[:, g, :], start=(g == 0), stop=False)
                            pe.matmul(bP[t % 2][:, :], ah[:, g, o], wpl[:, g, :], start=False, stop=False)
                            k = pe.matmul(bP[t % 2][:, :], al[:, g, o], wph[:, g, :], start=False, stop=(g == KC - 1))
                        k.then_inc(proj_done, 1)
                        if t == 0 and ahead:
                            denominators(i, s)
                else:
                    denominators(i, s)

            blocks(pe, body)

        @block.vector
        def _(dve):
            def split_x(i, c):
                dve.wait_ge(xh_out, i * KC + c + 1)
                dve.tensor_tensor(xl[:, c, :], xt[:, c, :], f32(xh[:, c, :]), ALU.subtract).then_inc(xl_out, 1)

            def out_tile(i, t):
                j = i - 1
                dve.wait_ge(proj_done, j * NT + t + 1)
                dve.wait_ge(xfb_out, j * NT + t + 1)
                wait(dve, stored[t], j * 16)
                dve.tensor_tensor(y[:, t, :], bP[t % 2][:, :], x[:, t, :], ALU.add).then_inc(y_out, 1)

            def reciprocals(i, half):
                o = slice(half * BLK // 2, (half + 1) * BLK // 2)
                dve.reciprocal(rc[:, o], dsum[:, o]).then_inc(rc_out, 1)

            def body(i, s, ahead=True, attend=True, more=True):
                for m in range(KC):
                    if attend:
                        n = (i - 1) * KC + m
                        dve.wait_ge(rb_out, n + 1)
                        dve.wait_ge(num_done, n + 1)
                        wait(dve, al_out, n - 1)
                        dve.tensor_tensor(at[:, m % 2, :], bN[m % 2][:, :], rb[:, m % 2, :], ALU.mult)\
                            .then_inc(at_out, 1)
                    if ahead:
                        n = i * KC + m
                        dve.wait_ge(qh_out, n + 1)
                        dve.scalar_tensor_tensor(out=ql[:, m, :], in0=bQ[m % 2][:, :], scalar=0.0,
                                                 in1=f32(qh[:, m, :]), op0=ALU.max, op1=ALU.subtract)\
                            .then_inc(ql_out, 1)
                    if attend:
                        n = (i - 1) * KC + m
                        dve.wait_ge(ah_out, n + 1)
                        dve.tensor_tensor(al[:, m, :], at[:, m % 2, :], f32(ah[:, m, :]), ALU.subtract)\
                            .then_inc(al_out, 1)
                if more:
                    split_x(i + 1, 0)
                    split_x(i + 1, 1)
                if attend:
                    out_tile(i, 0)
                if more:
                    split_x(i + 1, 2)
                if ahead:
                    dve.wait_ge(dlow_out, i + 1)
                    wait(dve, rc_out, 2 * i)
                    dve.scalar_tensor_tensor(out=dsum[:, :], in0=bDen[0:HEADS, :], scalar=DEN_EPS, in1=dlow[:, :],
                                             op0=ALU.add, op1=ALU.add).then_inc(dsum_out, 1)
                    dve.wait_ge(dsum_out, i + 1)
                    wait(dve, rcl_out, i)
                    reciprocals(i, 0)
                if attend:
                    out_tile(i, 1)
                if ahead:
                    reciprocals(i, 1)
                if attend:
                    out_tile(i, 2)
                if more:
                    split_x(i + 1, 3)
                if ahead:
                    dve.wait_ge(rch_out, i + 1)
                    dve.tensor_tensor(rc2[HEADS:2 * HEADS, :], rc[:, :], f32(rc2[0:HEADS, :]), ALU.subtract)\
                        .then_inc(rcl_out, 1)
                if attend:
                    out_tile(i, 3)

            for c in range(KC):
                split_x(0, c)
            close_sequence(dve, kv, 1)
            dve.wait_ge(consts, 5)
            dve.tensor_copy(fan[:, :, :], fanf[:, :, :]).then_inc(ready, 1)
            blocks(dve, body)


def build(nc, d, out_dram):
    d = dict(d)
    d["xt"] = nc.dram_tensor("xt_scratch", [P, NB * KC * BLK], F32).ap()
    d["ffn"] = nc.dram_tensor("ffn_scratch", [TOK // P, P, DIM], F32).ap()
    with ExitStack() as ctx:
        b = Bench(nc, ctx, "")
        branch = Branch(nc, Bench(nc, ctx, "b_"), d)
        over = Bench(nc, ctx, "over_").first_use("ffn", [P, NE * EH + KC * HID])
        ahead = {"wkv": [over[:, k * KC * DIM:(k + 1) * KC * DIM] for k in range(2)],
                 "xt": over[:, NE * EH:NE * EH + KC * HID],
                 "wkv_in": [b.sem(f"wkv_in{k}") for k in range(2)], "xt_in": [b.sem(f"xt_in{h}") for h in range(2)]}
        with ExitStack() as inner:
            w = ffn_weights(Bench(nc, inner, "w_"), branch)
            ffn_constants(nc, d, w)
            run_ffn(nc, d, w, branch, ahead)
        b.sb("over_keyvalue", [P, NE * EH + KC * HID])
        kv = {"numh": [b.sb(f"numh{s}", [P, KC, P], F32R) for s in range(BATCH)],
              "numl": [b.sb(f"numl{s}", [P, KC, P], F32R) for s in range(BATCH)],
              "den": [b.sb(f"den{s}", [P, KC, P], F32R) for s in range(BATCH)],
              "total": b.sb("total", [P, KC, VW]), "mask": b.sb("mask", [P, HG, HD]),
              "num": b.sb("num", [P, KC, P]), "numm": b.sb("numm", [P, KC, P]),
              "dent": b.sb("dent", [P, KC, HG]), "denth": b.sb("denth", [P, KC, HG], F32R),
              "closed": b.sem("closed")}
        att = {"w": [(b.sb(n + "h", [P, KC, DIM], F32R), b.sb(n + "l", [P, KC, DIM], F32R)) for n in ("wq", "wp")],
               "xt": b.sb("xt", [P, KC, BLK]), "xt_in": b.sem("att_xt_in")}
        run_keyvalue(nc, d, kv, att, branch, ahead)
        run_attention(nc, d, kv, att, out_dram)



def kernel(**inputs):
    import numpy as np
    import concourse.bacc as bacc
    from concourse.bass_utils import run_bass_kernel_spmd

    a = {k.removeprefix("L0_ffn_").removeprefix("L0_attn_"): np.asarray(v) for k, v in inputs.items()}

    def chunked(m):
        c = m.shape[0] // P
        return m.reshape(c, P, -1).transpose(1, 0, 2).reshape(P, -1)

    def every(v):
        return np.broadcast_to(v.reshape(1, -1), (P, v.size))

    def twice(m):
        return np.concatenate([m, m], axis=0)

    qkv_t = a["qkv_weight"].T
    vectors = {
        "enc_b": a["enc_b"].reshape(HC, P).T,
        "c2s_b": a["c2s_b"].reshape(HC, P).T,
        "e_b1": a["e_b1"].reshape(NJ, P).T,
        "r_b1": twice(a["r_b1"].reshape(MOE, 1)),
        "s2c_b": twice(a["s2c_b"].reshape(MOE, 1)),
        "r_b2": every(a["r_b2"]),
    }
    host = {
        "x": a["x"].reshape(TOK // P, P, DIM),
        "enc_w": chunked(a["enc_w"]),
        "s2c_w": np.concatenate([chunked(a["s2c_w"]).reshape(P, HC, MOE)] * 2, axis=2).reshape(P, HC * P),
        "e_w1": twice(a["e_w1"].transpose(1, 0, 2).reshape(MOE, NE * EH)),
        "e_w2": chunked(a["e_w2"].reshape(NE * EH, MOE)),
        "c2s_w": twice(a["c2s_w"]),
        "dec_w": chunked(a["dec_w"]),
        "small": np.concatenate([twice(np.concatenate([a["r_w1"], a["r_w1"]], axis=1)), twice(a["r_w2"]),
                                 np.tile(np.concatenate([a["e_b2"], a["e_b2"]], axis=1), (P // NE, 1))], axis=1),
        "cols": np.concatenate([vectors[name] for name, _ in COLUMNS], axis=1),
        "ln_g": every(a["ln_g"]),
        "dec_b": every(a["dec_b"]),
        "wkv": np.stack([chunked(qkv_t[:, DIM:2 * DIM]), chunked(qkv_t[:, 2 * DIM:3 * DIM])]),
        "wqp": np.stack([chunked(qkv_t[:, 0:DIM]), chunked(a["proj_weight"].T)]),
        "bias2": np.stack([every(a["proj_bias"]), every(a["ln_b"])], axis=1),
    }
    nc = bacc.Bacc("TRN2", target_bir_lowering=False, num_devices=1)
    arrays, d = {}, {}
    for name, v in host.items():
        v = np.ascontiguousarray(v)
        arrays[f"in_{name}"] = v
        d[name] = nc.dram_tensor(f"in_{name}", v.shape, mybir.dt.from_np(v.dtype), kind="ExternalInput").ap()
    out = nc.dram_tensor("out_y", (TOK // P, P, DIM), F32, kind="ExternalOutput").ap()
    build(nc, d, out)
    r = run_bass_kernel_spmd(nc, [arrays], core_ids=[0])
    return r.results[0]["out_y"].reshape(BATCH, SEQ, DIM)
```
